# Optimizing a Trainium2 kernel written in Bass

```python
import numpy as np
import jax
import jax.numpy as jnp

def _softmax(x, axis=-1):
    return jax.nn.softmax(x, axis=axis)

def _gelu(x):
    return jax.nn.gelu(x, approximate=True)

def _silu(x):
    return jax.nn.silu(x)

def _sigmoid(x):
    return jax.nn.sigmoid(x)

def _layernorm(x, axis=-1, eps=1e-05):
    m = jnp.mean(x, axis=axis, keepdims=True)
    v = jnp.var(x, axis=axis, keepdims=True)
    return (x - m) / jnp.sqrt(v + eps)

def _scatter_add(tgt, idx, src, axis=0):
    return tgt.at[idx].add(src)

def _segment_sum(src, seg, n):
    return jax.ops.segment_sum(src, seg, n)
kernel_name = 'mk_gps_d2_gnn_r16_509d36'

def setup_inputs(seed: int=0):
    np.random.seed(seed)
    _w = jnp.asarray

    def _rec_inputs():
        import jax
        import jax.numpy as jnp
        _gk = jax.random.key(seed)
        x = -0.0003713 + 1 * jax.random.normal(jax.random.fold_in(_gk, 1), (3125, 256), jnp.float32)
        _s = jax.random.randint(jax.random.fold_in(_gk, 2), (50000,), 0, 3125, jnp.int32)
        _d = jax.random.randint(jax.random.fold_in(_gk, 3), (50000,), 0, 3125, jnp.int32)
        _loop = jnp.arange(3125, dtype=jnp.int32)
        src = jnp.concatenate([_s, _d, _loop])
        dst = jnp.concatenate([_d, _s, _loop])
        _o = jnp.argsort(dst, stable=True)
        src = src[_o]
        dst = dst[_o]
        edge_attr_64 = 0.000189758 + 1.00013 * jax.random.normal(jax.random.fold_in(_gk, 11), (103125, 64), jnp.float32)
        return (x, src, dst, edge_attr_64)
    x, src, dst, edge_attr_64 = _rec_inputs()

    def _L0_gnn_setup():
        import jax, jax.numpy as jnp
        import numpy as np
        N, E, HID, HEADS, EDIM = (3125, 50000, 256, 8, 64)
        C = HID // HEADS

        def _layernorm(x, g, b, eps=1e-05):
            mu = jnp.mean(x, axis=-1, keepdims=True)
            var = jnp.var(x, axis=-1, keepdims=True)
            return (x - mu) * jax.lax.rsqrt(var + eps) * g + b

        def _transformer_conv(x, edge_index, edge_attr, Wq, bq, Wk, bk, Wv, bv, We, Wskip, bskip, Wbeta):
            n = x.shape[0]
            src, dst = (edge_index[0], edge_index[1])
            q = (x @ Wq.T + bq).reshape(n, HEADS, C)
            k = (x @ Wk.T + bk).reshape(n, HEADS, C)
            v = (x @ Wv.T + bv).reshape(n, HEADS, C)
            e = (edge_attr @ We.T).reshape(-1, HEADS, C)
            k_e = k[src] + e
            v_e = v[src] + e
            alpha = jnp.sum(q[dst] * k_e, axis=-1) / np.sqrt(C)
            amax = jax.ops.segment_max(alpha, dst, num_segments=n)
            amax = jnp.where(jnp.isfinite(amax), amax, 0.0)
            ex = jnp.exp(alpha - amax[dst])
            denom = jax.ops.segment_sum(ex, dst, num_segments=n)
            alpha = ex / (denom[dst] + 1e-16)
            out = jax.ops.segment_sum(v_e * alpha[..., None], dst, num_segments=n)
            out = out.reshape(n, HEADS * C)
            x_r = x @ Wskip.T + bskip
            beta = jax.nn.sigmoid(jnp.concatenate([out, x_r, out - x_r], axis=-1) @ Wbeta.T)
            return beta * x_r + (1.0 - beta) * out
        key = jax.random.key(seed)
        ks = jax.random.split(key, 20)
        s_in = 1.0 / np.sqrt(HID)
        s_e = 1.0 / np.sqrt(EDIM)
        s_ff = 1.0 / np.sqrt(4 * HID)
        s_b = 1.0 / np.sqrt(3 * HID)
        return {'x': jax.random.normal(ks[0], (N, HID), jnp.float32), 'edge_index': jax.random.randint(ks[1], (2, E), 0, N, jnp.int32), 'edge_attr': jax.random.normal(ks[2], (E, EDIM), jnp.float32), 'Wq': jax.random.uniform(ks[3], (HID, HID), jnp.float32, -s_in, s_in), 'bq': jnp.zeros((HID,), jnp.float32), 'Wk': jax.random.uniform(ks[4], (HID, HID), jnp.float32, -s_in, s_in), 'bk': jnp.zeros((HID,), jnp.float32), 'Wv': jax.random.uniform(ks[5], (HID, HID), jnp.float32, -s_in, s_in), 'bv': jnp.zeros((HID,), jnp.float32), 'We': jax.random.uniform(ks[6], (HID, EDIM), jnp.float32, -s_e, s_e), 'Wskip': jax.random.uniform(ks[7], (HID, HID), jnp.float32, -s_in, s_in), 'bskip': jnp.zeros((HID,), jnp.float32), 'Wbeta': jax.random.uniform(ks[8], (1, 3 * HID), jnp.float32, -s_b, s_b), 'ln1_g': jnp.ones((HID,), jnp.float32), 'ln1_b': jnp.zeros((HID,), jnp.float32), 'ln2_g': jnp.ones((HID,), jnp.float32), 'ln2_b': jnp.zeros((HID,), jnp.float32), 'W1': jax.random.uniform(ks[9], (4 * HID, HID), jnp.float32, -s_in, s_in), 'b1': jnp.zeros((4 * HID,), jnp.float32), 'W2': jax.random.uniform(ks[10], (HID, 4 * HID), jnp.float32, -s_ff, s_ff), 'b2': jnp.zeros((HID,), jnp.float32)}
    _L0_gnn_all = _L0_gnn_setup()
    _L0_gnn_in = {k: v for k, v in _L0_gnn_all.items() if k in ('Wq', 'bq', 'Wk', 'bk', 'Wv', 'bv', 'We', 'Wskip', 'bskip', 'Wbeta', 'ln1_g', 'ln1_b', 'ln2_g', 'ln2_b', 'W1', 'b1', 'W2', 'b2')}
    del _L0_gnn_all

    def _L0_mix_setup():
        import jax, jax.numpy as jnp
        import numpy as np
        D_MODEL = 256
        NUM_HEADS = 8
        DEPTH = D_MODEL // NUM_HEADS
        B, L = (32, 256)

        def _feature_map(x):
            return jax.nn.elu(x) + 1.0
        key = jax.random.key(seed)
        ks = jax.random.split(key, 9)
        sc = 1.0 / np.sqrt(D_MODEL)
        return {'x': jax.random.normal(ks[0], (B, L, D_MODEL), dtype=jnp.float32), 'wq': jax.random.normal(ks[1], (D_MODEL, D_MODEL), dtype=jnp.float32) * sc, 'bq': jnp.zeros((D_MODEL,), dtype=jnp.float32), 'wk': jax.random.normal(ks[2], (D_MODEL, D_MODEL), dtype=jnp.float32) * sc, 'bk': jnp.zeros((D_MODEL,), dtype=jnp.float32), 'wv': jax.random.normal(ks[3], (D_MODEL, D_MODEL), dtype=jnp.float32) * sc, 'bv': jnp.zeros((D_MODEL,), dtype=jnp.float32), 'wo': jax.random.normal(ks[4], (D_MODEL, D_MODEL), dtype=jnp.float32) * sc, 'bo': jnp.zeros((D_MODEL,), dtype=jnp.float32)}
    _L0_mix_all = _L0_mix_setup()
    _L0_mix_in = {k: v for k, v in _L0_mix_all.items() if k in ('wq', 'bq', 'wk', 'bk', 'wv', 'bv', 'wo', 'bo')}
    del _L0_mix_all

    def _L0_ffn_setup():
        import jax, jax.numpy as jnp
        import numpy as np
        B, N, D = (16, 256, 256)
        NUM_EXPERTS, TOP_K, HEADS = (4, 2, 4)
        N_EDGES = 65536
        LN_EPS = 1e-05

        def _layernorm(x, g, b):
            mu = x.mean(-1, keepdims=True)
            var = ((x - mu) ** 2).mean(-1, keepdims=True)
            return (x - mu) * jax.lax.rsqrt(var + LN_EPS) * g + b

        def _forward(x, edge_index, W_gat, att_src, att_dst, b_gat, ln_gamma, ln_beta, W1, b1, W2, b2):
            Bc, Nc, Dc = x.shape
            M = Bc * Nc
            x_flat = x.reshape(M, Dc)
            h = (x_flat @ W_gat).reshape(M, HEADS, NUM_EXPERTS)
            loops = jnp.arange(M, dtype=edge_index.dtype)
            src = jnp.concatenate([edge_index[0], loops])
            dst = jnp.concatenate([edge_index[1], loops])
            a_src = (h * att_src).sum(-1)
            a_dst = (h * att_dst).sum(-1)
            e = jax.nn.leaky_relu(a_src[src] + a_dst[dst], negative_slope=0.2)
            e_max = jax.ops.segment_max(e, dst, num_segments=M)
            ee = jnp.exp(e - e_max[dst])
            denom = jax.ops.segment_sum(ee, dst, num_segments=M)
            alpha = ee / (denom[dst] + 1e-16)
            msg = h[src] * alpha[:, :, None]
            agg = jax.ops.segment_sum(msg, dst, num_segments=M).reshape(M, HEADS * NUM_EXPERTS) + b_gat
            scores = _layernorm(agg, ln_gamma, ln_beta).reshape(M, HEADS, NUM_EXPERTS).mean(1)
            scores = scores.reshape(Bc, Nc, NUM_EXPERTS)
            topk_s, topk_i = jax.lax.top_k(scores, TOP_K)
            w = jax.nn.softmax(topk_s, axis=-1)
            out = jnp.zeros_like(x)
            for ei in range(NUM_EXPERTS):
                g = jnp.where(topk_i == ei, w, 0.0).sum(-1)
                hh = jax.nn.gelu(x @ W1[ei] + b1[ei], approximate=False)
                out = out + g[..., None] * (hh @ W2[ei] + b2[ei])
            return out
        key = jax.random.key(seed)
        ks = jax.random.split(key, 8)
        s = 0.05
        return {'x': jax.random.normal(ks[0], (B, N, D), jnp.float32), 'W_gat': jax.random.normal(ks[1], (D, HEADS * NUM_EXPERTS), jnp.float32) * s, 'att_src': jax.random.normal(ks[2], (HEADS, NUM_EXPERTS), jnp.float32) * s, 'att_dst': jax.random.normal(ks[3], (HEADS, NUM_EXPERTS), jnp.float32) * s, 'b_gat': jnp.zeros((HEADS * NUM_EXPERTS,), jnp.float32), 'ln_gamma': jnp.ones((HEADS * NUM_EXPERTS,), jnp.float32), 'ln_beta': jnp.zeros((HEADS * NUM_EXPERTS,), jnp.float32), 'W1': jax.random.normal(ks[4], (NUM_EXPERTS, D, 2 * D), jnp.float32) * s, 'b1': jnp.zeros((NUM_EXPERTS, 2 * D), jnp.float32), 'W2': jax.random.normal(ks[5], (NUM_EXPERTS, 2 * D, D), jnp.float32) * s, 'b2': jnp.zeros((NUM_EXPERTS, D), jnp.float32), 'edge_index': jax.random.randint(ks[6], (2, N_EDGES), 0, B * N, jnp.int32)}
    _L0_ffn_all = _L0_ffn_setup()
    _L0_ffn_in = {k: v for k, v in _L0_ffn_all.items() if k in ('W_gat', 'att_src', 'att_dst', 'b_gat', 'ln_gamma', 'ln_beta', 'W1', 'b1', 'W2', 'b2', 'edge_index')}
    del _L0_ffn_all

    def _L1_gnn_setup():
        import jax, jax.numpy as jnp
        import numpy as np
        N_NODES = 6250
        F_DIM = 256
        NNZ = 100000

        def _prelu(x, a):
            return jnp.where(x >= 0, x, a * x)

        def _hconv(x, W, b, src, dst, n):
            xt = x @ W
            ones = jnp.ones(src.shape, xt.dtype)
            D = jax.ops.segment_sum(ones, src, num_segments=n)
            B = jax.ops.segment_sum(ones, dst, num_segments=n)
            Dinv = jnp.where(D > 0, 1.0 / D, 0.0)
            Binv = jnp.where(B > 0, 1.0 / B, 0.0)
            m = jax.ops.segment_sum(xt[src], dst, num_segments=n) * Binv[:, None]
            out = jax.ops.segment_sum(m[dst], src, num_segments=n) * Dinv[:, None]
            return out + b
        key = jax.random.key(seed)
        k0, k1, k2, k3 = jax.random.split(key, 4)
        x = jax.random.normal(k0, (N_NODES, F_DIM), dtype=jnp.float32)
        edge_index = jax.random.randint(k1, (2, NNZ), 0, N_NODES, dtype=jnp.int32)
        scale = (2.0 / F_DIM) ** 0.5
        W1 = jax.random.normal(k2, (F_DIM, F_DIM), dtype=jnp.float32) * scale
        W2 = jax.random.normal(k3, (F_DIM, F_DIM), dtype=jnp.float32) * scale
        b1 = jnp.zeros((F_DIM,), jnp.float32)
        b2 = jnp.zeros((F_DIM,), jnp.float32)
        a = jnp.full((1,), 0.25, jnp.float32)
        return {'x': x, 'edge_index': edge_index, 'W1': W1, 'b1': b1, 'W2': W2, 'b2': b2, 'a': a}
    _L1_gnn_all = _L1_gnn_setup()
    _L1_gnn_in = {k: v for k, v in _L1_gnn_all.items() if k in ('W1', 'b1', 'W2', 'b2', 'a')}
    del _L1_gnn_all

    def _L1_mix_setup():
        import jax, jax.numpy as jnp
        import numpy as np
        HEADS = 8
        EPS = 1e-05

        def _ln(t, w, b, headc):
            m = jnp.mean(t, axis=-1, keepdims=True)
            d = t - m
            std = jnp.sqrt(jnp.sum(d * d, axis=-1, keepdims=True) / (headc - 1))
            return w * (d / (std + EPS)) + b
        key = jax.random.key(seed)
        B, N, C = (32, 256, 256)
        headc = C // HEADS
        x = jax.random.normal(key, (B, N, C), dtype=jnp.float32)
        return {'x': x, 'kln_weight': jnp.ones((HEADS, 1, headc), dtype=jnp.float32), 'kln_bias': jnp.zeros((HEADS, 1, headc), dtype=jnp.float32), 'vln_weight': jnp.ones((HEADS, 1, headc), dtype=jnp.float32), 'vln_bias': jnp.zeros((HEADS, 1, headc), dtype=jnp.float32)}
    _L1_mix_all = _L1_mix_setup()
    _L1_mix_in = {k: v for k, v in _L1_mix_all.items() if k in ('kln_weight', 'kln_bias', 'vln_weight', 'vln_bias')}
    del _L1_mix_all

    def _L1_ffn_setup():
        import jax, jax.numpy as jnp
        import numpy as np
        E = 8
        K = 2
        D = 256
        H = 512
        DOUT = 256
        EPS = 1e-05
        key = jax.random.key(seed)
        ks = jax.random.split(key, 9)
        s = 0.02
        return {'x': jax.random.normal(ks[0], (4, 512, D), jnp.float32), 'gamma': 1.0 + 0.05 * jax.random.normal(ks[1], (D,), jnp.float32), 'beta': 0.05 * jax.random.normal(ks[2], (D,), jnp.float32), 'Wr': 0.01 * jax.random.normal(ks[3], (D, E), jnp.float32), 'br': jnp.zeros((E,), jnp.float32), 'W1': s * jax.random.normal(ks[4], (E, D, H), jnp.float32), 'b1': s * jax.random.normal(ks[5], (E, H), jnp.float32), 'W2': s * jax.random.normal(ks[6], (E, H, DOUT), jnp.float32), 'b2': s * jax.random.normal(ks[7], (E, DOUT), jnp.float32)}
    _L1_ffn_all = _L1_ffn_setup()
    _L1_ffn_in = {k: v for k, v in _L1_ffn_all.items() if k in ('gamma', 'beta', 'Wr', 'br', 'W1', 'b1', 'W2', 'b2')}
    del _L1_ffn_all
    return {'x': x, 'src': src, 'dst': dst, 'edge_attr_64': edge_attr_64, 'L0_gnn_Wq': _L0_gnn_in['Wq'], 'L0_gnn_bq': _L0_gnn_in['bq'], 'L0_gnn_Wk': _L0_gnn_in['Wk'], 'L0_gnn_bk': _L0_gnn_in['bk'], 'L0_gnn_Wv': _L0_gnn_in['Wv'], 'L0_gnn_bv': _L0_gnn_in['bv'], 'L0_gnn_We': _L0_gnn_in['We'], 'L0_gnn_Wskip': _L0_gnn_in['Wskip'], 'L0_gnn_bskip': _L0_gnn_in['bskip'], 'L0_gnn_Wbeta': _L0_gnn_in['Wbeta'], 'L0_gnn_ln1_g': _L0_gnn_in['ln1_g'], 'L0_gnn_ln1_b': _L0_gnn_in['ln1_b'], 'L0_gnn_ln2_g': _L0_gnn_in['ln2_g'], 'L0_gnn_ln2_b': _L0_gnn_in['ln2_b'], 'L0_gnn_W1': _L0_gnn_in['W1'], 'L0_gnn_b1': _L0_gnn_in['b1'], 'L0_gnn_W2': _L0_gnn_in['W2'], 'L0_gnn_b2': _L0_gnn_in['b2'], 'L0_mix_wq': _L0_mix_in['wq'], 'L0_mix_bq': _L0_mix_in['bq'], 'L0_mix_wk': _L0_mix_in['wk'], 'L0_mix_bk': _L0_mix_in['bk'], 'L0_mix_wv': _L0_mix_in['wv'], 'L0_mix_bv': _L0_mix_in['bv'], 'L0_mix_wo': _L0_mix_in['wo'], 'L0_mix_bo': _L0_mix_in['bo'], 'L0_ffn_W_gat': _L0_ffn_in['W_gat'], 'L0_ffn_att_src': _L0_ffn_in['att_src'], 'L0_ffn_att_dst': _L0_ffn_in['att_dst'], 'L0_ffn_b_gat': _L0_ffn_in['b_gat'], 'L0_ffn_ln_gamma': _L0_ffn_in['ln_gamma'], 'L0_ffn_ln_beta': _L0_ffn_in['ln_beta'], 'L0_ffn_W1': _L0_ffn_in['W1'], 'L0_ffn_b1': _L0_ffn_in['b1'], 'L0_ffn_W2': _L0_ffn_in['W2'], 'L0_ffn_b2': _L0_ffn_in['b2'], 'L0_ffn_edge_index': _L0_ffn_in['edge_index'], 'L1_gnn_W1': _L1_gnn_in['W1'], 'L1_gnn_b1': _L1_gnn_in['b1'], 'L1_gnn_W2': _L1_gnn_in['W2'], 'L1_gnn_b2': _L1_gnn_in['b2'], 'L1_gnn_a': _L1_gnn_in['a'], 'L1_mix_kln_weight': _L1_mix_in['kln_weight'], 'L1_mix_kln_bias': _L1_mix_in['kln_bias'], 'L1_mix_vln_weight': _L1_mix_in['vln_weight'], 'L1_mix_vln_bias': _L1_mix_in['vln_bias'], 'L1_ffn_gamma': _L1_ffn_in['gamma'], 'L1_ffn_beta': _L1_ffn_in['beta'], 'L1_ffn_Wr': _L1_ffn_in['Wr'], 'L1_ffn_br': _L1_ffn_in['br'], 'L1_ffn_W1': _L1_ffn_in['W1'], 'L1_ffn_b1': _L1_ffn_in['b1'], 'L1_ffn_W2': _L1_ffn_in['W2'], 'L1_ffn_b2': _L1_ffn_in['b2']}

def reference(x, src, dst, edge_attr_64, L0_gnn_Wq, L0_gnn_bq, L0_gnn_Wk, L0_gnn_bk, L0_gnn_Wv, L0_gnn_bv, L0_gnn_We, L0_gnn_Wskip, L0_gnn_bskip, L0_gnn_Wbeta, L0_gnn_ln1_g, L0_gnn_ln1_b, L0_gnn_ln2_g, L0_gnn_ln2_b, L0_gnn_W1, L0_gnn_b1, L0_gnn_W2, L0_gnn_b2, L0_mix_wq, L0_mix_bq, L0_mix_wk, L0_mix_bk, L0_mix_wv, L0_mix_bv, L0_mix_wo, L0_mix_bo, L0_ffn_W_gat, L0_ffn_att_src, L0_ffn_att_dst, L0_ffn_b_gat, L0_ffn_ln_gamma, L0_ffn_ln_beta, L0_ffn_W1, L0_ffn_b1, L0_ffn_W2, L0_ffn_b2, L0_ffn_edge_index, L1_gnn_W1, L1_gnn_b1, L1_gnn_W2, L1_gnn_b2, L1_gnn_a, L1_mix_kln_weight, L1_mix_kln_bias, L1_mix_vln_weight, L1_mix_vln_bias, L1_ffn_gamma, L1_ffn_beta, L1_ffn_Wr, L1_ffn_br, L1_ffn_W1, L1_ffn_b1, L1_ffn_W2, L1_ffn_b2):
    import jax
    import jax.numpy as jnp

    def _L0_gnn_ref(x, edge_index, edge_attr, Wq, bq, Wk, bk, Wv, bv, We, Wskip, bskip, Wbeta, ln1_g, ln1_b, ln2_g, ln2_b, W1, b1, W2, b2):
        import jax, jax.numpy as jnp
        import numpy as np
        N, E, HID, HEADS, EDIM = (3125, 50000, 256, 8, 64)
        C = HID // HEADS

        def _layernorm(x, g, b, eps=1e-05):
            mu = jnp.mean(x, axis=-1, keepdims=True)
            var = jnp.var(x, axis=-1, keepdims=True)
            return (x - mu) * jax.lax.rsqrt(var + eps) * g + b

        def _transformer_conv(x, edge_index, edge_attr, Wq, bq, Wk, bk, Wv, bv, We, Wskip, bskip, Wbeta):
            n = x.shape[0]
            src, dst = (edge_index[0], edge_index[1])
            q = (x @ Wq.T + bq).reshape(n, HEADS, C)
            k = (x @ Wk.T + bk).reshape(n, HEADS, C)
            v = (x @ Wv.T + bv).reshape(n, HEADS, C)
            e = (edge_attr @ We.T).reshape(-1, HEADS, C)
            k_e = k[src] + e
            v_e = v[src] + e
            alpha = jnp.sum(q[dst] * k_e, axis=-1) / np.sqrt(C)
            amax = jax.ops.segment_max(alpha, dst, num_segments=n)
            amax = jnp.where(jnp.isfinite(amax), amax, 0.0)
            ex = jnp.exp(alpha - amax[dst])
            denom = jax.ops.segment_sum(ex, dst, num_segments=n)
            alpha = ex / (denom[dst] + 1e-16)
            out = jax.ops.segment_sum(v_e * alpha[..., None], dst, num_segments=n)
            out = out.reshape(n, HEADS * C)
            x_r = x @ Wskip.T + bskip
            beta = jax.nn.sigmoid(jnp.concatenate([out, x_r, out - x_r], axis=-1) @ Wbeta.T)
            return beta * x_r + (1.0 - beta) * out
        h = _transformer_conv(x, edge_index, edge_attr, Wq, bq, Wk, bk, Wv, bv, We, Wskip, bskip, Wbeta)
        x = _layernorm(x + h, ln1_g, ln1_b)
        h = jax.nn.gelu(x @ W1.T + b1, approximate=False) @ W2.T + b2
        return _layernorm(x + h, ln2_g, ln2_b)

    def _L0_mix_ref(x, wq, bq, wk, bk, wv, bv, wo, bo):
        import jax, jax.numpy as jnp
        import numpy as np
        D_MODEL = 256
        NUM_HEADS = 8
        DEPTH = D_MODEL // NUM_HEADS
        B, L = (32, 256)

        def _feature_map(x):
            return jax.nn.elu(x) + 1.0
        b, l, _ = x.shape
        q = (x @ wq + bq).reshape(b, l, NUM_HEADS, DEPTH)
        k = (x @ wk + bk).reshape(b, l, NUM_HEADS, DEPTH)
        v = (x @ wv + bv).reshape(b, l, NUM_HEADS, DEPTH)
        q = _feature_map(q)
        k = _feature_map(k)
        kv = jnp.einsum('blhd,blhe->bhde', k, v)
        k_sum = jnp.sum(k, axis=1)
        qkv = jnp.einsum('blhd,bhde->blhe', q, kv)
        normalizer = jnp.einsum('blhd,bhd->blh', q, k_sum) + 1e-06
        out = qkv / normalizer[..., None]
        out = out.reshape(b, l, D_MODEL)
        return out @ wo + bo

    def _L0_ffn_ref(x, W_gat, att_src, att_dst, b_gat, ln_gamma, ln_beta, W1, b1, W2, b2, edge_index):
        import jax, jax.numpy as jnp
        import numpy as np
        B, N, D = (16, 256, 256)
        NUM_EXPERTS, TOP_K, HEADS = (4, 2, 4)
        N_EDGES = 65536
        LN_EPS = 1e-05

        def _layernorm(x, g, b):
            mu = x.mean(-1, keepdims=True)
            var = ((x - mu) ** 2).mean(-1, keepdims=True)
            return (x - mu) * jax.lax.rsqrt(var + LN_EPS) * g + b

        def _forward(x, edge_index, W_gat, att_src, att_dst, b_gat, ln_gamma, ln_beta, W1, b1, W2, b2):
            Bc, Nc, Dc = x.shape
            M = Bc * Nc
            x_flat = x.reshape(M, Dc)
            h = (x_flat @ W_gat).reshape(M, HEADS, NUM_EXPERTS)
            loops = jnp.arange(M, dtype=edge_index.dtype)
            src = jnp.concatenate([edge_index[0], loops])
            dst = jnp.concatenate([edge_index[1], loops])
            a_src = (h * att_src).sum(-1)
            a_dst = (h * att_dst).sum(-1)
            e = jax.nn.leaky_relu(a_src[src] + a_dst[dst], negative_slope=0.2)
            e_max = jax.ops.segment_max(e, dst, num_segments=M)
            ee = jnp.exp(e - e_max[dst])
            denom = jax.ops.segment_sum(ee, dst, num_segments=M)
            alpha = ee / (denom[dst] + 1e-16)
            msg = h[src] * alpha[:, :, None]
            agg = jax.ops.segment_sum(msg, dst, num_segments=M).reshape(M, HEADS * NUM_EXPERTS) + b_gat
            scores = _layernorm(agg, ln_gamma, ln_beta).reshape(M, HEADS, NUM_EXPERTS).mean(1)
            scores = scores.reshape(Bc, Nc, NUM_EXPERTS)
            topk_s, topk_i = jax.lax.top_k(scores, TOP_K)
            w = jax.nn.softmax(topk_s, axis=-1)
            out = jnp.zeros_like(x)
            for ei in range(NUM_EXPERTS):
                g = jnp.where(topk_i == ei, w, 0.0).sum(-1)
                hh = jax.nn.gelu(x @ W1[ei] + b1[ei], approximate=False)
                out = out + g[..., None] * (hh @ W2[ei] + b2[ei])
            return out
        return _forward(x, edge_index, W_gat, att_src, att_dst, b_gat, ln_gamma, ln_beta, W1, b1, W2, b2)

    def _L1_gnn_ref(x, edge_index, W1, b1, W2, b2, a):
        import jax, jax.numpy as jnp
        import numpy as np
        N_NODES = 6250
        F_DIM = 256
        NNZ = 100000

        def _prelu(x, a):
            return jnp.where(x >= 0, x, a * x)

        def _hconv(x, W, b, src, dst, n):
            xt = x @ W
            ones = jnp.ones(src.shape, xt.dtype)
            D = jax.ops.segment_sum(ones, src, num_segments=n)
            B = jax.ops.segment_sum(ones, dst, num_segments=n)
            Dinv = jnp.where(D > 0, 1.0 / D, 0.0)
            Binv = jnp.where(B > 0, 1.0 / B, 0.0)
            m = jax.ops.segment_sum(xt[src], dst, num_segments=n) * Binv[:, None]
            out = jax.ops.segment_sum(m[dst], src, num_segments=n) * Dinv[:, None]
            return out + b
        src, dst = (edge_index[0], edge_index[1])
        n = x.shape[0]
        h = _prelu(_hconv(x, W1, b1, src, dst, n), a)
        h = _hconv(h, W2, b2, src, dst, n) + x
        return _prelu(h, a)

    def _L1_mix_ref(x, kln_weight, kln_bias, vln_weight, vln_bias):
        import jax, jax.numpy as jnp
        import numpy as np
        HEADS = 8
        EPS = 1e-05

        def _ln(t, w, b, headc):
            m = jnp.mean(t, axis=-1, keepdims=True)
            d = t - m
            std = jnp.sqrt(jnp.sum(d * d, axis=-1, keepdims=True) / (headc - 1))
            return w * (d / (std + EPS)) + b
        B, N, C = x.shape
        headc = C // HEADS
        qkv = x.reshape(B, N, HEADS, headc).transpose(0, 2, 1, 3)
        k = _ln(qkv, kln_weight, kln_bias, headc)
        v = _ln(qkv, vln_weight, vln_bias, headc)
        kv = jnp.einsum('bhnd,bhne->bhde', k, v) / N
        out = jnp.einsum('bhnd,bhde->bhne', qkv, kv)
        out = out.transpose(0, 2, 1, 3).reshape(B, N, C)
        return out + x

    def _L1_ffn_ref(x, gamma, beta, Wr, br, W1, b1, W2, b2):
        import jax, jax.numpy as jnp
        import numpy as np
        E = 8
        K = 2
        D = 256
        H = 512
        DOUT = 256
        EPS = 1e-05
        mu = jnp.mean(x, axis=-1, keepdims=True)
        var = jnp.mean(jnp.square(x - mu), axis=-1, keepdims=True)
        xn = (x - mu) * jax.lax.rsqrt(var + EPS) * gamma + beta
        logits = jnp.einsum('bsd,de->bse', xn, Wr) + br
        top_vals, top_idx = jax.lax.top_k(logits, K)
        w = jax.nn.softmax(top_vals, axis=-1)
        w_full = jnp.einsum('bsk,bske->bse', w, jax.nn.one_hot(top_idx, E, dtype=w.dtype))
        y = jnp.zeros(x.shape[:-1] + (DOUT,), x.dtype)
        for e in range(E):
            h = jax.nn.gelu(jnp.einsum('bsd,dh->bsh', xn, W1[e]) + b1[e], approximate=False)
            y_e = jnp.einsum('bsh,hd->bsd', h, W2[e]) + b2[e]
            y = y + y_e * w_full[..., e, None]
        return y
    edge_index = jnp.stack([src, dst])
    xn = _layernorm(x, axis=-1)
    x = x + _L0_gnn_ref(xn, edge_index, edge_attr_64, L0_gnn_Wq, L0_gnn_bq, L0_gnn_Wk, L0_gnn_bk, L0_gnn_Wv, L0_gnn_bv, L0_gnn_We, L0_gnn_Wskip, L0_gnn_bskip, L0_gnn_Wbeta, L0_gnn_ln1_g, L0_gnn_ln1_b, L0_gnn_ln2_g, L0_gnn_ln2_b, L0_gnn_W1, L0_gnn_b1, L0_gnn_W2, L0_gnn_b2) + _L0_mix_ref(xn[None], L0_mix_wq, L0_mix_bq, L0_mix_wk, L0_mix_bk, L0_mix_wv, L0_mix_bv, L0_mix_wo, L0_mix_bo)[0]
    x = x + _L0_ffn_ref(_layernorm(x, axis=-1)[None], L0_ffn_W_gat, L0_ffn_att_src, L0_ffn_att_dst, L0_ffn_b_gat, L0_ffn_ln_gamma, L0_ffn_ln_beta, L0_ffn_W1, L0_ffn_b1, L0_ffn_W2, L0_ffn_b2, L0_ffn_edge_index)[0]
    xn = _layernorm(x, axis=-1)
    x = x + _L1_gnn_ref(xn, edge_index, L1_gnn_W1, L1_gnn_b1, L1_gnn_W2, L1_gnn_b2, L1_gnn_a) + _L1_mix_ref(xn[None], L1_mix_kln_weight, L1_mix_kln_bias, L1_mix_vln_weight, L1_mix_vln_bias)[0]
    x = x + _L1_ffn_ref(_layernorm(x, axis=-1)[None], L1_ffn_gamma, L1_ffn_beta, L1_ffn_Wr, L1_ffn_br, L1_ffn_W1, L1_ffn_b1, L1_ffn_W2, L1_ffn_b2)[0]
    return x

_drawn_inputs = setup_inputs


def setup_inputs(seed=0):
    import zlib

    import numpy as np

    out = dict(_drawn_inputs(seed))
    spreads = {'L0_gnn_bq': (0.0, 0.788),
     'L0_gnn_bk': (0.0, 2.0),
     'L0_gnn_bv': (0.0, 0.1),
     'L0_gnn_bskip': (0.0, 0.1),
     'L0_gnn_ln1_g': (1.0, 0.2),
     'L0_gnn_ln1_b': (0.0, 0.1),
     'L0_gnn_ln2_g': (1.0, 0.2),
     'L0_gnn_ln2_b': (0.0, 0.1),
     'L0_gnn_b1': (0.0, 0.357),
     'L0_gnn_b2': (0.0, 0.1),
     'L0_mix_bq': (0.0, 2.0),
     'L0_mix_bk': (0.0, 2.0),
     'L0_mix_bv': (0.0, 0.1),
     'L0_mix_bo': (0.0, 0.1),
     'L0_ffn_b_gat': (0.0, 0.1),
     'L0_ffn_ln_gamma': (1.0, 0.2),
     'L0_ffn_ln_beta': (0.0, 0.1),
     'L0_ffn_b1': (0.0, 0.283),
     'L0_ffn_b2': (0.0, 0.1),
     'L1_gnn_b1': (0.0, 0.511),
     'L1_gnn_b2': (0.0, 0.491),
     'L1_mix_kln_weight': (1.0, 0.2),
     'L1_mix_kln_bias': (0.0, 0.414),
     'L1_mix_vln_weight': (1.0, 0.2),
     'L1_mix_vln_bias': (0.0, 0.4),
     'L1_ffn_br': (0.0, 0.8)}
    factors = {'L0_gnn_Wk': 3.166,
     'L0_mix_wq': 8.0,
     'L0_mix_wk': 3.936,
     'L0_ffn_att_dst': 3.331,
     'L1_ffn_gamma': 8.0,
     'L1_ffn_beta': 8.0,
     'L1_ffn_Wr': 5.741,
     'L1_ffn_W1': 5.0,
     'L1_ffn_b1': 36.197,
     'L1_ffn_W2': 4.866,
     'L1_ffn_b2': 58.626}
    for name, (base, spread) in spreads.items():
        noise = np.random.default_rng([zlib.crc32(name.encode()), seed]).standard_normal(out[name].shape)
        drawn = base * np.exp(spread * noise) if base else spread * noise
        out[name] = jnp.asarray(drawn.astype(out[name].dtype))
    for name, factor in factors.items():
        out[name] = (out[name] * factor).astype(out[name].dtype)
    return out
```

```python
from contextlib import ExitStack, nullcontext

import concourse.bass as bass
from concourse import mybir

P = 128
ALU = mybir.AluOpType
ACT = mybir.ActivationFunctionType
F32 = mybir.dt.float32
BF16 = mybir.dt.bfloat16
I32 = mybir.dt.int32
AX = mybir.AxisListType.X

N = 3125
D = 256
NB = -(-N // P)
NPAD = NB * P
BINS = 32
TOP = BINS * P - 1
UN = 8
GE = 2 * P
FAR = float(1 << 20)
LOW = -1.0e38


class EdgeList:

    def __init__(self, name, edges, heads, attr):
        self.name = name
        self.heads = heads
        self.attr = attr
        self.width = attr + 4
        self.chunks = -(-edges // (P * 2 * UN)) * 2 * UN
        self.groups = -(-((edges + NB * GE) // GE) // 8) * 8
        self.pieces = P // heads
        self.per_piece = -(-self.groups // self.pieces)
        self.all_groups = self.per_piece * self.pieces
        self.places = self.all_groups * GE


CONV = EdgeList("conv", 103125, 8, 64)
GAT = EdgeList("gat", 65536 + N, 4, 0)


class Chain:

    def __init__(self, engine, sem, base=0):
        self.engine, self.sem, self.base, self.n = engine, sem, base, 0

    def __call__(self, instruction):
        self.n += 1
        instruction.then_inc(self.sem, 1)
        self.engine.wait_ge(self.sem, self.base + self.n)


class Steps:

    def __init__(self, engine, sem, per):
        self.engine, self.sem, self.per, self.n = engine, sem, per, 0

    def at(self, number):
        assert self.n in (0, self.per), self.n
        self.number, self.n = number, 0

    def __call__(self, instruction):
        self.n += 1
        instruction.then_inc(self.sem, 1)
        self.engine.wait_ge(self.sem, self.number * self.per + self.n)


class Tools:

    def __init__(self, nc, phase, ctx):
        self.nc, self.phase, self.ctx, self.sems = nc, phase, ctx, []

    def sb(self, name, shape, dt=F32):
        return self.ctx.enter_context(self.nc.sbuf_tensor(f"{self.phase}_{name}", shape, dt))

    def ps(self, name, shape, dt=F32):
        return self.ctx.enter_context(self.nc.psum_tensor(f"{self.phase}_{name}", shape, dt))

    def sem(self, name):
        if not self.sems:
            self.ctx.callback(self.clear)
        self.sems.append(self.nc.alloc_semaphore(name=f"{self.phase}_{name}"))
        return self.sems[-1]

    def clear(self):
        self.nc.clear_and_free_semaphores(self.sems)
        self.nc.all_engine_barrier()


def make_constants(nc, t):
    k = {
        "iota_row": t.sb("iota_row", [P, P]),
        "iota_bf": t.sb("iota_bf", [P, P], BF16),
        "iota_col": t.sb("iota_col", [P, 1]),
        "ident": t.sb("ident", [P, P]),
        "before": t.sb("before", [P, P]),
        "minus_half": t.sb("minus_half", [P, 1]),
        "same_head": t.sb("same_head", [P, P]),
        "before_bf": t.sb("before_bf", [P, P], BF16),
        "ones": t.sb("ones", [P, P]),
        "exists": t.sb("exists", [P, BINS]),
        "group_start": t.sb("group_start", [P, 4]),
    }
    s_iota, s_dve = t.sem("iota"), t.sem("dve")
    row_i = t.sb("row_i", [P, P], I32)
    col_i = t.sb("col_i", [P, 1], I32)
    node_i = t.sb("node_i", [P, BINS], I32)
    group_i = t.sb("group_i", [P, 4], I32)
    col_f = t.sb("col_f", [P, 1])
    with nc.Block() as block:

        @block.gpsimd
        def _(pool):
            pool.iota(row_i[:], pattern=[[1, P]], base=0, channel_multiplier=0).then_inc(s_iota, 1)
            pool.iota(col_i[:], pattern=[[0, 1]], base=0, channel_multiplier=1).then_inc(s_iota, 1)
            pool.iota(node_i[:], pattern=[[P, BINS]], base=0, channel_multiplier=1).then_inc(s_iota, 1)
            pool.iota(group_i[:], pattern=[[P, 4]], base=0, channel_multiplier=1).then_inc(s_iota, 1)

        @block.vector
        def _(dve):
            link = Chain(dve, s_dve)
            dve.wait_ge(s_iota, 4)
            link(dve.memset(k["ones"][:], 1.0))
            link(dve.memset(k["minus_half"][:], -0.5))
            link(dve.tensor_copy(k["iota_row"][:], row_i[:]))
            link(dve.tensor_copy(k["iota_bf"][:], row_i[:]))
            link(dve.tensor_copy(k["iota_col"][:], col_i[:]))
            link(dve.tensor_copy(k["exists"][:], node_i[:]))
            link(dve.tensor_copy(k["group_start"][:], group_i[:]))
            link(dve.tensor_scalar(k["exists"][:], k["exists"][:], float(N), None, ALU.is_lt))
            link(dve.tensor_scalar(k["group_start"][:], k["group_start"][:], float(GE), None, ALU.mult))
            link(dve.tensor_scalar(k["ident"][:], k["iota_row"][:], k["iota_col"][:, 0:1], None, ALU.is_equal))
            link(dve.tensor_scalar(k["before"][:], k["iota_row"][:], k["iota_col"][:, 0:1], None, ALU.is_gt))
            link(dve.tensor_copy(k["before_bf"][:], k["before"][:]))
            link(dve.tensor_scalar(row_i[:], row_i[:], 5, None, ALU.logical_shift_right))
            link(dve.tensor_scalar(col_i[:], col_i[:], 5, None, ALU.logical_shift_right))
            link(dve.tensor_copy(k["same_head"][:], row_i[:]))
            link(dve.tensor_copy(col_f[:], col_i[:]))
            link(dve.tensor_scalar(k["same_head"][:], k["same_head"][:], col_f[:, 0:1], None, ALU.is_equal))
    return k


def sort_edges(nc, L, k, table, dst_rows, dst_cols, src_cols, attr, lo_dram, table_dram, sorted_rows):
    C, W, A = L.chunks, L.width, L.attr
    with ExitStack() as ctx:
        t = Tools(nc, f"sort_{L.name}", ctx)
        meta = t.sb("meta", [P, C, 4], I32)
        lo = t.sb("lo", [P, C])
        hi = t.sb("hi", [P, C])
        places = t.sb("places", [P, BINS])
        with ExitStack() as inner:
            u = Tools(nc, f"count_{L.name}", inner)
            dst_i = u.sb("dst_i", [P, C], I32)
            src_i = u.sb("src_i", [P, C], I32)
            hi_i = u.sb("hi_i", [P, C], I32)
            row_i = u.sb("row_i", [P, C], I32)
            row_f = u.sb("row_f", [P, C])
            fill = u.sb("fill", [P, L.per_piece * 2, W], I32)
            lo_hot = u.sb("lo_hot", [P, 2, UN, P], BF16)
            hi_hot = u.sb("hi_hot", [P, 2, UN, BINS], BF16)
            zero = u.sb("zero", [P, P], BF16)
            cnt = u.sb("cnt", [P, BINS])
            total_i = u.sb("total_i", [P, BINS], I32)
            padded = u.sb("padded", [P, NB])
            end = u.sb("end", [P, NB])
            tmp = u.sb("tmp", [P, BINS])
            onesrow = u.sb("onesrow", [P, NB])
            cmp = u.sb("cmp", [P, 4, NB])
            group_end = u.sb("group_end", [P, 4])
            found = u.sb("found", [P, 4])
            found_i = u.sb("found_i", [P, 2, 4], I32)
            bits = u.sb("bits", [1, 64, 8])
            not_end = u.sb("not_end", [1, 64, 8])
            word = u.sb("word", [1, 2, 64])
            hist = u.ps("hist", [P, BINS])
            totals = u.ps("totals", [P, BINS])
            prefix = u.ps("prefix", [P, BINS])
            s_in, s_row, s_rowf, s_fill, s_filled = (u.sem(x) for x in ("in", "row", "rowf", "fill", "filled"))
            s_prep, s_hot, s_counted, s_cnt, s_sums = (u.sem(x) for x in ("prep", "hot", "counted", "cnt", "sums"))
            s_dve, s_tab, s_tabd, s_lo = (u.sem(x) for x in ("dve", "tab", "tabd", "lo"))
            NF = L.places // (P * L.per_piece * 2)

            with nc.Block() as block:

                @block.sync
                def _(sp):
                    sp.dma_start(dst_i[:], dst_cols).then_inc(s_in, 16)
                    sp.dma_start(src_i[:], src_cols).then_inc(s_in, 16)
                    sp.dma_start(row_i[:], dst_rows.rearrange("(p c) -> p c", p=P)).then_inc(s_row, 16)
                    sp.wait_ge(s_rowf, 1)
                    sp.dma_start(lo_dram.rearrange("(p c) -> p c", p=P), row_f[:]).then_inc(s_lo, 16)
                    sp.wait_ge(s_fill, 3)
                    view = sorted_rows.rearrange("(f p c) w -> f p (c w)", f=NF, p=P)
                    for f in range(NF):
                        sp.dma_start(view[f], fill[:].rearrange("p c w -> p (c w)")).then_inc(s_filled, 16)
                    sp.wait_ge(s_tab, 2)
                    sp.dma_start(table_dram.rearrange("a (q p) -> p a q", p=P), found_i[:]).then_inc(s_tabd, 16)
                    sp.wait_ge(s_tabd, 16)
                    sp.dma_start(table[:, 0:1024], table_dram.rearrange("a g -> (a g)").rearrange("(o g) -> o g", o=1)
                                 ).then_inc(s_tabd, 16)
                    sp.wait_ge(s_tabd, 32)
                    sp.wait_ge(s_lo, 16)
                    sp.wait_ge(s_filled, 16 * NF)

                @block.gpsimd
                def _(pool):
                    pool.memset(zero[:], 0.0).then_inc(s_fill, 1)
                    pool.memset(fill[:], 0).then_inc(s_fill, 1)
                    pool.wait_ge(s_fill, 2)
                    pool.memset(fill[:, :, A + 1:A + 3], -1).then_inc(s_fill, 1)

                @block.vector
                def _(dve):
                    link = Chain(dve, s_dve)
                    dve.wait_ge(s_in, 32)
                    link(dve.tensor_scalar(dst_i[:], dst_i[:], float(TOP), None, ALU.min))
                    link(dve.tensor_scalar(hi_i[:], dst_i[:], 7, None, ALU.logical_shift_right))
                    link(dve.tensor_copy(hi[:], hi_i[:]))
                    link(dve.memset(meta[:], 0))
                    link(dve.tensor_scalar(meta[:, :, 0], src_i[:], float(N - 1), None, ALU.min))
                    link(dve.tensor_copy(meta[:, :, 1], dst_i[:]))
                    link(dve.tensor_scalar(meta[:, :, 2], dst_i[:], 127, None, ALU.bitwise_and))
                    link(dve.tensor_copy(lo[:], meta[:, :, 2]))
                    dve.wait_ge(s_row, 16)
                    link(dve.tensor_scalar(row_i[:], row_i[:], float(TOP), None, ALU.min))
                    link(dve.tensor_scalar(row_i[:], row_i[:], 127, None, ALU.bitwise_and))
                    dve.tensor_copy(row_f[:], row_i[:]).then_inc(s_rowf, 1)
                    with dve.Fori(0, C // (2 * UN)) as i:
                        for h in range(2):
                            c0 = i * (2 * UN) + h * UN
                            dve.wait_ge(s_counted, i * 2 + (h + 1))
                            dve.tensor_tensor(
                                lo_hot[:, h], k["iota_row"][:].unsqueeze(1).to_broadcast([P, UN, P]),
                                lo[:, bass.ds(c0, UN)].unsqueeze(2).to_broadcast([P, UN, P]), ALU.is_equal)
                            dve.tensor_tensor(
                                hi_hot[:, h], k["iota_row"][:, 0:BINS].unsqueeze(1).to_broadcast([P, UN, BINS]),
                                hi[:, bass.ds(c0, UN)].unsqueeze(2).to_broadcast([P, UN, BINS]),
                                ALU.is_equal).then_inc(s_hot, 1)
                    dve.wait_ge(s_counted, 2 + C // UN)
                    dve.tensor_tensor(cnt[:], hist[:], k["exists"][:], ALU.mult).then_inc(s_cnt, 1)
                    dve.wait_ge(s_sums, 1)
                    link(dve.tensor_scalar(tmp[:], totals[:], float(GE - 1), None, ALU.add))
                    link(dve.tensor_copy(total_i[:], tmp[:]))
                    link(dve.tensor_scalar(total_i[:], total_i[:], 8, None, ALU.logical_shift_right))
                    link(dve.tensor_copy(tmp[:], total_i[:]))
                    link(dve.tensor_scalar(padded[:], tmp[:, 0:NB], 1.0, float(GE), ALU.max, ALU.mult))
                    link(dve.memset(onesrow[:], 1.0))
                    link(dve.tensor_tensor_scan(end[:], onesrow[:], padded[:], 0.0, ALU.mult, ALU.add))
                    link(dve.tensor_scalar(tmp[:], k["exists"][:], -FAR, FAR, ALU.mult, ALU.add))
                    link(dve.tensor_tensor(places[:], prefix[:], tmp[:], ALU.add))
                    link(dve.tensor_tensor(places[:, 0:NB], places[:, 0:NB], end[:], ALU.add))
                    link(dve.tensor_tensor(places[:, 0:NB], places[:, 0:NB], padded[:], ALU.subtract))
                    ends = end[:].unsqueeze(1).to_broadcast([P, 4, NB])
                    link(dve.tensor_tensor(
                        cmp[:], ends, k["group_start"][:].unsqueeze(2).to_broadcast([P, 4, NB]), ALU.is_le))
                    link(dve.tensor_reduce(found[:], cmp[:], AX, ALU.add))
                    link(dve.tensor_scalar(found[:], found[:], float(NB - 1), None, ALU.min))
                    dve.tensor_copy(found_i[:, 0], found[:]).then_inc(s_tab, 1)
                    link(dve.tensor_scalar(group_end[:], k["group_start"][:], float(GE), None, ALU.add))
                    link(dve.tensor_tensor(
                        cmp[:], ends, group_end[:].unsqueeze(2).to_broadcast([P, 4, NB]), ALU.is_equal))
                    dve.wait_ge(s_tab, 1)
                    link(dve.tensor_reduce(found[:], cmp[:], AX, ALU.add))
                    dve.tensor_copy(found_i[:, 1], found[:]).then_inc(s_tab, 1)
                    blocks, lasts = (table[:, a * 512:a * 512 + 512].rearrange("o (i r) -> o i r", r=8)
                                     for a in range(2))
                    dve.wait_ge(s_tabd, 32)
                    link(dve.tensor_copy(bits[:], lasts))
                    for r in range(1, 8):
                        link(dve.tensor_scalar(bits[:, :, r:r + 1], bits[:, :, r:r + 1], float(1 << r), None, ALU.mult))
                    link(dve.tensor_reduce(word[:, 0], bits[:], AX, ALU.add))
                    link(dve.tensor_copy(table[:, 1088:1152], word[:, 0]))
                    link(dve.tensor_scalar(not_end[:], blocks, float(NB - 1), None, ALU.is_lt))
                    link(dve.tensor_tensor(bits[:], bits[:], not_end[:], ALU.mult))
                    link(dve.tensor_reduce(word[:, 0], bits[:], AX, ALU.add))
                    link(dve.tensor_copy(word[:, 1], blocks[:, :, 0]))
                    link(dve.tensor_scalar(word[:, 1], word[:, 1], 256.0, None, ALU.mult))
                    link(dve.tensor_tensor(word[:, 0], word[:, 0], word[:, 1], ALU.add))
                    link(dve.tensor_copy(table[:, 1024:1088], word[:, 0]))

                @block.tensor
                def _(pe):
                    pe.wait_ge(s_fill, 1)
                    pe.matmul(hist[:], zero[:], zero[:, 0:BINS], start=True, stop=False,
                              skip_group_check=True).then_inc(s_counted, 1)
                    pe.matmul(hist[:], zero[:], zero[:, 0:BINS], start=False, stop=False,
                              skip_group_check=True).then_inc(s_counted, 1)
                    with pe.Fori(0, C // (2 * UN)) as i:
                        for h in range(2):
                            pe.wait_ge(s_hot, i * 2 + (h + 1))
                            for j in range(UN):
                                last = pe.matmul(hist[:], lo_hot[:, h, j], hi_hot[:, h, j], start=False,
                                                 stop=False, skip_group_check=True)
                            last.then_inc(s_counted, 1)
                    pe.wait_ge(s_cnt, 1)
                    pe.matmul(totals[:], k["ones"][:], cnt[:], start=True, stop=True)
                    pe.matmul(prefix[:], k["before"][:], cnt[:], start=True, stop=True).then_inc(s_sums, 1)

        with ExitStack() as inner:
            u = Tools(nc, f"place_{L.name}", inner)
            rows = u.sb("rows", [P, 2, UN, W], I32)
            lo_row = u.sb("lo_row", [P, 2, UN * P])
            lo_hot = u.sb("lo_hot", [P, 2, UN, P], BF16)
            hi_hot = u.sb("hi_hot", [P, 2, UN, BINS], BF16)
            lo_hot_t = u.sb("lo_hot_t", [P, 2, UN * P])
            earlier = u.sb("earlier", [P, 2, UN, P], BF16)
            zero = u.sb("zero", [P, P], BF16)
            snap = u.sb("snap", [P, 2, BINS])
            masked = u.sb("masked", [P, 2, UN, BINS])
            where = u.sb("where", [P, 2, UN])
            where_i = u.sb("where_i", [P, 2, UN], I32)
            running = u.ps("running", [P, BINS])
            looked = u.ps("looked", [P, 2, 512])
            s_zero, s_base, s_snap, s_run, s_look, s_dve, s_hot, s_where = (
                u.sem(x) for x in ("zero", "base", "snap", "run", "look", "dve", "hot", "where"))
            s_lo = [u.sem(f"lo{h}") for h in range(2)]
            s_attr = [u.sem(f"attr{h}") for h in range(2)]
            s_meta = u.sem("meta")
            s_out = [u.sem(f"out{h}") for h in range(2)]
            s_go = u.sem("go")
            STEPS = C // (2 * UN)

            with nc.Block() as block:

                @block.sync
                def _(sp):
                    attr_v = attr.rearrange("(c p) f -> p c f", p=P) if A else None
                    with sp.Fori(0, STEPS) as i:
                        for h in range(2):
                            c0 = i * (2 * UN) + h * UN
                            sp.wait_ge(s_hot, i * 2 + h)
                            src = lo_dram.rearrange("(o e) -> o e", o=1)[:, bass.ds(c0 * P, UN * P)]
                            sp.dma_start(lo_row[:, h], src.to_broadcast([P, UN * P])).then_inc(s_lo[h], 16)
                            if A:
                                sp.wait_ge(s_out[h], i * (16 * UN))
                                sp.dma_start(rows[:, h, :, 0:A].bitcast(F32), attr_v[:, bass.ds(c0, UN), :]
                                             ).then_inc(s_attr[h], 16)

                @block.scalar
                def _(act):
                    act.copy(snap[:, 0], places[:]).then_inc(s_snap, 1)
                    act.wait_ge(s_snap, 1)
                    with act.Fori(0, STEPS) as i:
                        for h in range(2):
                            c0 = i * (2 * UN) + h * UN
                            for j in range(UN):
                                act.wait_ge(s_run, i * (2 * UN) + (h * UN + j + 1))
                                act.wait_ge(s_look, i * (2 * UN) + (h * UN + j))
                                act.copy(snap[:, j % 2], running[:]).then_inc(s_snap, 1)
                            act.wait_ge(s_out[h], i * (16 * UN))
                            act.copy(rows[:, h, :, A:A + 4], meta[:, bass.ds(c0, UN), :]).then_inc(s_meta, 1)

                @block.tensor
                def _(pe):
                    pe.wait_ge(s_zero, 1)
                    pe.matmul(running[:], zero[:], zero[:, 0:BINS], start=True, stop=False,
                              skip_group_check=True)
                    pe.matmul(running[:], k["ident"][:], places[:], start=False, stop=False,
                              skip_group_check=True).then_inc(s_run, 1)
                    pe.matmul(looked[:, 0, 0:BINS], zero[:], zero[:, 0:BINS], start=True, stop=True
                              ).then_inc(s_look, 1)
                    with pe.Fori(0, STEPS) as i:
                        for h in range(2):
                            pe.wait_ge(s_hot, i * 2 + (h + 2))
                            pe.wait_ge(s_where, i * 2 + h)
                            for j in range(UN):
                                out = looked[:, h, j * BINS:(j + 1) * BINS]
                                pe.wait_ge(s_snap, i * (2 * UN) + (h * UN + j + 2))
                                pe.matmul(running[:], lo_hot[:, h, j], hi_hot[:, h, j], start=False,
                                          stop=False, skip_group_check=True).then_inc(s_run, 1)
                                pe.matmul(out, lo_hot_t[:, h, j * P:(j + 1) * P], snap[:, j % 2],
                                          start=True, stop=False)
                                pe.matmul(out, earlier[:, h, j], hi_hot[:, h, j], start=False,
                                          stop=True).then_inc(s_look, 1)

                @block.vector
                def _(dve):
                    def codes(h, c0, landed):
                        dve.tensor_tensor(
                            lo_hot[:, h], k["iota_row"][:].unsqueeze(1).to_broadcast([P, UN, P]),
                            lo[:, bass.ds(c0, UN)].unsqueeze(2).to_broadcast([P, UN, P]), ALU.is_equal)
                        dve.tensor_tensor(
                            hi_hot[:, h], k["iota_row"][:, 0:BINS].unsqueeze(1).to_broadcast([P, UN, BINS]),
                            hi[:, bass.ds(c0, UN)].unsqueeze(2).to_broadcast([P, UN, BINS]), ALU.is_equal)
                        dve.wait_ge(s_lo[h], landed)
                        dve.tensor_scalar(lo_hot_t[:, h], lo_row[:, h], k["iota_col"][:, 0:1], None, ALU.is_equal)
                        for j in range(UN):
                            last = dve.scalar_tensor_tensor(
                                earlier[:, h, j], lo_row[:, h, j * P:(j + 1) * P], lo[:, bass.ds(c0 + j, 1)],
                                k["before"][:], ALU.is_equal, ALU.mult)
                        last.then_inc(s_hot, 1)

                    def find(h, i):
                        dve.wait_ge(s_look, i * (2 * UN) + ((h + 1) * UN + 1))
                        dve.tensor_tensor(masked[:, h], looked[:, h, 0:UN * BINS].rearrange(
                            "p (j b) -> p j b", j=UN), hi_hot[:, h], ALU.mult).then_inc(s_dve, 1)
                        dve.wait_ge(s_dve, i * 4 + (h * 2 + 1))
                        dve.tensor_reduce(where[:, h], masked[:, h], AX, ALU.add).then_inc(s_dve, 1)
                        dve.wait_ge(s_dve, i * 4 + (h * 2 + 2))
                        dve.wait_ge(s_out[h], i * (16 * UN))
                        dve.tensor_copy(where_i[:, h], where[:, h]).then_inc(s_where, 1)

                    dve.memset(zero[:], 0.0).then_inc(s_zero, 1)
                    dve.memset(where[:], 0.0).then_inc(s_hot, 1)
                    dve.memset(where_i[:], 0).then_inc(s_where, 1)
                    dve.wait_ge(s_hot, 1)
                    dve.wait_ge(s_where, 1)
                    codes(0, 0, 16)
                    with dve.Fori(0, STEPS - 1) as i:
                        codes(1, i * (2 * UN) + UN, i * 16 + 16)
                        find(0, i)
                        codes(0, i * (2 * UN) + 2 * UN, i * 16 + 32)
                        find(1, i)
                    codes(1, (STEPS - 1) * 2 * UN + UN, STEPS * 16)
                    find(0, STEPS - 1)
                    find(1, STEPS - 1)

                @block.gpsimd
                def _(pool):
                    most = pool.to_reg(L.places - 1)
                    with pool.Fori(0, STEPS) as i:
                        for h in range(2):
                            pool.wait_ge(s_where, i * 2 + (h + 2))
                            pool.wait_ge(s_meta, i * 2 + (h + 1))
                            if A:
                                pool.wait_ge(s_attr[h], i * 16 + 16)
                            pool.sem_inc(s_go, 1)
                            for j in range(UN):
                                pool.indirect_dma_start(
                                    out=sorted_rows, out_offset=bass.IndirectOffsetOnAxis(
                                        ap=where_i[:, h, j:j + 1], axis=0),
                                    in_=rows[:, h, j], in_offset=None, bounds_check=most,
                                    oob_is_err=False).then_inc(s_out[h], 16)
                    for h in range(2):
                        pool.wait_ge(s_out[h], STEPS * 16 * UN)


def per_tile(engine, body):
    with engine.Fori(0, NB // 2) as i:
        body(i, 0)
        body(i, 1)
    body(NB // 2, 0)


class Norm:

    def __init__(self, k, t, per=1):
        self.per, self.half = per, k["minus_half"][:]
        self.stats = t.sb("ln_stats", [P, 6])
        self.mv = t.sb("ln_mv", [P, per, 2])
        self.rstd = t.sb("ln_rstd", [P, per])
        self.s_var, self.s_rstd, self.s_carry = t.sem("ln_var"), t.sem("ln_rstd"), t.sem("ln_carry")

    def power(self, pool, tt, j=0):
        pool.wait_ge(self.s_var, tt * self.per + (j + 1))
        pool.sem_inc(self.s_carry, 1)
        pool.tensor_tensor(self.rstd[:, j:j + 1], self.mv[:, j, 1:2], self.half, ALU.pow
                           ).then_inc(self.s_rstd, 1)

    def __call__(self, dve, link, out, x, tt, j=0):
        link(dve.bn_stats(self.stats[:], x))
        dve.sem_inc(self.s_carry, 1)
        link(dve.bn_aggr(self.mv[:, j], self.stats[:]))
        dve.tensor_scalar(self.mv[:, j, 1:2], self.mv[:, j, 1:2], 1e-5, None, ALU.add).then_inc(self.s_var, 1)
        dve.wait_ge(self.s_rstd, tt * self.per + (j + 1))
        return dve.tensor_scalar(out, x, self.mv[:, j, 0:1], self.rstd[:, j:j + 1], ALU.subtract, ALU.mult)


def spread(row):
    return row.rearrange("(o n) -> o n", o=1).to_broadcast([P, row.shape[0]])


def project(nc, k, w, x_dram, xn_dram, q3, q_mix, kv_all, kv_dram, skip_dram):
    WIDE = 6 * D
    with ExitStack() as ctx:
        t = Tools(nc, "proj", ctx)
        wcat = t.sb("wcat", [P, 2, WIDE])
        bcat = t.sb("bcat", [P, WIDE])
        wq = t.sb("wq", [P, 2, D])
        bq = t.sb("bq", [P, 2])
        xb = t.sb("xb", [P, 2, D])
        xnb = t.sb("xnb", [P, 2, D])
        norm = Norm(k, t)
        xt = t.sb("xt", [P, 2, 2, P])
        kvb = t.sb("kvb", [P, 2, 2 * D])
        skb = t.sb("skb", [P, 2, D])
        qf = t.sb("qf", [P, D])
        mk = t.sb("mk", [P, 2, 2, D])
        low = t.sb("low", [P, 2, 2, D])
        up = t.sb("up", [P, 2, 2, D])
        feat = t.sb("feat", [P, 2, D])
        mv1 = t.sb("mv1", [P, 2, D + 1])
        warm = t.sb("warm", [P, 1])
        p_t = t.ps("p_t", [P, 2, 512])
        p_w = t.ps("p_w", [P, 3, 512])
        p_q = t.ps("p_q", [P, 512])
        p_kv = t.ps("p_kv", [P, 2, 512])
        s_w, s_one = t.sem("w"), t.sem("one")
        s_x = [t.sem(f"x{h}") for h in range(2)]
        s_st = [t.sem(f"st{h}") for h in range(2)]
        s_xn, s_tr, s_xt, s_pw, s_dw, s_low, s_up, s_feat, s_kv = (
            t.sem(x) for x in ("xn", "tr", "xt", "pw", "dw", "low", "up", "feat", "kv"))
        s_dve = t.sem("dve")
        s_sent = t.sem("sent")
        with nc.Block() as block:

            @block.sync
            def _(sp):
                sp.dma_start(wcat[:], w["wcat"].rearrange("(k p) n -> p k n", p=P)).then_inc(s_w, 16)
                sp.dma_start(bcat[:], spread(w["bcat"])).then_inc(s_w, 16)
                sp.dma_start(wq[:], w["mix_wq"].rearrange("(k p) n -> p k n", p=P)).then_inc(s_w, 16)
                sp.dma_start(bq[:], w["mix_bq"].rearrange("(k p) -> p k", p=P)).then_inc(s_w, 16)

                def load(i, h):
                    sp.wait_ge(s_xn, i * 2 + h)
                    sp.dma_start(xb[:, h], x_dram[bass.ds((i * 2 + h) * P, P), :]).then_inc(s_x[h], 16)

                per_tile(sp, load)

            @block.gpsimd
            def _(pool):
                def store(i, h):
                    tt = i * 2 + h
                    norm.power(pool, tt)
                    pool.wait_ge(s_xn, tt + 2)
                    pool.sem_inc(s_sent, 1)
                    pool.dma_start(xn_dram[bass.ds(tt * P, P), :], xnb[:, h]).then_inc(s_st[h], 16)
                    pool.wait_ge(s_dw, tt + 2)
                    pool.sem_inc(s_sent, 1)
                    pool.dma_start(kv_dram[bass.ds(tt * P, P), :], kvb[:, h]).then_inc(s_st[h], 16)
                    pool.dma_start(skip_dram[bass.ds(tt * P, P), :], skb[:, h]).then_inc(s_st[h], 16)

                per_tile(pool, store)
                pool.wait_ge(s_st[0], (NB + 1) // 2 * 48)
                pool.wait_ge(s_st[1], NB // 2 * 48)

            @block.vector
            def _(dve):
                for s in (s_xn, s_dw, s_low, s_feat):
                    dve.sem_inc(s, 1)
                dve.memset(mv1[:, :, D:D + 1], 1.0).then_inc(s_one, 1)
                dve.wait_ge(s_w, 64)
                dve.wait_ge(s_one, 1)
                link = Steps(dve, s_dve, 9)

                def tile(i, h):
                    tt = i * 2 + h
                    link.at(tt)
                    dve.wait_ge(s_x[h], i * 16 + 16)
                    dve.wait_ge(s_tr, tt)
                    dve.wait_ge(s_st[h], i * 48)
                    norm(dve, link, xnb[:, h], xb[:, h], tt).then_inc(s_xn, 1)
                    dve.wait_ge(s_pw, tt + 2)
                    link(dve.tensor_tensor(qf[:], p_w[:, 0, 0:D], bcat[:, 0:D], ALU.add))
                    for part in range(3):
                        out = q3[:, bass.ds(tt * (3 * D) + part * D, D)]
                        link(dve.tensor_copy(out, qf[:]))
                        if part < 2:
                            link(dve.tensor_tensor(qf[:], qf[:], out, ALU.subtract))
                    dve.tensor_tensor(kvb[:, h, 0:D], p_w[:, 0, D:2 * D], bcat[:, D:2 * D], ALU.add)
                    dve.tensor_tensor(kvb[:, h, D:2 * D], p_w[:, 1, 0:D], bcat[:, 2 * D:3 * D], ALU.add)
                    dve.tensor_tensor(skb[:, h], p_w[:, 1, D:2 * D], bcat[:, 3 * D:4 * D], ALU.add)
                    dve.wait_ge(s_kv, tt)
                    dve.tensor_tensor(mk[:, h, 0], p_w[:, 2, 0:D], bcat[:, 4 * D:5 * D], ALU.add)
                    dve.tensor_tensor(mv1[:, h, 0:D], p_w[:, 2, D:2 * D], bcat[:, 5 * D:6 * D], ALU.add)
                    for a in range(2):
                        last = dve.tensor_scalar(mk[:, h, 1, a * P:(a + 1) * P], p_q[:, a * P:(a + 1) * P],
                                                 bq[:, a:a + 1], None, ALU.add)
                    last.then_inc(s_dw, 1)
                    dve.wait_ge(s_dw, tt + 2)
                    dve.tensor_scalar(low[:, h], mk[:, h], 0.0, None, ALU.min).then_inc(s_low, 1)
                    dve.wait_ge(s_up, tt + 2)
                    link(dve.scalar_tensor_tensor(feat[:, h], mk[:, h, 0], 0.0, up[:, h, 0], ALU.max, ALU.add))
                    if isinstance(i, int):
                        dve.tensor_scalar(feat[:, h], feat[:, h], k["exists"][:, NB - 1:NB], None, ALU.mult)
                    dve.scalar_tensor_tensor(q_mix[:, bass.ds(tt * D, D)], mk[:, h, 1], 0.0, up[:, h, 1],
                                             ALU.max, ALU.add).then_inc(s_feat, 1)

                per_tile(dve, tile)
                dve.wait_ge(s_kv, NB + 1)
                dve.tensor_copy(kv_all[:], p_kv[:, :, 0:D + 1]).then_inc(s_one, 1)

            @block.scalar
            def _(act):
                act.sem_inc(s_xt, 1)
                act.sem_inc(s_up, 1)
                act.wait_ge(s_w, 64)
                act.activation(warm[:], k["ones"][:, 0:1], ACT.Exp)

                def tile(i, h):
                    tt = i * 2 + h
                    act.wait_ge(s_tr, tt + 2)
                    act.wait_ge(s_pw, tt)
                    act.copy(xt[:, h], p_t[:, h, 0:D].rearrange("p (a b) -> p a b", a=2)).then_inc(s_xt, 1)
                    act.wait_ge(s_low, tt + 2)
                    act.wait_ge(s_feat, tt)
                    act.activation(up[:, h], low[:, h], ACT.Exp).then_inc(s_up, 1)

                per_tile(act, tile)

            @block.tensor
            def _(pe):
                for s in (s_tr, s_pw, s_kv):
                    pe.sem_inc(s, 1)
                pe.wait_ge(s_w, 64)

                def turn(i, h):
                    tt = i * 2 + h
                    pe.wait_ge(s_xn, tt + 2)
                    pe.wait_ge(s_xt, tt)
                    for a in range(2):
                        last = pe.transpose(p_t[:, h, a * P:(a + 1) * P], xnb[:, h, a * P:(a + 1) * P], k["ident"][:])
                    last.then_inc(s_tr, 1)

                def products(i, h):
                    tt = i * 2 + h
                    pe.wait_ge(s_xt, tt + 2)
                    pe.wait_ge(s_dw, tt + 1)
                    for c in range(3):
                        for a in range(2):
                            pe.matmul(p_w[:, c], xt[:, h, a], wcat[:, a, c * 512:(c + 1) * 512],
                                      start=(a == 0), stop=(a == 1))
                    for b in range(2):
                        for a in range(2):
                            last = pe.matmul(p_q[:, b * P:(b + 1) * P], wq[:, a, b * P:(b + 1) * P], xt[:, h, a],
                                             start=(a == 0), stop=(a == 1))
                    last.then_inc(s_pw, 1)

                def sums(i, h, first=False):
                    tt = i * 2 + h
                    pe.wait_ge(s_feat, tt + 2)
                    for a in range(2):
                        last = pe.matmul(p_kv[:, a, 0:D + 1], feat[:, h, a * P:(a + 1) * P], mv1[:, h],
                                         start=first, stop=False, skip_group_check=True)
                    last.then_inc(s_kv, 1)

                turn(0, 0)
                products(0, 0)
                turn(0, 1)
                products(0, 1)
                sums(0, 0, first=True)
                with pe.Fori(1, NB // 2) as i:
                    turn(i, 0)
                    products(i, 0)
                    sums(i - 1, 1)
                    turn(i, 1)
                    products(i, 1)
                    sums(i, 0)
                turn(NB // 2, 0)
                products(NB // 2, 0)
                sums(NB // 2 - 1, 1)
                sums(NB // 2, 0)


def conv_scores(nc, k, table, sorted_rows, kv_dram, we2, q3, alpha, ids, index, ve_dram):
    L = CONV
    G, A, W = L.groups, L.attr, L.width
    R = 8
    with ExitStack() as ctx:
        t = Tools(nc, "scores", ctx)
        we = t.sb("we", [A, D])
        rows = t.sb("rows", [P, R, 2, W], I32)
        hot = t.sb("hot", [P, R, 2, P], BF16)
        hot_t = t.sb("hot_t", [P, R, 2 * P], BF16)
        attr_t = t.sb("attr_t", [A, R, 2 * P])
        kv = t.sb("kv", [P, R, 2, 2 * D])
        prod = t.sb("prod", [P, 2 * D])
        ident_bf = t.sb("ident_bf", [P, P], BF16)
        p_at = t.ps("p_at", [P, 2, 512])
        p_ht = t.ps("p_ht", [P, 2, 1024], BF16)
        p_e = t.ps("p_e", [P, 2, 512])
        p_q = t.ps("p_q", [P, 2, 512])
        s_w, s_id, s_go, s_carry = t.sem("w"), t.sem("id"), t.sem("go"), t.sem("carry")
        s_rows = [t.sem(f"rows{r}") for r in range(R)]
        s_got = [t.sem(f"got{r}") for r in range(R)]
        s_ve = [t.sem(f"ve{r}") for r in range(R)]
        s_hot, s_turn, s_cat, s_e, s_q, s_kv, s_prod, s_alpha = (
            t.sem(x) for x in ("hot", "turn", "cat", "e", "q", "kv", "prod", "alpha"))
        with nc.Block() as block:
            AHEAD = R - 1

            @block.sync
            def _(sp):
                sp.dma_start(we[:], we2).then_inc(s_w, 16)
                view = sorted_rows.rearrange("(g p j) w -> g p (j w)", p=P, j=2)

                def load(g, i, r):
                    sp.wait_ge(s_got[r], i * 32)
                    sp.sem_inc(s_carry, 1)
                    sp.wait_ge(s_turn, g)
                    sp.wait_ge(s_hot, g)
                    sp.sem_inc(s_carry, 1)
                    sp.dma_start(rows[:, r].rearrange("p j w -> p (j w)"), view[bass.ds(g, 1)].squeeze(0)
                                 ).then_inc(s_rows[r], 16)

                def store(g, i, r):
                    sp.wait_ge(s_got[r], i * 32 + 32)
                    sp.sem_inc(s_carry, 1)
                    sp.dma_start(ve_dram[bass.ds(g, 1)].squeeze(0), kv[:, r, :, D:2 * D]).then_inc(s_ve[r], 16)

                for r in range(R):
                    load(r, 0, r)
                with sp.Fori(0, G // R - 1) as i:
                    for r in range(R):
                        store(i * R + r, i, r)
                        load(i * R + (R + r), i + 1, r)
                for r in range(R):
                    store(G - R + r, G // R - 1, r)
                for r in range(R):
                    sp.wait_ge(s_ve[r], G // R * 16)

            @block.vector
            def _(dve):
                dve.sem_inc(s_hot, AHEAD)
                dve.sem_inc(s_prod, AHEAD)
                dve.sem_inc(s_alpha, AHEAD)
                dve.tensor_copy(ident_bf[:], k["ident"][:]).then_inc(s_id, 1)
                if G < L.all_groups:
                    dve.memset(alpha[:, G * 16:], 0.0)
                    dve.memset(ids[:, G * 4:], -1.0)

                def codes(g, i, r):
                    dve.wait_ge(s_rows[r], i * 16 + 16)
                    dve.wait_ge(s_turn, g)
                    dve.tensor_tensor(hot[:, r], k["iota_row"][:].unsqueeze(1).to_broadcast([P, 2, P]),
                                      rows[:, r, :, A + 2:A + 3].to_broadcast([P, 2, P]), ALU.is_equal)
                    dve.tensor_copy(index[:, bass.ds(g * 2, 2)], rows[:, r, :, A])
                    dve.tensor_copy(ids[:, bass.ds(g * 4, 4)].rearrange("p (j w) -> p j w", j=2),
                                    rows[:, r, :, A + 1:A + 3]).then_inc(s_hot, 1)

                def scores(g, i, r):
                    dve.wait_ge(s_got[r], i * 32 + 32)
                    dve.wait_ge(s_q, g + AHEAD + 1)
                    dve.wait_ge(s_alpha, g + AHEAD)
                    dve.tensor_tensor(prod[:].rearrange("p (j f) -> p j f", j=2), kv[:, r, :, 0:D],
                                      p_q[:, r % 2].rearrange("p (j f) -> p j f", j=2), ALU.mult
                                      ).then_inc(s_prod, 1)
                    dve.wait_ge(s_prod, g + AHEAD + 1)
                    dve.tensor_reduce(alpha[:, bass.ds(g * 16, 16)], prod[:].rearrange("p (x f) -> p x f", f=32),
                                      AX, ALU.add).then_inc(s_alpha, 1)

                staged_groups(dve, G, R, (5, codes), (0, scores))

            @block.scalar
            def _(act):
                act.sem_inc(s_cat, AHEAD)
                act.sem_inc(s_kv, AHEAD)
                act.copy(attr_t[:, 0, 0:P], k["iota_row"][0:A]).then_inc(s_id, 1)
                act.wait_ge(s_id, 2)

                def turned(g, i, r):
                    act.wait_ge(s_turn, g + AHEAD + 1)
                    act.wait_ge(s_q, g)
                    act.copy(attr_t[:, r], p_at[0:A, r % 2, 0:2 * P])
                    act.copy(hot_t[:, r], p_ht[:, r % 2, 0:2 * P]).then_inc(s_cat, 1)

                def start_kv(g, i, r):
                    act.wait_ge(s_e, g + AHEAD + 1)
                    act.wait_ge(s_prod, g)
                    act.wait_ge(s_ve[r], i * 16)
                    act.copy(kv[:, r].rearrange("p j (c f) -> p j c f", c=2),
                             p_e[:, r % 2].rearrange("p (j f) -> p j f", j=2).unsqueeze(2)
                             .to_broadcast([P, 2, 2, D])).then_inc(s_kv, 1)

                staged_groups(act, G, R, (4, turned), (3, start_kv))

            @block.gpsimd
            def _(pool):
                with pool.Fori(0, G // R) as i:
                    for r in range(R):
                        pool.wait_ge(s_kv, i * R + (r + AHEAD + 1))
                        pool.sem_inc(s_go, 1)
                        for j in range(2):
                            pool.indirect_dma_start(
                                out=kv[:, r, j], out_offset=None, in_=kv_dram,
                                in_offset=bass.IndirectOffsetOnAxis(ap=rows[:, r, j, A:A + 1], axis=0),
                                compute_op=ALU.add).then_inc(s_got[r], 16)
                for r in range(R):
                    pool.wait_ge(s_got[r], G // R * 32)

            @block.tensor
            def _(pe):
                pe.sem_inc(s_turn, AHEAD)
                pe.sem_inc(s_e, AHEAD)
                pe.sem_inc(s_q, AHEAD)
                pe.wait_ge(s_w, 16)
                pe.wait_ge(s_id, 2)

                def turn(g, i, r):
                    pe.wait_ge(s_hot, g + AHEAD + 1)
                    pe.wait_ge(s_cat, g + (AHEAD - 1))
                    for j in range(2):
                        pe.transpose(p_ht[:, r % 2, j * P:(j + 1) * P], hot[:, r, j], ident_bf[:])
                    for j in range(2):
                        last = pe.transpose(p_at[0:A, r % 2, j * P:(j + 1) * P],
                                            rows[:, r, j, 0:A].bitcast(F32), k["ident"][:])
                    last.then_inc(s_turn, 1)

                def product_e(g, i, r):
                    pe.wait_ge(s_cat, g + AHEAD + 1)
                    pe.wait_ge(s_kv, g + (AHEAD - 1))
                    for j in range(2):
                        last = pe.matmul(p_e[:, r % 2, j * D:(j + 1) * D], attr_t[:, r, j * P:(j + 1) * P],
                                         we[:], start=True, stop=True)
                    last.then_inc(s_e, 1)

                def product_q(g, i, r):
                    block_of = blocks[r]
                    pe.wait_ge(s_prod, g + (AHEAD - 1))
                    for j in range(2):
                        for part in range(3):
                            last = pe.matmul(p_q[:, r % 2, j * D:(j + 1) * D], hot_t[:, r, j * P:(j + 1) * P],
                                             q3[:, bass.ds(block_of * (3 * D) + part * D, D)],
                                             start=(part == 0), stop=(part == 2))
                    last.then_inc(s_q, 1)

                blocks = {}

                def load_blocks(i):
                    blocks.update(enumerate(block_numbers(pe, table, i)))

                staged_groups(pe, G, R, (4, turn), (3, product_e), (0, product_q), head=load_blocks)


def segment_softmax(nc, k, L, alpha, ids, scale):
    H, M, Q = L.heads, L.pieces, L.per_piece
    LEN = 2 * Q * P
    with ExitStack() as ctx:
        t = Tools(nc, f"soft_{L.name}", ctx)
        a = t.sb("a", [P, LEN])
        seg = t.sb("seg", [P, LEN + 1])
        best = t.sb("best", [P, LEN])
        wide = t.sb("wide", [P, 4, P])
        edge = t.sb("edge", [P, 8])
        row = t.sb("row", [1, 8, P])
        p_t = t.ps("p_t", [P, 4, 512])
        p_row = t.ps("p_row", [P, 512])
        p_col = t.ps("p_col", [P, 512])
        s_wide, s_t, s_out = (t.sem(x) for x in ("wide", "t", "out"))
        s_dve, s_ask, s_turned, s_exp = (t.sem(x) for x in ("dve", "ask", "turned", "exp"))
        b_wide, b_t, b_out = (t.sem(x) for x in ("b_wide", "b_t", "b_out"))
        av = alpha[:, 0:M * 2 * Q * H].rearrange("p (m t w) -> p m t w", m=M, w=H)
        idv = ids[:, 0:M * 2 * Q * 2].rearrange("p (m t w) -> p m t w", m=M, w=2)

        def ordered(x, q, j):
            return x.rearrange("p (q e j) -> p q j e", q=Q, j=2)[:, bass.ds(q, 1), j, :].squeeze(1)

        with nc.Block() as block:

            @block.vector
            def _(dve):
                dve.sem_inc(s_wide, 3)
                with dve.Fori(0, Q) as q:
                    for n in range(4):
                        dve.wait_ge(s_t, q * 4 + n)
                        c = bass.ds(q * 2 + n // 2, 1)
                        src = (idv[:, :, c, 0:1].squeeze(2).to_broadcast([P, M, H]) if n % 2 == 0
                               else av[:, :, c, :].squeeze(2))
                        dve.tensor_copy(wide[:, n].rearrange("p (m h) -> p m h", m=M), src).then_inc(s_wide, 1)

            @block.tensor
            def _(pe):
                pe.sem_inc(s_t, 3)
                with pe.Fori(0, Q) as q:
                    for n in range(4):
                        pe.wait_ge(s_wide, q * 4 + (n + 4))
                        pe.wait_ge(s_out, q * 4 + n)
                        pe.transpose(p_t[:, n, 0:P], wide[:, n], k["ident"][:]).then_inc(s_t, 1)

            @block.scalar
            def _(act):
                act.sem_inc(s_out, 3)
                act.copy(row[0:1, 0], k["ones"][0:1]).then_inc(s_exp, 1)
                with act.Fori(0, Q) as q:
                    for n in range(4):
                        act.wait_ge(s_t, q * 4 + (n + 4))
                        act.copy(ordered(seg[:, 0:LEN] if n % 2 == 0 else a[:], q, n // 2), p_t[:, n, 0:P]
                                 ).then_inc(s_out, 1)
                act.wait_ge(s_exp, 1)

        with nc.Block() as block:

            @block.vector
            def _(dve):
                link = Chain(dve, s_dve)
                asked = [0]

                def turned():
                    asked[0] += 1
                    dve.sem_inc(s_ask, 1)
                    dve.wait_ge(s_turned, asked[0])

                link(dve.tensor_copy(edge[:, 0:1], seg[:, 0:1]))
                link(dve.tensor_copy(edge[:, 1:2], seg[:, LEN - 1:LEN]))
                link(dve.tensor_tensor(best[:, 1:LEN], seg[:, 1:LEN], seg[:, 0:LEN - 1], ALU.not_equal))
                turned()
                link(dve.tensor_copy(row[:, 0:2].rearrange("o a p -> o (a p)"), p_row[0:1, 0:2 * P]))
                link(dve.memset(row[:, 2:4], 1.0))
                link(dve.tensor_tensor(row[:, 2, H:P], row[:, 0, H:P], row[:, 1, 0:P - H], ALU.not_equal))
                link(dve.tensor_copy(row[:, 3, 0:P - H], row[:, 2, H:P]))
                link(dve.tensor_scalar(row[:, 2:4], row[:, 2:4], LOW, None, ALU.mult))
                turned()
                link(dve.tensor_copy(seg[:, 0:1], p_col[:, 0:1]))
                link(dve.tensor_copy(seg[:, LEN:LEN + 1], p_col[:, 1:2]))
                link(dve.tensor_scalar(seg[:, 1:LEN], best[:, 1:LEN], LOW, None, ALU.mult))
                link(dve.tensor_reduce(edge[:, 2:3], seg[:, 0:LEN], AX, ALU.min))
                link(dve.tensor_reduce(edge[:, 3:4], seg[:, 1:LEN + 1], AX, ALU.min))
                forth = (seg[:, 0:LEN], a[:])
                back_out = alpha[:, 0:LEN]
                back = (seg[:, 1:LEN + 1][:, ::-1], a[:, ::-1])
                link(dve.tensor_tensor_scan(best[:], *forth, LOW, ALU.add, ALU.max))
                link(dve.tensor_tensor_scan(back_out[:, ::-1], *back, LOW, ALU.add, ALU.max))
                link(dve.tensor_copy(edge[:, 0:1], best[:, LEN - 1:LEN]))
                link(dve.tensor_copy(edge[:, 1:2], back_out[:, 0:1]))
                turned()
                link(dve.tensor_copy(row[:, 0:4].rearrange("o a (h m) -> o a h m", h=H),
                                     p_row[0:1, 0:4 * P].rearrange("o (a m h) -> o a h m", a=4, h=H)))
                by_head = row[:].rearrange("o a (h m) -> o a h m", h=H)
                link(dve.memset(by_head[:, 2, :, 0:1], LOW))
                link(dve.memset(by_head[:, 3, :, M - 1:M], LOW))
                link(dve.tensor_tensor_scan(row[:, 4], row[:, 2], row[:, 0], LOW, ALU.add, ALU.max))
                link(dve.tensor_tensor_scan(row[:, 5, ::-1], row[:, 3, ::-1], row[:, 1, ::-1], LOW, ALU.add, ALU.max))
                link(dve.memset(row[:, 6:8], LOW))
                by_piece = row[:].rearrange("o a (m h) -> o a h m", h=H)
                link(dve.tensor_copy(by_piece[:, 6, :, 1:M], by_head[:, 4, :, 0:M - 1]))
                link(dve.tensor_copy(by_piece[:, 7, :, 0:M - 1], by_head[:, 5, :, 1:M]))
                turned()
                link(dve.tensor_copy(edge[:, 4:6], p_col[:, 0:2]))
                link(dve.tensor_tensor_scan(best[:], *forth, edge[:, 4:5], ALU.add, ALU.max))
                link(dve.tensor_tensor_scan(back_out[:, ::-1], *back, edge[:, 5:6], ALU.add, ALU.max))
                link(dve.tensor_tensor(best[:], best[:], back_out, ALU.max))
                dve.tensor_tensor(a[:], a[:], best[:], ALU.subtract).then_inc(s_ask, 1)

            @block.tensor
            def _(pe):
                one = k["ident"][0:1, 0:1]
                for n, (cols, rows) in enumerate((((0, 1), ()), ((), (2, 3)), ((0, 1, 2, 3), ()), ((), (6, 7)))):
                    pe.wait_ge(s_ask, n + 1)
                    for c in cols:
                        last = pe.transpose(p_row[0:1, c * P:(c + 1) * P], edge[:, c:c + 1], k["ident"][:])
                    for c, r in enumerate(rows):
                        last = pe.transpose(p_col[:, c:c + 1], row[0:1, r], one)
                    last.then_inc(s_turned, 1)

            @block.scalar
            def _(act):
                act.wait_ge(s_ask, 5)
                act.activation(a[:], a[:], ACT.Exp, scale=scale).then_inc(s_exp, 1)
                act.wait_ge(s_exp, 2)

        with nc.Block() as block:

            @block.tensor
            def _(pe):
                pe.sem_inc(b_t, 1)
                with pe.Fori(0, Q) as q:
                    for n in range(2):
                        pe.wait_ge(b_wide, q * 2 + (n + 1))
                        pe.wait_ge(b_out, q * 2 + n)
                        pe.transpose(p_t[:, n, 0:P], wide[:, n], k["ident"][:]).then_inc(b_t, 1)

            @block.vector
            def _(dve):
                with dve.Fori(0, Q) as q:
                    for n in range(2):
                        dve.wait_ge(b_t, q * 2 + n)
                        dve.tensor_copy(wide[:, n], ordered(a[:], q, n)).then_inc(b_wide, 1)

            @block.scalar
            def _(act):
                act.sem_inc(b_out, 1)
                act.copy(edge[:, 0:1], k["ones"][:, 0:1]).then_inc(s_exp, 1)
                with act.Fori(0, Q) as q:
                    for n in range(2):
                        act.wait_ge(b_t, q * 2 + (n + 2))
                        act.copy(av[:, :, bass.ds(q * 2 + n, 1), :].squeeze(2),
                                 p_t[:, n, 0:P].rearrange("p (m h) -> p m h", m=M)).then_inc(b_out, 1)
                act.wait_ge(s_exp, 3)


def block_sums(nc, k, L, table, ids, weights, acc, values_dram=None, values=None):
    G, H = L.groups, L.heads
    F = D if L is CONV else 16
    R = 8
    with ExitStack() as ctx:
        t = Tools(nc, f"sums_{L.name}", ctx)
        hot = t.sb("hot", [P, R, 2, P])
        msg = t.sb("msg", [P, R, 2, F + H])
        zero = t.sb("zero", [P, P], BF16)
        vb = t.sb("vb", [P, R, 2, F]) if values_dram is not None else None
        p_acc = t.ps("p_acc", [P, 512])
        s_v = [t.sem(f"v{r}") for r in range(R)]
        s_zero, s_full, s_copied, s_carry = t.sem("zero"), t.sem("full"), t.sem("copied"), t.sem("carry")
        s_w, s_msg, s_sum = (t.sem(x) for x in ("w", "msg", "sum"))
        with nc.Block() as block:

            if values_dram is not None:
                @block.sync
                def _(sp):
                    with sp.Fori(0, G // R) as i:
                        for r in range(R):
                            sp.wait_ge(s_msg, i * R + r)
                            sp.sem_inc(s_carry, 1)
                            sp.dma_start(vb[:, r], values_dram[bass.ds(i * R + r, 1)].squeeze(0)
                                         ).then_inc(s_v[r], 16)

            @block.gpsimd
            def _(pool):
                pool.memset(zero[:], 0.0).then_inc(s_zero, 1)
                with pool.Fori(0, G // R) as i:
                    for r in range(R):
                        g = i * R + r
                        pool.wait_ge(s_sum, g)
                        pool.tensor_copy(msg[:, r, :, F:F + H],
                                         weights[:, bass.ds(g * 2 * H, 2 * H)].rearrange("p (j h) -> p j h", j=2)
                                         ).then_inc(s_w, 1)

            @block.vector
            def _(dve):
                dve.sem_inc(s_msg, 7)
                with dve.Fori(0, G // R) as i:
                    for r in range(R):
                        g = i * R + r
                        if vb is not None:
                            dve.wait_ge(s_v[r], i * 16 + 16)
                            src = vb[:, r]
                        else:
                            src = values[:, bass.ds(g * 2 * F, 2 * F)].rearrange("p (j f) -> p j f", j=2)
                        dve.wait_ge(s_sum, g)
                        w = weights[:, bass.ds(g * 2 * H, 2 * H)].rearrange("p (j h) -> p j h", j=2)
                        for j in range(2):
                            dve.tensor_scalar(hot[:, r, j], k["iota_row"][:], ids[:, bass.ds(g * 4 + (2 * j + 1), 1)],
                                              None, ALU.is_equal)
                        last = dve.tensor_tensor(
                            msg[:, r, :, 0:F].rearrange("p j (h f) -> p j h f", h=H),
                            src.rearrange("p j (h f) -> p j h f", h=H),
                            w.unsqueeze(3).to_broadcast([P, 2, H, F // H]), ALU.mult)
                        last.then_inc(s_msg, 1)

            @block.tensor
            def _(pe):
                pe.sem_inc(s_sum, 7)
                pe.wait_ge(s_zero, 1)

                def clear():
                    pe.matmul(p_acc[:, 0:F + H], zero[:], acc_zero, start=True, stop=False, skip_group_check=True)

                acc_zero = zero[:, 0:1].to_broadcast([P, F + H])
                clear()
                with pe.Fori(0, G // R) as i:
                    block_of, is_last = block_numbers(pe, table, i), last_groups(pe, table, i)
                    for r in range(R):
                        g = i * R + r
                        pe.wait_ge(s_w, g + 1)
                        pe.wait_ge(s_msg, g + 8)
                        for j in range(2):
                            last = pe.matmul(p_acc[:, 0:F + H], hot[:, r, j], msg[:, r, j], start=False,
                                             stop=False, skip_group_check=True)
                        last.then_inc(s_sum, 1)
                        with pe.If(is_last[r] == 1):
                            pe.matmul(p_acc[:, 0:F + H], zero[:], acc_zero, start=False, stop=False,
                                      skip_group_check=True).then_inc(s_full, 1)
                            pe.wait_ge(s_copied, block_of[r] + 1)
                            clear()

            @block.scalar
            def _(act):
                with act.Fori(0, NB) as b:
                    act.wait_ge(s_full, b + 1)
                    act.copy(acc[:, bass.ds(b * (F + H), F + H)], p_acc[:, 0:F + H]).then_inc(s_copied, 1)
                act.wait_ge(s_copied, NB)


def one_ahead(engine, first, second):
    first(0, 0)
    with engine.Fori(0, NB // 2) as i:
        first(i, 1)
        second(i, 0)
        first(i + 1, 0)
        second(i, 1)
    second(NB // 2, 0)


def staged_groups(engine, G, R, *stages, head=None):
    for lead, body in stages:
        for g in range(lead):
            body(g, 0, g)
    with engine.Fori(0, G // R - 1) as i:
        if head:
            head(i)
        for r in range(R):
            for lead, body in stages:
                later = (r + lead) // R
                body(i * R + (r + lead), i + later, (r + lead) % R)
    if head:
        head(G // R - 1)
    for g in range(G - R, G):
        for lead, body in stages:
            if g + lead < G:
                body(g + lead, (g + lead) // R, (g + lead) % R)


def block_numbers(engine, table, i):
    held = lambda value, most: engine.snap(engine.to_reg(value), min_val=0, max_val=most)
    word = engine.value_load(table[0:1, bass.ds(i + 1024, 1)], min_val=0, max_val=NB * 256 - 1)
    blocks = [held(word >> 8, NB - 1)]
    for r in range(7):
        blocks.append(held(blocks[r] + ((word >> r) & 1), NB - 1))
    return blocks


def last_groups(engine, table, i):
    word = engine.value_load(table[0:1, bass.ds(i + 1088, 1)], min_val=0, max_val=255)
    return [(word >> r) & 1 for r in range(8)]


def load_all(sp, sem, pairs):
    for out, src in pairs:
        sp.dma_start(out, src).then_inc(sem, 16)
    return 16 * len(pairs)


def linear_attention(nc, k, w, x_dram, q_mix, kv_all, out_dram):
    with ExitStack() as ctx:
        t = Tools(nc, "mixer", ctx)
        wo = t.sb("wo", [P, 2, D])
        bo = t.sb("bo", [P, D])
        kv_m = t.sb("kv_m", [P, 2, P])
        ks_m = t.sb("ks_m", [P, 2, P])
        xb = t.sb("xb", [P, 2, D])
        den = t.sb("den", [P, D])
        o_t = t.sb("o_t", [P, 2, D])
        yb = t.sb("yb", [P, 2, D])
        p_o = t.ps("p_o", [P, 2, 512])
        p_y = t.ps("p_y", [P, 2, 512])
        s_w, s_set, s_ratio, s_add = (t.sem(x) for x in ("w", "set", "ratio", "add"))
        s_x = [t.sem(f"x{h}") for h in range(2)]
        s_st = [t.sem(f"st{h}") for h in range(2)]
        s_o, s_ot, s_py, s_y = (t.sem(x) for x in ("o", "ot", "py", "y"))
        s_sent = t.sem("sent")
        with nc.Block() as block:

            @block.sync
            def _(sp):
                load_all(sp, s_w, [(wo[:], w["mix_wo"].rearrange("(k p) n -> p k n", p=P)),
                                   (bo[:], spread(w["mix_bo"]))])

                def load(i, h):
                    sp.wait_ge(s_y, i * 2 + h)
                    sp.dma_start(xb[:, h], x_dram[bass.ds((i * 2 + h) * P, P), :]).then_inc(s_x[h], 16)

                per_tile(sp, load)

            @block.gpsimd
            def _(pool):
                def store(i, h):
                    pool.wait_ge(s_y, i * 2 + (h + 2))
                    pool.sem_inc(s_sent, 1)
                    pool.dma_start(out_dram[bass.ds((i * 2 + h) * P, P), :], yb[:, h]).then_inc(s_st[h], 16)

                per_tile(pool, store)
                pool.wait_ge(s_st[0], (NB + 1) // 2 * 16)
                pool.wait_ge(s_st[1], NB // 2 * 16)

            @block.vector
            def _(dve):
                dve.sem_inc(s_ot, 1)
                dve.sem_inc(s_y, 1)
                for a in range(2):
                    dve.tensor_tensor(kv_m[:, a], kv_all[:, a, a * P:(a + 1) * P], k["same_head"][:], ALU.mult)
                    last = dve.tensor_scalar(ks_m[:, a], k["same_head"][:], kv_all[:, a, D:D + 1], None, ALU.mult)
                last.then_inc(s_set, 1)
                dve.wait_ge(s_w, 32)
                link = Steps(dve, s_ratio, 2)
                add = Steps(dve, s_add, 1)

                def ratio(i, h):
                    tt = i * 2 + h
                    link.at(tt)
                    dve.wait_ge(s_o, tt + 2)
                    dve.wait_ge(s_ot, tt + 1)
                    link(dve.tensor_scalar(den[:], p_o[:, h, D:2 * D], 1e-6, None, ALU.add))
                    link(dve.reciprocal(den[:], den[:]))
                    dve.wait_ge(s_py, tt)
                    dve.tensor_tensor(o_t[:, h], p_o[:, h, 0:D], den[:], ALU.mult).then_inc(s_ot, 1)

                def total(i, h):
                    tt = i * 2 + h
                    add.at(tt)
                    dve.wait_ge(s_py, tt + 2)
                    dve.wait_ge(s_st[h], i * 16)
                    add(dve.tensor_tensor(yb[:, h], p_y[:, h, 0:D], bo[:], ALU.add))
                    dve.wait_ge(s_x[h], i * 16 + 16)
                    dve.tensor_tensor(yb[:, h], yb[:, h], xb[:, h], ALU.add).then_inc(s_y, 1)

                one_ahead(dve, ratio, total)

            @block.tensor
            def _(pe):
                pe.sem_inc(s_o, 1)
                pe.sem_inc(s_py, 1)
                pe.wait_ge(s_set, 1)
                pe.wait_ge(s_w, 32)

                def mix(i, h):
                    tt = i * 2 + h
                    pe.wait_ge(s_ot, tt)
                    for a in range(2):
                        q = q_mix[:, bass.ds(tt * D + a * P, P)]
                        pe.matmul(p_o[:, h, a * P:(a + 1) * P], kv_m[:, a], q, start=True, stop=True)
                        last = pe.matmul(p_o[:, h, D + a * P:D + (a + 1) * P], ks_m[:, a], q, start=True, stop=True)
                    last.then_inc(s_o, 1)

                def out(i, h):
                    tt = i * 2 + h
                    pe.wait_ge(s_ot, tt + 2)
                    pe.wait_ge(s_y, tt)
                    for a in range(2):
                        last = pe.matmul(p_y[:, h, 0:D], o_t[:, h, a * P:(a + 1) * P], wo[:, a],
                                         start=(a == 0), stop=(a == 1))
                    last.then_inc(s_py, 1)

                one_ahead(pe, mix, out)


def conv_tail(nc, k, w, acc, xn_dram, skip_dram, out_dram):
    H = CONV.heads
    F = D + H
    with ExitStack() as ctx:
        t = Tools(nc, "tail", ctx)
        wb = t.sb("wb", [P, 3 * D])
        g1 = t.sb("g1", [P, D])
        b1 = t.sb("b1", [P, D])
        euler = t.sb("euler", [P, 1])
        cat = t.sb("cat", [P, 2, 3, D])
        xb = t.sb("xb", [P, 2, D])
        prod = t.sb("prod", [P, 3 * D])
        den = t.sb("den", [P, H])
        z = t.sb("z", [P, 2])
        ez = t.sb("ez", [P, 1])
        res = t.sb("res", [P, D])
        yb = t.sb("yb", [P, 2, D])
        norm = Norm(k, t)
        s_w, s_dve, s_z, s_ez, s_e, s_carry, s_carry2 = (
            t.sem(x) for x in ("w", "dve", "z", "ez", "e", "carry", "carry2"))
        s_in = [t.sem(f"in{h}") for h in range(2)]
        s_st = [t.sem(f"st{h}") for h in range(2)]
        s_y = t.sem("y")
        s_g = t.sem("g")
        s_sent = t.sem("sent")
        with nc.Block() as block:

            @block.sync
            def _(sp):
                load_all(sp, s_w, [(wb[:], spread(w["wbeta"])), (g1[:], spread(w["ln1_g"])),
                                   (b1[:], spread(w["ln1_b"]))])

                def load(i, h):
                    tt = i * 2 + h
                    sp.wait_ge(s_y, tt)
                    sp.sem_inc(s_carry, 1)
                    sp.dma_start(cat[:, h, 1], skip_dram[bass.ds(tt * P, P), :]).then_inc(s_in[h], 16)
                    sp.dma_start(xb[:, h], xn_dram[bass.ds(tt * P, P), :]).then_inc(s_in[h], 16)

                per_tile(sp, load)

            @block.gpsimd
            def _(pool):
                pool.memset(euler[:], 2.718281828459045).then_inc(s_e, 1)
                pool.wait_ge(s_e, 1)

                def tile(i, h):
                    tt = i * 2 + h
                    pool.wait_ge(s_z, tt + 1)
                    pool.sem_inc(s_carry2, 1)
                    pool.tensor_tensor(ez[:], euler[:], z[:, 0:1], ALU.pow).then_inc(s_ez, 1)
                    norm.power(pool, tt)
                    pool.wait_ge(s_y, tt + 2)
                    pool.sem_inc(s_sent, 1)
                    pool.dma_start(out_dram[bass.ds(tt * P, P), :], yb[:, h]).then_inc(s_st[h], 16)

                per_tile(pool, tile)
                pool.wait_ge(s_st[0], (NB + 1) // 2 * 16)
                pool.wait_ge(s_st[1], NB // 2 * 16)

            @block.vector
            def _(dve):
                dve.sem_inc(s_y, 1)
                dve.wait_ge(s_w, 48)
                link = Steps(dve, s_dve, 13)

                def tile(i, h):
                    tt = i * 2 + h
                    link.at(tt)
                    o, skip, diff = (cat[:, h, c] for c in range(3))
                    link(dve.tensor_scalar(den[:], acc[:, bass.ds(tt * F + D, H)], 1e-16, None, ALU.add))
                    link(dve.reciprocal(den[:], den[:]))
                    link(dve.tensor_tensor(o.rearrange("p (h f) -> p h f", h=H),
                                           acc[:, bass.ds(tt * F, D)].rearrange("p (h f) -> p h f", h=H),
                                           den[:].unsqueeze(2).to_broadcast([P, H, D // H]), ALU.mult))
                    dve.wait_ge(s_in[h], i * 32 + 32)
                    link(dve.tensor_tensor(diff, o, skip, ALU.subtract))
                    link(dve.tensor_tensor(prod[:], cat[:, h].rearrange("p c f -> p (c f)"), wb[:], ALU.mult))
                    link(dve.tensor_reduce(z[:, 1:2], prod[:], AX, ALU.add))
                    dve.tensor_scalar(z[:, 0:1], z[:, 1:2], -1.0, None, ALU.mult).then_inc(s_z, 1)
                    link(dve.tensor_tensor(res[:], o, xb[:, h], ALU.add))
                    dve.wait_ge(s_ez, tt + 1)
                    link(dve.tensor_scalar(z[:, 1:2], ez[:], 1.0, None, ALU.add))
                    link(dve.reciprocal(z[:, 1:2], z[:, 1:2]))
                    link(dve.tensor_scalar(diff, diff, z[:, 1:2], None, ALU.mult))
                    link(dve.tensor_tensor(res[:], res[:], diff, ALU.subtract))
                    dve.wait_ge(s_st[h], i * 16)
                    norm(dve, link, yb[:, h], res[:], tt).then_inc(s_g, 1)
                    dve.wait_ge(s_g, tt * 2 + 1)
                    dve.tensor_tensor(yb[:, h], yb[:, h], g1[:], ALU.mult).then_inc(s_g, 1)
                    dve.wait_ge(s_g, tt * 2 + 2)
                    dve.tensor_tensor(yb[:, h], yb[:, h], b1[:], ALU.add).then_inc(s_y, 1)

                per_tile(dve, tile)


def experts(nc, k, name, units, w, x_dram, base_dram, out_dram, gates=None):
    HID = 512
    with ExitStack() as ctx:
        t = Tools(nc, name, ctx)
        w1 = t.sb("w1", [P, units, 2, HID])
        w2 = t.sb("w2", [P, units, 4, D])
        b1 = t.sb("b1", [P, units * 4])
        b2 = t.sb("b2", [P, D * (units if gates is not None else 1)])
        xb = t.sb("xb", [P, 2, D])
        yb = t.sb("yb", [P, 2, D])
        part = t.sb("part", [P, D])
        warm = t.sb("warm", [P, 1])
        xt = t.sb("xt", [P, 2, D])
        ht = t.sb("ht", [P, 2, HID])
        p_t = t.ps("p_t", [P, 2, 512])
        p_h = t.ps("p_h", [P, 2, 512])
        p_y = t.ps("p_y", [P, 2, 512])
        s_w, s_carry, s_dve, s_done = (t.sem(x) for x in ("w", "carry", "dve", "done"))
        s_x = [t.sem(f"x{h}") for h in range(2)]
        s_base = [t.sem(f"base{h}") for h in range(2)]
        s_st = [t.sem(f"st{h}") for h in range(2)]
        s_turn, s_xt, s_h, s_gelu, s_y, s_read = (
            t.sem(x) for x in ("turn", "xt", "h", "gelu", "y", "read"))
        NW = 16 * (2 * units + 2)

        def with_next(engine, tile):
            with engine.Fori(0, NB // 2) as i:
                tile(i, 0, (i, 1))
                tile(i, 1, (i + 1, 0))
            tile(NB // 2, 0, None)

        s_sent = t.sem("sent")
        with nc.Block() as block:

            @block.sync
            def _(sp):
                for u in range(units):
                    load_all(sp, s_w, [(w1[:, u], w["w1"][u].rearrange("(a p) n -> p a n", p=P)),
                                       (w2[:, u], w["w2"][u].rearrange("(c p) n -> p c n", p=P))])
                load_all(sp, s_w, [(b1[:], w["b1"].rearrange("(u p) -> p u", p=P)), (b2[:], spread(w["b2"]))])

                def load(i, h):
                    tt = i * 2 + h
                    sp.wait_ge(s_turn, tt)
                    sp.sem_inc(s_carry, 1)
                    sp.dma_start(xb[:, h], x_dram[bass.ds(tt * P, P), :]).then_inc(s_x[h], 16)
                    sp.wait_ge(s_st[h], i * 16)
                    sp.sem_inc(s_carry, 1)
                    sp.dma_start(yb[:, h], base_dram[bass.ds(tt * P, P), :]).then_inc(s_base[h], 16)

                per_tile(sp, load)

            @block.gpsimd
            def _(pool):
                def store(i, h):
                    pool.wait_ge(s_done, i * 2 + (h + 1))
                    pool.sem_inc(s_sent, 1)
                    pool.dma_start(out_dram[bass.ds((i * 2 + h) * P, P), :], yb[:, h]).then_inc(s_st[h], 16)

                per_tile(pool, store)
                pool.wait_ge(s_st[0], (NB + 1) // 2 * 16)
                pool.wait_ge(s_st[1], NB // 2 * 16)

            @block.vector
            def _(dve):
                dve.sem_inc(s_read, 1)
                dve.wait_ge(s_w, NW)
                shift = Steps(dve, s_dve, units if gates is not None else 1)

                def tile(i, h):
                    tt = i * 2 + h
                    shift.at(tt)
                    dve.wait_ge(s_base[h], i * 16 + 16)
                    for u in range(units):
                        v = tt * units + u
                        y = p_y[:, u % 2, 0:D]
                        dve.wait_ge(s_y, v + 2)
                        if gates is not None:
                            shift(dve.tensor_tensor(part[:], y, b2[:, u * D:(u + 1) * D], ALU.add))
                            last = dve.scalar_tensor_tensor(yb[:, h], part[:], gates[:, bass.ds(v, 1)],
                                                            yb[:, h], ALU.mult, ALU.add)
                        else:
                            if u == 0:
                                shift(dve.tensor_tensor(yb[:, h], yb[:, h], b2[:], ALU.add))
                            last = dve.tensor_tensor(yb[:, h], yb[:, h], y, ALU.add)
                        last.then_inc(s_read, 1)
                        dve.wait_ge(s_read, v + 2)
                    dve.sem_inc(s_done, 1)

                per_tile(dve, tile)

            @block.scalar
            def _(act):
                act.sem_inc(s_xt, 1)
                act.sem_inc(s_gelu, 1)
                act.wait_ge(s_w, NW)
                act.activation(warm[:], k["ones"][:, 0:1], ACT.Gelu)

                def copy(i, h):
                    tt = i * 2 + h
                    act.wait_ge(s_turn, tt + 2)
                    act.copy(xt[:, h], p_t[:, h, 0:D]).then_inc(s_xt, 1)

                def tile(i, h, nxt):
                    tt = i * 2 + h
                    for u in range(units):
                        v = tt * units + u
                        act.wait_ge(s_h, v + 2)
                        act.wait_ge(s_y, v)
                        for c in range(4):
                            last = act.activation(ht[:, u % 2, c * P:(c + 1) * P], p_h[:, u % 2, c * P:(c + 1) * P],
                                                  ACT.Gelu, bias=b1[:, u * 4 + c:u * 4 + c + 1])
                        last.then_inc(s_gelu, 1)
                        if u == 0 and nxt is not None:
                            copy(*nxt)

                copy(0, 0)
                with_next(act, tile)

            @block.tensor
            def _(pe):
                for s in (s_turn, s_h, s_y):
                    pe.sem_inc(s, 1)
                pe.wait_ge(s_w, NW)

                def turn(i, h):
                    tt = i * 2 + h
                    pe.wait_ge(s_x[h], i * 16 + 16)
                    pe.wait_ge(s_xt, tt)
                    for a in range(2):
                        last = pe.transpose(p_t[:, h, a * P:(a + 1) * P], xb[:, h, a * P:(a + 1) * P], k["ident"][:])
                    last.then_inc(s_turn, 1)

                def hidden(i, h, u):
                    tt = i * 2 + h
                    v = tt * units + u
                    if u == 0:
                        pe.wait_ge(s_xt, tt + 2)
                    pe.wait_ge(s_gelu, v)
                    for c in range(4):
                        for a in range(2):
                            last = pe.matmul(p_h[:, u % 2, c * P:(c + 1) * P], w1[:, u, a, c * P:(c + 1) * P],
                                             xt[:, h, a * P:(a + 1) * P], start=(a == 0), stop=(a == 1))
                    last.then_inc(s_h, 1)

                def outer(i, h, u):
                    v = (i * 2 + h) * units + u
                    pe.wait_ge(s_gelu, v + 2)
                    pe.wait_ge(s_read, v)
                    for c in range(4):
                        last = pe.matmul(p_y[:, u % 2, 0:D], ht[:, u % 2, c * P:(c + 1) * P], w2[:, u, c],
                                         start=(c == 0), stop=(c == 3))
                    last.then_inc(s_y, 1)

                def tile(i, h, nxt):
                    if nxt is not None:
                        turn(*nxt)
                    for u in range(units):
                        if u + 1 < units:
                            hidden(i, h, u + 1)
                        elif nxt is not None:
                            hidden(*nxt, 0)
                        outer(i, h, u)

                turn(0, 0)
                hidden(0, 0, 0)
                with_next(pe, tile)


class Product:

    def __init__(self, k, t):
        self.ident = k["ident"]
        self.turned = t.sb("turned", [P, 2, D])
        self.p_t = t.ps("p_t", [P, 2, 512])
        self.p_out = t.ps("p_out", [P, 2, 512])
        self.s_made, self.s_turned, self.s_copied, self.s_product, self.s_used = (
            t.sem(x) for x in ("made", "turned", "copied", "product", "used"))

    def turn(self, pe, tt, h, rows):
        pe.wait_ge(self.s_made, tt + 2)
        pe.wait_ge(self.s_copied, tt)
        for a in range(2):
            last = pe.transpose(self.p_t[:, h, a * P:(a + 1) * P], rows[:, a * P:(a + 1) * P], self.ident[:])
        last.then_inc(self.s_turned, 1)

    def copy(self, act, tt, h):
        act.wait_ge(self.s_turned, tt + 2)
        act.wait_ge(self.s_product, tt)
        act.copy(self.turned[:, h], self.p_t[:, h, 0:D]).then_inc(self.s_copied, 1)

    def multiply(self, pe, tt, h, weights):
        pe.wait_ge(self.s_copied, tt + 2)
        pe.wait_ge(self.s_used, tt)
        for first, halves in weights:
            for n, (a, wa) in enumerate(halves):
                last = pe.matmul(self.p_out[:, h, first:first + wa.shape[1]], self.turned[:, h, a * P:(a + 1) * P],
                                 wa, start=(n == 0), stop=(n == len(halves) - 1))
        last.then_inc(self.s_product, 1)


def gat_in(nc, k, w, z_dram, xm_dram, x1_dram, xl_dram, h_dram, ad3):
    with ExitStack() as ctx:
        t = Tools(nc, "gat_in", ctx)
        wg = t.sb("wg", [P, 2, 16])
        att = t.sb("att", [P, 2, 16])
        g2 = t.sb("g2", [P, D])
        b2 = t.sb("b2", [P, D])
        zb = t.sb("zb", [P, 2, D])
        xm = t.sb("xm", [P, 2, D])
        res = t.sb("res", [P, D])
        x1 = t.sb("x1", [P, 2, D])
        xl = t.sb("xl", [P, 2, D])
        hb = t.sb("hb", [P, 2, 20])
        prod = t.sb("prod", [P, 2, 16])
        score = t.sb("score", [P, 8])
        norm = Norm(k, t, 2)
        mul = Product(k, t)
        s_w, s_make, s_use, s_x1, s_carry = (t.sem(x) for x in ("w", "make", "use", "x1", "carry"))
        s_in = [t.sem(f"in{h}") for h in range(2)]
        s_st = [t.sem(f"st{h}") for h in range(2)]
        s_sth = [t.sem(f"sth{h}") for h in range(2)]
        s_sent = t.sem("sent")
        with nc.Block() as block:

            @block.sync
            def _(sp):
                load_all(sp, s_w, [(wg[:], w["w_gat"].rearrange("(a p) n -> p a n", p=P)),
                                   (att[:].rearrange("p a b -> p (a b)"), spread(w["att"])),
                                   (g2[:], spread(w["ln2_g"])), (b2[:], spread(w["ln2_b"]))])

                def load(i, h):
                    tt = i * 2 + h
                    sp.wait_ge(mul.s_made, tt)
                    sp.sem_inc(s_carry, 1)
                    sp.dma_start(zb[:, h], z_dram[bass.ds(tt * P, P), :]).then_inc(s_in[h], 16)
                    sp.dma_start(xm[:, h], xm_dram[bass.ds(tt * P, P), :]).then_inc(s_in[h], 16)

                per_tile(sp, load)

            @block.gpsimd
            def _(pool):
                def rows(i, h):
                    tt = i * 2 + h
                    norm.power(pool, tt, 0)
                    norm.power(pool, tt, 1)
                    pool.wait_ge(mul.s_made, tt + 2)
                    pool.sem_inc(s_sent, 1)
                    pool.dma_start(x1_dram[bass.ds(tt * P, P), :], x1[:, h]).then_inc(s_st[h], 16)
                    pool.dma_start(xl_dram[bass.ds(tt * P, P), :], xl[:, h]).then_inc(s_st[h], 16)

                def heads(i, h):
                    tt = i * 2 + h
                    pool.wait_ge(mul.s_used, tt + 2)
                    pool.sem_inc(s_sent, 1)
                    pool.dma_start(h_dram[bass.ds(tt * P, P), :], hb[:, h]).then_inc(s_sth[h], 16)

                one_ahead(pool, rows, heads)
                for h, n in ((0, (NB + 1) // 2), (1, NB // 2)):
                    pool.wait_ge(s_st[h], n * 32)
                    pool.wait_ge(s_sth[h], n * 16)

            @block.vector
            def _(dve):
                dve.sem_inc(mul.s_made, 1)
                dve.sem_inc(mul.s_used, 1)
                dve.wait_ge(s_w, 64)
                make, use = Steps(dve, s_make, 8), Steps(dve, s_use, 8)

                def rows(i, h):
                    tt = i * 2 + h
                    make.at(tt)
                    dve.wait_ge(s_in[h], i * 32 + 32)
                    dve.wait_ge(s_st[h], i * 32)
                    dve.wait_ge(mul.s_turned, tt)
                    make(norm(dve, make, res[:], zb[:, h], tt, 0))
                    make(dve.tensor_tensor(res[:], res[:], g2[:], ALU.mult))
                    make(dve.tensor_tensor(res[:], res[:], b2[:], ALU.add))
                    make(dve.tensor_tensor(x1[:, h], res[:], xm[:, h], ALU.add))
                    norm(dve, make, xl[:, h], x1[:, h], tt, 1).then_inc(mul.s_made, 1)

                def heads(i, h):
                    tt = i * 2 + h
                    use.at(tt)
                    dve.wait_ge(mul.s_product, tt + 2)
                    dve.wait_ge(s_sth[h], i * 16)
                    use(dve.tensor_copy(hb[:, h, 0:16], mul.p_out[:, h, 0:16]))
                    use(dve.tensor_tensor(prod[:], hb[:, h, 0:16].unsqueeze(1).to_broadcast([P, 2, 16]),
                                          att[:], ALU.mult))
                    use(dve.tensor_reduce(score[:], prod[:].rearrange("p a (h e) -> p (a h) e", e=4), AX, ALU.add))
                    for part in range(3):
                        out = ad3[:, bass.ds(tt * 12 + part * 4, 4)]
                        use(dve.tensor_copy(out, score[:, 4:8]))
                        if part < 2:
                            use(dve.tensor_tensor(score[:, 4:8], score[:, 4:8], out, ALU.subtract))
                    dve.tensor_copy(hb[:, h, 16:20], score[:, 0:4]).then_inc(mul.s_used, 1)

                one_ahead(dve, rows, heads)

            @block.scalar
            def _(act):
                act.sem_inc(mul.s_copied, 1)
                per_tile(act, lambda i, h: mul.copy(act, i * 2 + h, h))

            @block.tensor
            def _(pe):
                pe.sem_inc(mul.s_turned, 1)
                pe.sem_inc(mul.s_product, 1)
                pe.wait_ge(s_w, 64)
                one_ahead(pe, lambda i, h: mul.turn(pe, i * 2 + h, h, xl[:, h]),
                          lambda i, h: mul.multiply(pe, i * 2 + h, h, [(0, [(a, wg[:, a]) for a in range(2)])]))


def load_meta(nc, L, sorted_rows, ids, index):
    G, GA = L.groups, L.all_groups
    with ExitStack() as ctx:
        t = Tools(nc, f"meta_{L.name}", ctx)
        meta = t.sb("meta", [P, G * 2, 4], I32)
        s_in, s_out = t.sem("in"), t.sem("out")
        CUT = 8
        with nc.Block() as block:

            @block.sync
            def _(sp):
                view = sorted_rows.rearrange("(g p j) w -> p g (j w)", p=P, j=2)
                for c in range(CUT):
                    g0, g1 = G * c // CUT, G * (c + 1) // CUT
                    sp.dma_start(meta[:, 2 * g0:2 * g1].rearrange("p (g j) w -> p g (j w)", j=2), view[:, g0:g1]
                                 ).then_inc(s_in, 16)

            @block.vector
            def _(dve):
                if G < GA and ids.shape[1] > G * 4:
                    dve.memset(ids[:, G * 4:], -1.0)
                dve.wait_ge(s_in, 16 * CUT)
                dve.tensor_copy(ids[:, 0:G * 4].rearrange("p (c w) -> p c w", w=2), meta[:, :, 1:3])
                dve.tensor_copy(index[:], meta[:, :, 0]).then_inc(s_out, 1)
                dve.wait_ge(s_out, 1)


def gat_scores(nc, k, table, h_dram, ad3, alpha, ids, index, values):
    L = GAT
    G, H = L.groups, L.heads
    R = 8
    AHEAD = R - 1
    with ExitStack() as ctx:
        t = Tools(nc, "gscore", ctx)
        hot = t.sb("hot", [P, R, 2, P], BF16)
        hot_t = t.sb("hot_t", [P, R, 2 * P], BF16)
        idx = t.sb("idx", [P, R, 2], I32)
        got = t.sb("got", [P, R, 2, 20])
        total = t.sb("total", [P, 2, 2, H])
        ident_bf = t.sb("ident_bf", [P, P], BF16)
        p_ht = t.ps("p_ht", [P, 2, 1024], BF16)
        p_a = t.ps("p_a", [P, 2, 512])
        s_id, s_go = t.sem("id"), t.sem("go")
        s_got = [t.sem(f"got{r}") for r in range(R)]
        s_hot, s_turn, s_cat, s_q, s_sum, s_alpha = (t.sem(x) for x in ("hot", "turn", "cat", "q", "sum", "alpha"))
        with nc.Block() as block:

            @block.vector
            def _(dve):
                for s in (s_hot, s_sum, s_alpha):
                    dve.sem_inc(s, AHEAD)
                dve.tensor_copy(ident_bf[:], k["ident"][:]).then_inc(s_id, 1)
                if G < L.all_groups:
                    dve.memset(alpha[:, G * 2 * H:], 0.0)

                def codes(g, i, r):
                    dve.wait_ge(s_alpha, g)
                    dve.wait_ge(s_turn, g)
                    dve.tensor_copy(idx[:, r], index[:, bass.ds(g * 2, 2)])
                    dve.tensor_tensor(hot[:, r], k["iota_row"][:].unsqueeze(1).to_broadcast([P, 2, P]),
                                      ids[:, bass.ds(g * 4, 4)].rearrange("p (j w) -> p j w", w=2)[:, :, 1:2]
                                      .to_broadcast([P, 2, P]), ALU.is_equal).then_inc(s_hot, 1)

                def scores(g, i, r):
                    dve.wait_ge(s_got[r], i * 32 + 32)
                    dve.wait_ge(s_q, g + AHEAD + 1)
                    a = alpha[:, bass.ds(g * 2 * H, 2 * H)].rearrange("p (j h) -> p j h", j=2)
                    dve.wait_ge(s_alpha, g + (AHEAD - 1))
                    dve.tensor_copy(values[:, bass.ds(g * 32, 32)].rearrange("p (j f) -> p j f", j=2),
                                    got[:, r, :, 0:16])
                    dve.tensor_tensor(total[:, r % 2], got[:, r, :, 16:20],
                                      p_a[:, r % 2, 0:2 * H].rearrange("p (j h) -> p j h", j=2), ALU.add
                                      ).then_inc(s_sum, 1)
                    dve.wait_ge(s_sum, g + AHEAD + 1)
                    dve.scalar_tensor_tensor(a, total[:, r % 2], 0.2, total[:, r % 2], ALU.mult, ALU.max
                                             ).then_inc(s_alpha, 1)

                staged_groups(dve, G, R, (5, codes), (0, scores))

            @block.scalar
            def _(act):
                act.sem_inc(s_cat, AHEAD)

                def turned(g, i, r):
                    act.wait_ge(s_turn, g + AHEAD + 1)
                    act.wait_ge(s_q, g)
                    act.copy(hot_t[:, r], p_ht[:, r % 2, 0:2 * P]).then_inc(s_cat, 1)

                staged_groups(act, G, R, (0, turned))

            @block.gpsimd
            def _(pool):
                with pool.Fori(0, G // R) as i:
                    for r in range(R):
                        pool.wait_ge(s_hot, i * R + (r + AHEAD + 1))
                        pool.sem_inc(s_go, 1)
                        for j in range(2):
                            pool.indirect_dma_start(
                                out=got[:, r, j], out_offset=None, in_=h_dram,
                                in_offset=bass.IndirectOffsetOnAxis(ap=idx[:, r, j:j + 1], axis=0),
                                ).then_inc(s_got[r], 16)

            @block.tensor
            def _(pe):
                pe.sem_inc(s_turn, AHEAD)
                pe.sem_inc(s_q, AHEAD)
                pe.wait_ge(s_id, 1)

                def turn(g, i, r):
                    pe.wait_ge(s_hot, g + AHEAD + 1)
                    pe.wait_ge(s_cat, g + (AHEAD - 1))
                    for j in range(2):
                        last = pe.transpose(p_ht[:, r % 2, j * P:(j + 1) * P], hot[:, r, j], ident_bf[:])
                    last.then_inc(s_turn, 1)

                blocks = {}

                def load_blocks(i):
                    blocks.update(enumerate(block_numbers(pe, table, i)))

                def product(g, i, r):
                    pe.wait_ge(s_cat, g + AHEAD + 1)
                    pe.wait_ge(s_sum, g + (AHEAD - 1))
                    for j in range(2):
                        for part in range(3):
                            last = pe.matmul(p_a[:, r % 2, j * H:(j + 1) * H], hot_t[:, r, j * P:(j + 1) * P],
                                             ad3[:, bass.ds(blocks[r] * (3 * H) + part * H, H)],
                                             start=(part == 0), stop=(part == 2))
                    last.then_inc(s_q, 1)

                staged_groups(pe, G, R, (2, turn), (0, product), head=load_blocks)


def pick_two(nc, k, name, E, scores, gates):
    NE = NB * E
    with ExitStack() as ctx:
        t = Tools(nc, name, ctx)
        col_i = t.sb("col_i", [P, 2, E, E], I32)
        col = t.sb("col", [P, 2, E, E])
        lower = t.sb("lower", [P, E, E])
        more = t.sb("more", [P, NB, E, E])
        same = t.sb("same", [P, NB, E, E])
        rank = t.sb("rank", [P, NE])
        is_it = t.sb("is_it", [P, 2, NE])
        part = t.sb("part", [P, 2, NE])
        top = t.sb("top", [P, 2, NB])
        gap = t.sb("gap", [P, NB])
        weight = t.sb("weight", [P, 2, NB])
        s_i, s_dve, s_gap, s_exp = (t.sem(x) for x in ("i", "dve", "gap", "exp"))
        with nc.Block() as block:

            @block.gpsimd
            def _(pool):
                pool.iota(col_i[:, 0], pattern=[[1, E], [0, E]], base=0, channel_multiplier=0).then_inc(s_i, 1)
                pool.iota(col_i[:, 1], pattern=[[0, E], [1, E]], base=0, channel_multiplier=0).then_inc(s_i, 1)

            @block.vector
            def _(dve):
                link = Chain(dve, s_dve)
                by = lambda x: x.rearrange("p (b e) -> p b e", e=E)
                mine = by(scores[:]).unsqueeze(3).to_broadcast([P, NB, E, E])
                other = by(scores[:]).unsqueeze(2).to_broadcast([P, NB, E, E])
                dve.wait_ge(s_i, 2)
                link(dve.tensor_copy(col[:], col_i[:]))
                link(dve.tensor_tensor(lower[:], col[:, 1], col[:, 0], ALU.is_lt))
                link(dve.tensor_tensor(more[:], other, mine, ALU.is_gt))
                link(dve.tensor_tensor(same[:], other, mine, ALU.is_equal))
                link(dve.tensor_tensor(same[:], same[:], lower[:].unsqueeze(1).to_broadcast([P, NB, E, E]), ALU.mult))
                link(dve.tensor_tensor(more[:], more[:], same[:], ALU.add))
                link(dve.tensor_reduce(rank[:], more[:].rearrange("p b e f -> p (b e) f"), AX, ALU.add))
                for n in range(2):
                    link(dve.tensor_scalar(is_it[:, n], rank[:], float(n), None, ALU.is_equal))
                    link(dve.tensor_tensor(part[:, n], is_it[:, n], scores[:], ALU.mult))
                    link(dve.tensor_reduce(top[:, n], by(part[:, n]), AX, ALU.add))
                dve.tensor_tensor(gap[:], top[:, 1], top[:, 0], ALU.subtract).then_inc(s_gap, 1)
                dve.wait_ge(s_exp, 1)
                link(dve.tensor_scalar(top[:, 0], weight[:, 1], 1.0, None, ALU.add))
                link(dve.reciprocal(weight[:, 0], top[:, 0]))
                link(dve.tensor_tensor(weight[:, 1], weight[:, 1], weight[:, 0], ALU.mult))
                for n in range(2):
                    link(dve.tensor_tensor(by(part[:, n]), by(is_it[:, n]),
                                           weight[:, n].unsqueeze(2).to_broadcast([P, NB, E]), ALU.mult))
                link(dve.tensor_tensor(gates[:], part[:, 0], part[:, 1], ALU.add))

            @block.scalar
            def _(act):
                act.wait_ge(s_gap, 1)
                act.activation(weight[:, 1], gap[:], ACT.Exp).then_inc(s_exp, 1)


def gat_gates(nc, k, w, acc, scores):
    with ExitStack() as ctx:
        t = Tools(nc, "gat_ln", ctx)
        bias = t.sb("bias", [P, 3, 16])
        den = t.sb("den", [P, NB, 4])
        agg = t.sb("agg", [P, NB, 16])
        sq = t.sb("sq", [P, NB, 16])
        mean = t.sb("mean", [P, NB])
        var = t.sb("var", [P, NB])
        half = t.sb("half", [P, NB])
        rstd = t.sb("rstd", [P, NB])
        s_w, s_dve, s_var, s_rstd = (t.sem(x) for x in ("w", "dve", "var", "rstd"))
        with nc.Block() as block:

            @block.sync
            def _(sp):
                load_all(sp, s_w, [(bias[:].rearrange("p a b -> p (a b)"), spread(w["gat_ln"]))])

            @block.gpsimd
            def _(pool):
                pool.wait_ge(s_var, 1)
                pool.tensor_tensor(rstd[:], var[:], half[:], ALU.pow).then_inc(s_rstd, 1)

            @block.vector
            def _(dve):
                link = Chain(dve, s_dve)
                wide = lambda x: x.unsqueeze(2).to_broadcast([P, NB, 16])
                each = lambda n: bias[:, n].unsqueeze(1).to_broadcast([P, NB, 16])
                a = acc[:].rearrange("p (b f) -> p b f", f=20)
                dve.wait_ge(s_w, 16)
                link(dve.memset(half[:], -0.5))
                link(dve.tensor_scalar(den[:], a[:, :, 16:20], 1e-16, None, ALU.add))
                link(dve.reciprocal(den[:], den[:]))
                link(dve.tensor_tensor(agg[:].rearrange("p b (h e) -> p b h e", e=4),
                                       a[:, :, 0:16].rearrange("p b (h e) -> p b h e", e=4),
                                       den[:].unsqueeze(3).to_broadcast([P, NB, 4, 4]), ALU.mult))
                link(dve.tensor_tensor(agg[:], agg[:], each(0), ALU.add))
                link(dve.tensor_reduce(mean[:], agg[:], AX, ALU.add))
                link(dve.tensor_scalar(mean[:], mean[:], 1.0 / 16, None, ALU.mult))
                link(dve.tensor_tensor(agg[:], agg[:], wide(mean[:]), ALU.subtract))
                link(dve.tensor_tensor(sq[:], agg[:], agg[:], ALU.mult))
                link(dve.tensor_reduce(var[:], sq[:], AX, ALU.add))
                dve.tensor_scalar(var[:], var[:], 1.0 / 16, 1e-5, ALU.mult, ALU.add).then_inc(s_var, 1)
                dve.wait_ge(s_rstd, 1)
                link(dve.tensor_tensor(agg[:], agg[:], wide(rstd[:]), ALU.mult))
                link(dve.tensor_tensor(agg[:], agg[:], each(1), ALU.mult))
                link(dve.tensor_tensor(agg[:], agg[:], each(2), ALU.add))
                link(dve.tensor_reduce(scores[:].rearrange("p (b e) -> p b e", e=4),
                                       agg[:].rearrange("p b (h e) -> p b e h", e=4), AX, ALU.add))
                link(dve.tensor_scalar(scores[:], scores[:], 0.25, None, ALU.mult))


def l1_in(nc, k, w, x_dram, xn_dram, parts, kv):
    H, C = 8, D // 8
    with ExitStack() as ctx:
        t = Tools(nc, "l1_in", ctx)
        w1 = t.sb("w1", [P, 2, D])
        affine = t.sb("affine", [P, 4, D])
        xb = t.sb("xb", [P, 2, D])
        xn = t.sb("xn", [P, 2, D])
        xt = t.sb("xt", [P, D])
        mean = t.sb("mean", [P, H])
        dev = t.sb("dev", [P, D])
        sq = t.sb("sq", [P, D])
        var = t.sb("var", [P, H])
        std = t.sb("std", [P, H])
        half = t.sb("half", [P, H])
        zero = t.sb("zero", [P, D])
        kk = t.sb("kk", [P, 2, D])
        vv = t.sb("vv", [P, 2, D])
        norm = Norm(k, t)
        mul = Product(k, t)
        p_kv = t.ps("p_kv", [P, 512])
        s_w, s_make, s_use, s_var, s_std, s_carry, s_carry2, s_one = (
            t.sem(x) for x in ("w", "make", "use", "var", "std", "carry", "carry2", "one"))
        s_in = [t.sem(f"in{h}") for h in range(2)]
        s_st = [t.sem(f"st{h}") for h in range(2)]
        s_kv, s_sum = t.sem("kv"), t.sem("sum")
        s_sent = t.sem("sent")
        with nc.Block() as block:

            @block.sync
            def _(sp):
                load_all(sp, s_w, [(w1[:], w["gnn_w1"].rearrange("(a p) n -> p a n", p=P)),
                                   (affine[:].rearrange("p a b -> p (a b)"), spread(w["kvln"]))])

                def load(i, h):
                    tt = i * 2 + h
                    sp.wait_ge(mul.s_made, tt)
                    sp.sem_inc(s_carry, 1)
                    sp.dma_start(xb[:, h], x_dram[bass.ds(tt * P, P), :]).then_inc(s_in[h], 16)

                per_tile(sp, load)

            @block.gpsimd
            def _(pool):
                def rows(i, h):
                    tt = i * 2 + h
                    norm.power(pool, tt)
                    pool.wait_ge(mul.s_made, tt + 2)
                    pool.sem_inc(s_sent, 1)
                    pool.dma_start(xn_dram[bass.ds(tt * P, P), :], xn[:, h]).then_inc(s_st[h], 16)

                def heads(i, h):
                    tt = i * 2 + h
                    pool.wait_ge(s_var, tt + 1)
                    pool.sem_inc(s_carry2, 1)
                    pool.tensor_tensor(std[:], var[:], half[:], ALU.pow).then_inc(s_std, 1)

                one_ahead(pool, rows, heads)
                for h, n in ((0, (NB + 1) // 2), (1, NB // 2)):
                    pool.wait_ge(s_st[h], n * 16)

            @block.vector
            def _(dve):
                dve.sem_inc(mul.s_made, 1)
                dve.sem_inc(mul.s_used, 1)
                dve.sem_inc(s_kv, 1)
                dve.memset(zero[:], 0.0)
                dve.memset(half[:], 0.5).then_inc(s_one, 1)
                dve.wait_ge(s_w, 32)
                dve.wait_ge(s_one, 1)
                make, use = Steps(dve, s_make, 2), Steps(dve, s_use, 14)
                by = lambda x: x.rearrange("p (h c) -> p h c", h=H)
                wide = lambda x: x.unsqueeze(2).to_broadcast([P, H, C])

                def rows(i, h):
                    tt = i * 2 + h
                    make.at(tt)
                    dve.wait_ge(s_in[h], i * 16 + 16)
                    dve.wait_ge(s_st[h], i * 16)
                    dve.wait_ge(mul.s_turned, tt)
                    norm(dve, make, xn[:, h], xb[:, h], tt).then_inc(mul.s_made, 1)

                def heads(i, h):
                    tt = i * 2 + h
                    use.at(tt)
                    dve.wait_ge(mul.s_made, tt + 2)
                    dve.wait_ge(s_kv, tt + 1)
                    dve.wait_ge(mul.s_used, tt + 1)
                    use(dve.tensor_reduce(mean[:], by(xn[:, h]), AX, ALU.add))
                    use(dve.tensor_scalar(mean[:], mean[:], 1.0 / C, None, ALU.mult))
                    use(dve.tensor_tensor(by(dev[:]), by(xn[:, h]), wide(mean[:]), ALU.subtract))
                    use(dve.tensor_tensor(sq[:], dev[:], dev[:], ALU.mult))
                    use(dve.tensor_reduce(var[:], by(sq[:]), AX, ALU.add))
                    dve.tensor_scalar(var[:], var[:], 1.0 / (C - 1), None, ALU.mult).then_inc(s_var, 1)
                    dve.wait_ge(mul.s_product, tt + 2)
                    use(dve.tensor_copy(xt[:], mul.p_out[:, h, 0:D]))
                    split_parts(dve, use, parts, tt, xt[:]).then_inc(mul.s_used, 1)
                    dve.wait_ge(s_std, tt + 1)
                    use(dve.tensor_scalar(mean[:], std[:], 1e-5, None, ALU.add))
                    use(dve.reciprocal(mean[:], mean[:]))
                    use(dve.tensor_tensor(by(dev[:]), by(dev[:]), wide(mean[:]), ALU.mult))
                    dve.wait_ge(s_sum, tt)
                    dve.tensor_tensor(kk[:, h], dev[:], affine[:, 0], ALU.mult)
                    use(dve.tensor_tensor(vv[:, h], dev[:], affine[:, 2], ALU.mult))
                    dve.tensor_tensor(vv[:, h], vv[:, h], affine[:, 3], ALU.add)
                    if isinstance(i, int):
                        dve.tensor_tensor(kk[:, h], kk[:, h], affine[:, 1], ALU.add).then_inc(s_one, 1)
                        dve.wait_ge(s_one, 2)
                        dve.tensor_scalar(kk[:, h], kk[:, h], k["exists"][:, NB - 1:NB], None, ALU.mult
                                          ).then_inc(s_kv, 1)
                    else:
                        dve.tensor_tensor(kk[:, h], kk[:, h], affine[:, 1], ALU.add).then_inc(s_kv, 1)

                one_ahead(dve, rows, heads)
                dve.wait_ge(s_sum, NB + 1)
                for a in range(2):
                    last = dve.scalar_tensor_tensor(kv[:, a], p_kv[:, a * P:(a + 1) * P], 1.0 / N,
                                                    k["same_head"][:], ALU.mult, ALU.mult)
                last.then_inc(s_one, 1)
                dve.wait_ge(s_one, 3)

            @block.scalar
            def _(act):
                act.sem_inc(mul.s_copied, 1)
                per_tile(act, lambda i, h: mul.copy(act, i * 2 + h, h))

            @block.tensor
            def _(pe):
                for s in (mul.s_turned, mul.s_product, s_sum):
                    pe.sem_inc(s, 1)
                pe.wait_ge(s_w, 32)
                pe.wait_ge(s_one, 1)
                pe.matmul(p_kv[:, 0:D], k["ident"][:], zero[:], start=True, stop=False, skip_group_check=True)

                def products(i, h):
                    tt = i * 2 + h
                    mul.multiply(pe, tt, h, [(0, [(a, w1[:, a]) for a in range(2)])])
                    pe.wait_ge(s_kv, tt + 2)
                    for a in range(2):
                        last = pe.matmul(p_kv[:, a * P:(a + 1) * P], kk[:, h, a * P:(a + 1) * P],
                                         vv[:, h, a * P:(a + 1) * P], start=False, stop=False,
                                         skip_group_check=True)
                    last.then_inc(s_sum, 1)

                one_ahead(pe, lambda i, h: mul.turn(pe, i * 2 + h, h, xn[:, h]), products)


def guarded(engine, flag):
    if flag is None:
        return nullcontext()
    return engine.If(engine.value_load(flag[0:1, 0:1], min_val=0, max_val=1) == 1)


WIDE_BANKS = -(-NPAD // 512)


def count_matrix(nc, k, phase, table, ids, index, by_target, by_source, rest=None):
    L = CONV
    G, R, C = L.groups, 8, 8
    with ExitStack() as ctx:
        t = Tools(nc, phase, ctx)
        number = t.sb("number", [P, NPAD], mybir.dt.int16)
        key = t.sb("key", [P, G * 2], I32)
        hot_to = t.sb("hot_to", [P, C, P], BF16)
        hot_from = t.sb("hot_from", [P, C, NPAD], BF16)
        counts = t.sb("counts", [P, NPAD], BF16)
        turned = t.sb("turned", [P, NB * P], BF16)
        ident_bf = t.sb("ident_bf", [P, P], BF16)
        minus = t.sb("minus", [P, P], BF16)
        zero = t.sb("zero", [P, 512], BF16)
        p_cnt = t.ps("p_cnt", [P, WIDE_BANKS * 512])
        p_t = t.ps("p_t", [P, 1024], BF16)
        s_set, s_full, s_hi, s_sub, s_out, s_turn, s_back = (
            t.sem(x) for x in ("set", "full", "hi", "sub", "out", "turn", "back"))
        s_hot, s_used = t.sem("hot"), t.sem("used")
        s_st = t.sem("st")
        banks = [(n * 512, min(NPAD, (n + 1) * 512)) for n in range(WIDE_BANKS)]
        batches = [(s0, min(NB, s0 + 8)) for s0 in range(0, NB, 8)]
        NBAT = len(batches)
        after = {min(WIDE_BANKS - 1, (s1 * P - 1) // 512): q for q, (s0, s1) in enumerate(batches)}
        with ExitStack() as early:
            e = Tools(nc, phase + "_set", early)
            number_i = e.sb("number_i", [P, NPAD], I32)
            with nc.Block() as block:

                @block.gpsimd
                def _(pool):
                    pool.iota(number_i[:], pattern=[[1, NPAD]], base=0x4000, channel_multiplier=0
                              ).then_inc(s_set, 1)

                @block.vector
                def _(dve):
                    dve.wait_ge(s_set, 1)
                    dve.tensor_copy(number[:], number_i[:])
                    dve.memset(zero[:], 0.0)
                    dve.tensor_copy(ident_bf[:], k["ident"][:])
                    dve.tensor_scalar(minus[:], k["ident"][:], -1.0, None, ALU.mult)
                    dve.tensor_scalar(key[:], index[:], float(0x4000), None, ALU.add).then_inc(s_set, 1)
                    dve.wait_ge(s_set, 2)
                    dve.tensor_scalar(key[:], key[:], 16, None, ALU.logical_shift_left).then_inc(s_set, 1)
                    dve.wait_ge(s_set, 3)

        with nc.Block() as block:

            @block.sync
            def _(sp):
                with guarded(sp, rest):
                    with sp.Fori(0, NB) as b:
                        sp.wait_ge(s_out, b * WIDE_BANKS + WIDE_BANKS)
                        sp.dma_start(by_target[bass.ds(b, 1)].squeeze(0), counts[:]).then_inc(s_st, 16)
                        sp.wait_ge(s_back, b * NBAT + NBAT)
                        sp.dma_start(by_source[bass.ds(b, 1)].squeeze(0), turned[:]).then_inc(s_st, 16)
                    sp.wait_ge(s_st, NB * 32)

            @block.vector
            def _(dve):
                with guarded(dve, rest):
                    with dve.Fori(0, G // R) as i:
                        for c in range(2 * R):
                            chunk = i * (2 * R) + c
                            dve.wait_ge(s_used, chunk)
                            dve.tensor_scalar(hot_to[:, c % C], k["iota_bf"][:], ids[:, bass.ds(chunk * 2 + 1, 1)],
                                              None, ALU.is_equal)
                            dve.tensor_scalar(hot_from[:, c % C], number[:].bitcast(BF16),
                                              key[:, bass.ds(chunk, 1)].bitcast(F32), None, ALU.is_equal
                                              ).then_inc(s_hot, 1)

            @block.scalar
            def _(act):
                act.copy(counts[:, 0:P], k["iota_bf"][:])
                act.drain()
                with guarded(act, rest):
                    with act.Fori(0, NB) as b:
                        act.wait_ge(s_full, b + 1)
                        act.wait_ge(s_st, b * 32)
                        for n, (c0, c1) in enumerate(banks):
                            if rest is not None:
                                act.copy(counts[:, c0:c1], p_cnt[:, c0:c1]).then_inc(s_hi, 1)
                                act.wait_ge(s_sub, b * WIDE_BANKS + (n + 1))
                            act.copy(counts[:, c0:c1], p_cnt[:, c0:c1]).then_inc(s_out, 1)
                            if n in after:
                                s0, s1 = batches[after[n]]
                                act.wait_ge(s_turn, b * NBAT + (after[n] + 1))
                                act.copy(turned[:, s0 * P:s1 * P], p_t[:, 0:(s1 - s0) * P]).then_inc(s_back, 1)

            @block.tensor
            def _(pe):
                def clear(n):
                    c0, c1 = banks[n]
                    pe.matmul(p_cnt[:, c0:c1], zero[:, 0:P], zero[:, 0:c1 - c0], start=True, stop=False,
                              skip_group_check=True)

                with guarded(pe, rest):
                    pe.sem_inc(s_used, C - 1)
                    for n in range(WIDE_BANKS):
                        clear(n)
                    with pe.Fori(0, G // R) as i:
                        block_of, is_last = block_numbers(pe, table, i), last_groups(pe, table, i)
                        for r in range(R):
                            for j in range(2):
                                c = 2 * r + j
                                pe.wait_ge(s_hot, i * (2 * R) + (c + 1))
                                for c0, c1 in banks:
                                    last = pe.matmul(p_cnt[:, c0:c1], hot_to[:, c % C], hot_from[:, c % C, c0:c1],
                                                     start=False, stop=False, skip_group_check=True)
                                last.then_inc(s_used, 1)
                            with pe.If(is_last[r] == 1):
                                b = block_of[r]
                                pe.matmul(p_cnt[:, 0:1], zero[:, 0:P], zero[:, 0:1], start=False, stop=False,
                                          skip_group_check=True).then_inc(s_full, 1)
                                for n, (c0, c1) in enumerate(banks):
                                    if rest is not None:
                                        pe.wait_ge(s_hi, b * WIDE_BANKS + (n + 1))
                                        pe.matmul(p_cnt[:, c0:c1], minus[:], counts[:, c0:c1], start=False,
                                                  stop=False, skip_group_check=True).then_inc(s_sub, 1)
                                    pe.wait_ge(s_out, b * WIDE_BANKS + (n + 1))
                                    clear(n)
                                    if n in after:
                                        q = after[n]
                                        s0, s1 = batches[q]
                                        pe.wait_ge(s_back, b * NBAT + q)
                                        for s in range(s0, s1):
                                            turn = pe.transpose(p_t[:, (s - s0) * P:(s - s0 + 1) * P],
                                                                counts[:, s * P:(s + 1) * P], ident_bf[:])
                                        turn.then_inc(s_turn, 1)


def rounded_counts(nc, k, by_source, flag):
    with ExitStack() as ctx:
        t = Tools(nc, "rounded", ctx)
        counts = t.sb("counts", [P, 2, NPAD], BF16)
        biggest = t.sb("biggest", [P, NB + 1])
        row = t.sb("row", [1, 4])
        p_row = t.ps("p_row", [P, 512])
        s_in = [t.sem(f"in{h}") for h in range(2)]
        s_used, s_dve, s_turn = t.sem("used"), t.sem("dve"), t.sem("turn")
        with nc.Block() as block:

            @block.sync
            def _(sp):
                def load(i, h):
                    sp.wait_ge(s_used, i * 2 + h)
                    sp.dma_start(counts[:, h], by_source[bass.ds(i * 2 + h, 1)].squeeze(0)).then_inc(s_in[h], 16)

                per_tile(sp, load)

            @block.vector
            def _(dve):
                dve.sem_inc(s_used, 1)
                link = Chain(dve, s_dve)

                def tile(i, h):
                    dve.wait_ge(s_in[h], i * 16 + 16)
                    dve.tensor_reduce(biggest[:, bass.ds(i * 2 + h, 1)], counts[:, h], AX, ALU.max
                                      ).then_inc(s_used, 1)

                per_tile(dve, tile)
                dve.wait_ge(s_used, NB + 1)
                link(dve.tensor_reduce(biggest[:, NB:NB + 1], biggest[:, 0:NB], AX, ALU.max))
                dve.wait_ge(s_turn, 1)
                link(dve.tensor_reduce(row[:, 0:1], p_row[0:1, 0:P], AX, ALU.max))
                link(dve.tensor_scalar(row[:, 1:2], row[:, 0:1], 256.0, None, ALU.is_ge))
                link(dve.tensor_copy(flag[:], row[:, 1:2]))

            @block.tensor
            def _(pe):
                pe.wait_ge(s_dve, 1)
                pe.transpose(p_row[0:1, 0:P], biggest[:, NB:NB + 1], k["ident"][:]).then_inc(s_turn, 1)


def sums_by_target(nc, phase, by_source, parts, acc, counts=None, flag=None):
    with ExitStack() as ctx:
        t = Tools(nc, phase, ctx)
        cnt = t.sb("cnt", [P, 2, NPAD], BF16)
        ones = t.sb("ones", [P, 1], BF16)
        p_sum = t.ps("p_sum", [P, 2, 512])
        s_in = [t.sem(f"in{h}") for h in range(2)]
        s_one, s_sum, s_copied = t.sem("one"), t.sem("sum"), t.sem("copied")
        with nc.Block() as block:

            @block.sync
            def _(sp):
                with guarded(sp, flag):
                    def load(i, h):
                        sp.wait_ge(s_sum, i * 2 + h)
                        sp.dma_start(cnt[:, h], by_source[bass.ds(i * 2 + h, 1)].squeeze(0)).then_inc(s_in[h], 16)

                    per_tile(sp, load)

            @block.vector
            def _(dve):
                with guarded(dve, flag):
                    dve.sem_inc(s_copied, 1)
                    dve.memset(ones[:], 1.0).then_inc(s_one, 1)

                    def tile(i, h):
                        tt = i * 2 + h
                        dve.wait_ge(s_sum, tt + 2)
                        for out, src in ([(acc[:, bass.ds(tt * D, D)], p_sum[:, h, 0:D])] +
                                         ([(counts[:, bass.ds(tt, 1)], p_sum[:, h, D:D + 1])] if counts is not None
                                          else [])):
                            if flag is None:
                                last = dve.tensor_copy(out, src)
                            else:
                                last = dve.tensor_tensor(out, src, out, ALU.add)
                        last.then_inc(s_copied, 1)

                    per_tile(dve, tile)
                    dve.wait_ge(s_copied, NB + 1)

            @block.tensor
            def _(pe):
                with guarded(pe, flag):
                    pe.sem_inc(s_sum, 1)
                    pe.wait_ge(s_one, 1)

                    def tile(i, h):
                        pe.wait_ge(s_in[h], i * 16 + 16)
                        pe.wait_ge(s_copied, i * 2 + h)
                        for s in range(NB):
                            block_s = cnt[:, h, s * P:(s + 1) * P]
                            for part in range(3):
                                last = pe.matmul(p_sum[:, h, 0:D], block_s, parts[:, (s * 3 + part) * D:
                                                                                  (s * 3 + part + 1) * D],
                                                 start=(s == 0 and part == 0), stop=(s == NB - 1 and part == 2))
                        if counts is not None:
                            for s in range(NB):
                                last = pe.matmul(p_sum[:, h, D:D + 1], cnt[:, h, s * P:(s + 1) * P], ones[:],
                                                 start=(s == 0), stop=(s == NB - 1))
                        last.then_inc(s_sum, 1)

                    per_tile(pe, tile)


def sums_by_source(nc, phase, by_target, parts, acc, counts=None, flag=None):
    HALVES = [(0, 14), (14, NB)]
    with ExitStack() as ctx:
        t = Tools(nc, phase, ctx)
        cnt = t.sb("cnt", [P, 2, 14 * P], BF16)
        ones = t.sb("ones", [P, 1], BF16)
        zero = t.sb("zero", [P, 512], BF16)
        p_sum = t.ps("p_sum", [P, 7 * 512])
        p_cnt = t.ps("p_cnt", [P, 512])
        s_in = [t.sem(f"in{h}") for h in range(2)]
        s_one, s_done, s_copied = t.sem("one"), t.sem("done"), t.sem("copied")
        s_used = t.sem("used")
        steps = NB // 2 + 1
        with nc.Block() as block:

            @block.sync
            def _(sp):
                with guarded(sp, flag):
                    for half, (s0, s1) in enumerate(HALVES):
                        def load(i, h):
                            tt = i * 2 + (half * NB + h)
                            sp.wait_ge(s_used, tt)
                            sp.dma_start(cnt[:, (h + half) % 2, 0:(s1 - s0) * P],
                                         by_target[bass.ds(i * 2 + h, 1)].squeeze(0)[:, s0 * P:s1 * P]
                                         ).then_inc(s_in[(h + half) % 2], 16)

                        per_tile(sp, load)

            @block.vector
            def _(dve):
                with guarded(dve, flag):
                    dve.memset(zero[:], 0.0)
                    dve.memset(ones[:], 1.0).then_inc(s_one, 1)
                    for half, (s0, s1) in enumerate(HALVES):
                        dve.wait_ge(s_done, half + 1)
                        pairs = [(acc[:, s0 * D + n * 512:min(s0 * D + n * 512 + 512, s1 * D)],
                                  p_sum[:, n * 512:min(n * 512 + 512, (s1 - s0) * D)]) for n in range((s1 - s0 + 1) // 2)]
                        if counts is not None:
                            pairs.append((counts[:, s0:s1], p_cnt[:, s0:s1]))
                        for out, src in pairs:
                            if flag is None:
                                last = dve.tensor_copy(out, src)
                            else:
                                last = dve.tensor_tensor(out, src, out, ALU.add)
                        last.then_inc(s_copied, 1)
                    dve.wait_ge(s_copied, 2)

            @block.tensor
            def _(pe):
                with guarded(pe, flag):
                    pe.sem_inc(s_used, 1)
                    pe.wait_ge(s_one, 1)
                    for half, (s0, s1) in enumerate(HALVES):
                        if half:
                            pe.wait_ge(s_copied, half)
                        for n in range(7):
                            pe.matmul(p_sum[:, n * 512:(n + 1) * 512], zero[:, 0:P], zero[:], start=True,
                                      stop=False, skip_group_check=True)
                        if not half and counts is not None:
                            pe.matmul(p_cnt[:], zero[:, 0:P], zero[:], start=True, stop=False,
                                      skip_group_check=True)

                        def tile(i, h):
                            tt = i * 2 + h
                            slot = (h + half) % 2
                            before = half * (steps if slot == 0 else steps - 1)
                            pe.wait_ge(s_in[slot], i * 16 + (before * 16 + 16))
                            for s in range(s0, s1):
                                block_s = cnt[:, slot, (s - s0) * P:(s - s0 + 1) * P]
                                for part in range(3):
                                    last = pe.matmul(p_sum[:, (s - s0) * D:(s - s0 + 1) * D], block_s,
                                                     parts[:, bass.ds(tt * (3 * D) + part * D, D)],
                                                     start=False, stop=False, skip_group_check=True)
                                if counts is not None:
                                    last = pe.matmul(p_cnt[:, s:s + 1], block_s, ones[:], start=False, stop=False,
                                                     skip_group_check=True)
                            last.then_inc(s_used, 1)

                        per_tile(pe, tile)
                        pe.matmul(p_sum[:, 0:1], zero[:, 0:P], zero[:, 0:1], start=False, stop=False,
                                  skip_group_check=True).then_inc(s_done, 1)


def inverse_counts(nc, phase, counts, inverse):
    with ExitStack() as ctx:
        t = Tools(nc, phase, ctx)
        some = t.sb("some", [P, NB])
        s_dve = t.sem("dve")
        with nc.Block() as block:

            @block.vector
            def _(dve):
                link = Chain(dve, s_dve)
                link(dve.tensor_scalar(some[:], counts[:], 1.0, None, ALU.min))
                link(dve.tensor_scalar(inverse[:], counts[:], 1.0, None, ALU.max))
                link(dve.reciprocal(inverse[:], inverse[:]))
                link(dve.tensor_tensor(inverse[:], inverse[:], some[:], ALU.mult))


def split_parts(dve, link, parts, tt, value):
    for part in range(3):
        out = parts[:, bass.ds(tt * (3 * D) + part * D, D)]
        if part == 2:
            return dve.tensor_copy(out, value)
        link(dve.tensor_copy(out, value))
        link(dve.tensor_tensor(value, value, out, ALU.subtract))


def mean_parts(nc, phase, acc, inverse, parts):
    with ExitStack() as ctx:
        t = Tools(nc, phase, ctx)
        val = t.sb("val", [P, D])
        s_dve, s_y = t.sem("dve"), t.sem("y")
        with nc.Block() as block:

            @block.vector
            def _(dve):
                link = Steps(dve, s_dve, 5)
                dve.sem_inc(s_y, 1)

                def tile(i, h):
                    tt = i * 2 + h
                    link.at(tt)
                    dve.wait_ge(s_y, tt + 1)
                    link(dve.tensor_scalar(val[:], acc[:, bass.ds(tt * D, D)], inverse[:, bass.ds(tt, 1)], None,
                                           ALU.mult))
                    split_parts(dve, link, parts, tt, val[:]).then_inc(s_y, 1)

                per_tile(dve, tile)
                dve.wait_ge(s_y, NB + 1)


def prelu(dve, link, out, x, low, slope):
    link(dve.tensor_scalar(low, x, 0.0, slope, ALU.min, ALU.mult))
    return dve.scalar_tensor_tensor(out, x, 0.0, low, ALU.max, ALU.add)


def gnn_middle(nc, k, w, acc, inverse, parts):
    with ExitStack() as ctx:
        t = Tools(nc, "middle", ctx)
        w2 = t.sb("w2", [P, 2, D])
        b1 = t.sb("b1", [P, D])
        slope = t.sb("slope", [P, 1])
        pre = t.sb("pre", [P, D])
        low = t.sb("low", [P, D])
        rows_b = t.sb("rows", [P, 2, D])
        xt = t.sb("xt", [P, D])
        mul = Product(k, t)
        s_w, s_dve, s_use = t.sem("w"), t.sem("dve"), t.sem("use")
        with nc.Block() as block:

            @block.sync
            def _(sp):
                load_all(sp, s_w, [(w2[:], w["gnn_w2"].rearrange("(a p) n -> p a n", p=P)),
                                   (b1[:], spread(w["gnn_b1"])), (slope[:], spread(w["gnn_a"]))])

            @block.vector
            def _(dve):
                dve.sem_inc(mul.s_made, 1)
                dve.sem_inc(mul.s_used, 1)
                dve.wait_ge(s_w, 48)
                link, use = Steps(dve, s_dve, 2), Steps(dve, s_use, 5)

                def rows(i, h):
                    tt = i * 2 + h
                    link.at(tt)
                    dve.wait_ge(mul.s_made, tt + 1)
                    link(dve.scalar_tensor_tensor(pre[:], acc[:, bass.ds(tt * D, D)], inverse[:, bass.ds(tt, 1)],
                                                  b1[:], ALU.mult, ALU.add))
                    dve.wait_ge(mul.s_turned, tt)
                    prelu(dve, link, rows_b[:, h], pre[:], low[:], slope[:, 0:1]).then_inc(mul.s_made, 1)

                def out(i, h):
                    tt = i * 2 + h
                    use.at(tt)
                    dve.wait_ge(mul.s_product, tt + 2)
                    dve.wait_ge(mul.s_used, tt + 1)
                    use(dve.tensor_copy(xt[:], mul.p_out[:, h, 0:D]))
                    split_parts(dve, use, parts, tt, xt[:]).then_inc(mul.s_used, 1)

                one_ahead(dve, rows, out)
                dve.wait_ge(mul.s_used, NB + 1)

            @block.scalar
            def _(act):
                act.sem_inc(mul.s_copied, 1)
                per_tile(act, lambda i, h: mul.copy(act, i * 2 + h, h))

            @block.tensor
            def _(pe):
                pe.sem_inc(mul.s_turned, 1)
                pe.sem_inc(mul.s_product, 1)
                pe.wait_ge(s_w, 48)
                one_ahead(pe, lambda i, h: mul.turn(pe, i * 2 + h, h, rows_b[:, h]),
                          lambda i, h: mul.multiply(pe, i * 2 + h, h, [(0, [(a, w2[:, a]) for a in range(2)])]))


def l1_mix(nc, k, w, acc, inverse, kv, xn_dram, x2_dram, x3_dram):
    with ExitStack() as ctx:
        t = Tools(nc, "l1_mix", ctx)
        b2 = t.sb("b2", [P, D])
        slope = t.sb("slope", [P, 1])
        xn = t.sb("xn", [P, 2, D])
        x2 = t.sb("x2", [P, 2, D])
        pre = t.sb("pre", [P, D])
        low = t.sb("low", [P, D])
        total = t.sb("total", [P, 2, D])
        mul = Product(k, t)
        s_w, s_dve, s_carry = t.sem("w"), t.sem("dve"), t.sem("carry")
        s_xn = [t.sem(f"xn{h}") for h in range(2)]
        s_x2 = [t.sem(f"x2{h}") for h in range(2)]
        s_st = [t.sem(f"st{h}") for h in range(2)]
        s_sent = t.sem("sent")
        with nc.Block() as block:

            @block.sync
            def _(sp):
                load_all(sp, s_w, [(b2[:], spread(w["gnn_b2"])), (slope[:], spread(w["gnn_a"]))])

                def load(i, h):
                    tt = i * 2 + h
                    sp.wait_ge(mul.s_used, tt)
                    sp.sem_inc(s_carry, 1)
                    sp.dma_start(xn[:, h], xn_dram[bass.ds(tt * P, P), :]).then_inc(s_xn[h], 16)
                    sp.dma_start(x2[:, h], x2_dram[bass.ds(tt * P, P), :]).then_inc(s_x2[h], 16)

                per_tile(sp, load)

            @block.gpsimd
            def _(pool):
                def store(i, h):
                    pool.wait_ge(mul.s_used, i * 2 + (h + 2))
                    pool.sem_inc(s_sent, 1)
                    pool.dma_start(x3_dram[bass.ds((i * 2 + h) * P, P), :], total[:, h]).then_inc(s_st[h], 16)

                per_tile(pool, store)
                pool.wait_ge(s_st[0], (NB + 1) // 2 * 16)
                pool.wait_ge(s_st[1], NB // 2 * 16)

            @block.vector
            def _(dve):
                dve.sem_inc(mul.s_used, 1)
                dve.wait_ge(s_w, 32)
                link = Steps(dve, s_dve, 6)

                def tile(i, h):
                    tt = i * 2 + h
                    link.at(tt)
                    dve.wait_ge(s_xn[h], i * 16 + 16)
                    dve.wait_ge(s_x2[h], i * 16 + 16)
                    dve.wait_ge(mul.s_used, tt + 1)
                    dve.wait_ge(s_st[h], i * 16)
                    link(dve.scalar_tensor_tensor(pre[:], acc[:, bass.ds(tt * D, D)], inverse[:, bass.ds(tt, 1)],
                                                  b2[:], ALU.mult, ALU.add))
                    link(dve.tensor_tensor(pre[:], pre[:], xn[:, h], ALU.add))
                    link(prelu(dve, link, total[:, h], pre[:], low[:], slope[:, 0:1]))
                    link(dve.tensor_tensor(total[:, h], total[:, h], x2[:, h], ALU.add))
                    dve.wait_ge(mul.s_product, tt + 2)
                    link(dve.tensor_tensor(total[:, h], total[:, h], mul.p_out[:, h, 0:D], ALU.add))
                    dve.tensor_tensor(total[:, h], total[:, h], xn[:, h], ALU.add).then_inc(mul.s_used, 1)

                per_tile(dve, tile)

            @block.scalar
            def _(act):
                act.sem_inc(mul.s_copied, 1)
                per_tile(act, lambda i, h: mul.copy(act, i * 2 + h, h))

            @block.tensor
            def _(pe):
                pe.sem_inc(mul.s_turned, 1)
                pe.sem_inc(mul.s_product, 1)
                pe.sem_inc(mul.s_made, 2 + NB)

                def turn(i, h):
                    pe.wait_ge(s_xn[h], i * 16 + 16)
                    mul.turn(pe, i * 2 + h, h, xn[:, h])

                one_ahead(pe, turn,
                          lambda i, h: mul.multiply(pe, i * 2 + h, h, [(a * P, [(a, kv[:, a])]) for a in range(2)]))


def l1_router(nc, k, w, x_dram, xf_dram, scores):
    E = 8
    with ExitStack() as ctx:
        t = Tools(nc, "router", ctx)
        wr = t.sb("wr", [P, 2, E])
        br = t.sb("br", [P, E])
        gamma = t.sb("gamma", [P, D])
        beta = t.sb("beta", [P, D])
        xb = t.sb("xb", [P, 2, D])
        mid = t.sb("mid", [P, D])
        xf = t.sb("xf", [P, 2, D])
        norm = Norm(k, t, 2)
        mul = Product(k, t)
        s_w, s_dve, s_carry = t.sem("w"), t.sem("dve"), t.sem("carry")
        s_in = [t.sem(f"in{h}") for h in range(2)]
        s_st = [t.sem(f"st{h}") for h in range(2)]
        s_sent = t.sem("sent")
        with nc.Block() as block:

            @block.sync
            def _(sp):
                load_all(sp, s_w, [(wr[:], w["wr"].rearrange("(a p) n -> p a n", p=P)), (br[:], spread(w["br"])),
                                   (gamma[:], spread(w["gamma"])), (beta[:], spread(w["beta"]))])

                def load(i, h):
                    tt = i * 2 + h
                    sp.wait_ge(mul.s_made, tt)
                    sp.sem_inc(s_carry, 1)
                    sp.dma_start(xb[:, h], x_dram[bass.ds(tt * P, P), :]).then_inc(s_in[h], 16)

                per_tile(sp, load)

            @block.gpsimd
            def _(pool):
                def tile(i, h):
                    tt = i * 2 + h
                    norm.power(pool, tt, 0)
                    norm.power(pool, tt, 1)
                    pool.wait_ge(mul.s_made, tt + 2)
                    pool.sem_inc(s_sent, 1)
                    pool.dma_start(xf_dram[bass.ds(tt * P, P), :], xf[:, h]).then_inc(s_st[h], 16)

                per_tile(pool, tile)
                pool.wait_ge(s_st[0], (NB + 1) // 2 * 16)
                pool.wait_ge(s_st[1], NB // 2 * 16)

            @block.vector
            def _(dve):
                dve.sem_inc(mul.s_made, 1)
                dve.sem_inc(mul.s_used, 1)
                dve.wait_ge(s_w, 64)
                link = Steps(dve, s_dve, 7)

                def rows(i, h):
                    tt = i * 2 + h
                    link.at(tt)
                    dve.wait_ge(s_in[h], i * 16 + 16)
                    dve.wait_ge(s_st[h], i * 16)
                    dve.wait_ge(mul.s_turned, tt)
                    link(norm(dve, link, mid[:], xb[:, h], tt, 0))
                    link(norm(dve, link, xf[:, h], mid[:], tt, 1))
                    link(dve.tensor_tensor(xf[:, h], xf[:, h], gamma[:], ALU.mult))
                    dve.tensor_tensor(xf[:, h], xf[:, h], beta[:], ALU.add).then_inc(mul.s_made, 1)

                def out(i, h):
                    tt = i * 2 + h
                    dve.wait_ge(mul.s_product, tt + 2)
                    dve.tensor_tensor(scores[:, bass.ds(tt * E, E)], mul.p_out[:, h, 0:E], br[:], ALU.add
                                      ).then_inc(mul.s_used, 1)

                one_ahead(dve, rows, out)
                dve.wait_ge(mul.s_used, NB + 1)

            @block.scalar
            def _(act):
                act.sem_inc(mul.s_copied, 1)
                per_tile(act, lambda i, h: mul.copy(act, i * 2 + h, h))

            @block.tensor
            def _(pe):
                pe.sem_inc(mul.s_turned, 1)
                pe.sem_inc(mul.s_product, 1)
                pe.wait_ge(s_w, 64)
                one_ahead(pe, lambda i, h: mul.turn(pe, i * 2 + h, h, xf[:, h]),
                          lambda i, h: mul.multiply(pe, i * 2 + h, h, [(0, [(a, wr[:, a]) for a in range(2)])]))



def program(nc, w, out, scratch):
    node = lambda name, width=D: scratch(name, [NPAD, width], F32)
    with ExitStack() as whole, nc.allow_non_contiguous_dma("small tables and strided tiles"):
        t = Tools(nc, "all", whole)
        k = make_constants(nc, t)
        table = {L.name: t.sb(f"table_{L.name}", [1, 1152], I32) for L in (CONV, GAT)}
        ids = t.sb("conv_ids", [P, CONV.all_groups * 4])
        index = t.sb("conv_index", [P, CONV.groups * 2], I32)
        rows = {L.name: scratch(f"rows_{L.name}", [L.places, L.width], I32) for L in (CONV, GAT)}

        def sort(L, attr=None):
            sort_edges(nc, L, k, table[L.name], w[f"{L.name}_dst_rows"], w[f"{L.name}_dst_cols"],
                       w[f"{L.name}_src_cols"], attr, scratch(f"lo_{L.name}", [L.chunks * P], F32),
                       scratch(f"tab_{L.name}", [2, 512], I32), rows[L.name])

        xn, kv_d, skip, xm, x2, z = node("xn"), node("kv", 2 * D), node("skip"), node("xm"), node("h1"), node("z")
        with ExitStack() as c:
            u = Tools(nc, "conv", c)
            alpha = u.sb("alpha", [P, CONV.all_groups * 16])
            with ExitStack() as c2:
                v = Tools(nc, "queries", c2)
                q3 = v.sb("q3", [P, NB * 3 * D], BF16)
                with ExitStack() as c3:
                    m = Tools(nc, "attention", c3)
                    q_mix = m.sb("q_mix", [P, NB * D])
                    kv_all = m.sb("kv_all", [P, 2, D + 1])
                    project(nc, k, w, w["x"], xn, q3, q_mix, kv_all, kv_d, skip)
                    linear_attention(nc, k, w, w["x"], q_mix, kv_all, xm)
                sort(CONV, w["attr"])
                ve = scratch("ve", [CONV.groups, P, 2, D], F32)
                conv_scores(nc, k, table["conv"], rows["conv"], kv_d, w["we"], q3, alpha, ids, index, ve)
            segment_softmax(nc, k, CONV, alpha, ids, (D // CONV.heads) ** -0.5)
            acc = u.sb("acc", [P, NB * (D + CONV.heads)])
            block_sums(nc, k, CONV, table["conv"], ids, alpha, acc, values_dram=ve)
            conv_tail(nc, k, w, acc, xn, skip, x2)
        experts(nc, k, "run_ffn", 2, {"w1": w["ffn_w1"], "b1": w["ffn_b1"], "w2": w["ffn_w2"], "b2": w["ffn_b2"]},
                x2, x2, z)

        x1, xl, h_d, xb = node("x1"), node("xl"), node("h", 20), node("xb")
        with ExitStack() as c:
            u = Tools(nc, "gat", c)
            gates = u.sb("gates", [P, NB * 4])
            scores = u.sb("scores", [P, NB * 4])
            ad3 = u.sb("ad3", [P, NB * 12], BF16)
            gat_in(nc, k, w, z, xm, x1, xl, h_d, ad3)
            with ExitStack() as c2:
                v = Tools(nc, "gat_edges", c2)
                sort(GAT)
                alpha = v.sb("alpha", [P, GAT.all_groups * 8])
                gids = v.sb("ids", [P, GAT.all_groups * 4])
                gindex = v.sb("index", [P, GAT.groups * 2], I32)
                values = v.sb("values", [P, GAT.groups * 32])
                acc = v.sb("acc", [P, NB * 20])
                load_meta(nc, GAT, rows["gat"], gids, gindex)
                gat_scores(nc, k, table["gat"], h_d, ad3, alpha, gids, gindex, values)
                segment_softmax(nc, k, GAT, alpha, gids, 1.0)
                block_sums(nc, k, GAT, table["gat"], gids, alpha, acc, values=values)
                gat_gates(nc, k, w, acc, scores)
            pick_two(nc, k, "pick4", 4, scores, gates)
            experts(nc, k, "run_moe4", 4, {"w1": w["moe4_w1"], "b1": w["moe4_b1"], "w2": w["moe4_w2"],
                                       "b2": w["moe4_b2"]}, xl, x1, xb, gates)

        xn1, x3, xf = node("xn1"), node("x3"), node("xf")
        matrices = {n: scratch(f"counts_{n}", [NB, P, NPAD], BF16) for n in ("t", "s", "t_rest", "s_rest")}
        with ExitStack() as c:
            u = Tools(nc, "l1", c)
            kv = u.sb("kv", [P, 2, P])
            inv_dst = u.sb("inv_dst", [P, NB])
            inv_src = u.sb("inv_src", [P, NB])
            counts = u.sb("counts", [P, NB])
            flag = u.sb("flag", [1, 1], I32)
            edges = (table["conv"], ids, index)
            count_matrix(nc, k, "matrix", *edges, matrices["t"], matrices["s"])
            rounded_counts(nc, k, matrices["s"], flag)
            count_matrix(nc, k, "rest", *edges, matrices["t_rest"], matrices["s_rest"], rest=flag)
            acc = u.sb("acc", [P, NB * D])
            parts = u.sb("parts", [P, NB * 3 * D], BF16)
            l1_in(nc, k, w, xb, xn1, parts, kv)

            def sums(kind, name, counted=None):
                fn = sums_by_target if kind == "s" else sums_by_source
                fn(nc, name, matrices[kind], parts, acc, counted)
                fn(nc, name + "r", matrices[kind + "_rest"], parts, acc, counted, flag)

            sums("s", "sweep1", counts)
            inverse_counts(nc, "inverse1", counts, inv_dst)
            mean_parts(nc, "mean1", acc, inv_dst, parts)
            sums("t", "sweep2", counts)
            inverse_counts(nc, "inverse2", counts, inv_src)
            gnn_middle(nc, k, w, acc, inv_src, parts)
            sums("s", "sweep3")
            mean_parts(nc, "mean3", acc, inv_dst, parts)
            sums("t", "sweep4")
            l1_mix(nc, k, w, acc, inv_src, kv, xn1, xb, x3)

        with ExitStack() as c:
            u = Tools(nc, "l1_moe", c)
            gates = u.sb("gates", [P, NB * 8])
            scores = u.sb("scores", [P, NB * 8])
            l1_router(nc, k, w, x3, xf, scores)
            pick_two(nc, k, "pick8", 8, scores, gates)
            experts(nc, k, "run_moe8", 8, {"w1": w["moe8_w1"], "b1": w["moe8_b1"], "w2": w["moe8_w2"],
                                       "b2": w["moe8_b2"]}, xf, x3, out, gates)


def layout(inputs):
    import numpy as np
    g = {n: np.asarray(a) for n, a in inputs.items()}
    f = lambda *names: np.concatenate([g[n].reshape(-1) for n in names])
    w = {"x": np.concatenate([g["x"], np.zeros((NPAD - N, D), g["x"].dtype)])}

    def edges(L, src, dst):
        pad = L.chunks * P - len(src)
        cols = lambda a: np.ascontiguousarray(a.reshape(L.chunks, P).T)
        dst = np.concatenate([dst, np.full(pad, TOP, dst.dtype)])
        src = np.concatenate([src, np.zeros(pad, src.dtype)])
        w[f"{L.name}_dst_rows"], w[f"{L.name}_dst_cols"], w[f"{L.name}_src_cols"] = dst, cols(dst), cols(src)

    edges(CONV, g["src"], g["dst"])
    loops = np.arange(N, dtype=g["L0_ffn_edge_index"].dtype)
    edges(GAT, *(np.concatenate([g["L0_ffn_edge_index"][n], loops]) for n in range(2)))
    attr = g["edge_attr_64"]
    w["attr"] = np.concatenate([attr, np.zeros((CONV.chunks * P - attr.shape[0], attr.shape[1]), attr.dtype)])
    G, M, F = "L0_gnn_", "L0_mix_", "L0_ffn_"
    w["wcat"] = np.concatenate([g[G + n].T for n in ("Wq", "Wk", "Wv", "Wskip")] + [g[M + "wk"], g[M + "wv"]], 1)
    w["bcat"] = f(G + "bq", G + "bk", G + "bv", G + "bskip", M + "bk", M + "bv")
    for n in ("wq", "bq", "wo", "bo"):
        w["mix_" + n] = g[M + n]
    w["we"] = g[G + "We"].T
    w["wbeta"] = g[G + "Wbeta"].reshape(-1)
    for n in ("ln1_g", "ln1_b", "ln2_g", "ln2_b"):
        w[n] = g[G + n]
    w["ffn_w1"] = g[G + "W1"].T.reshape(D, 2, 512).transpose(1, 0, 2)
    w["ffn_w2"] = g[G + "W2"].T.reshape(2, 512, D)
    w["ffn_b1"], w["ffn_b2"] = g[G + "b1"], g[G + "b2"]
    w["w_gat"] = g[F + "W_gat"]
    w["att"] = f(F + "att_src", F + "att_dst")
    w["gat_ln"] = f(F + "b_gat", F + "ln_gamma", F + "ln_beta")
    for name, prefix in (("moe4", F), ("moe8", "L1_ffn_")):
        w[name + "_w1"], w[name + "_w2"] = g[prefix + "W1"], g[prefix + "W2"]
        w[name + "_b1"], w[name + "_b2"] = f(prefix + "b1"), f(prefix + "b2")
    for n in ("W1", "W2", "b1", "b2", "a"):
        w["gnn_" + n.lower()] = g["L1_gnn_" + n]
    w["kvln"] = f(*("L1_mix_" + n for n in ("kln_weight", "kln_bias", "vln_weight", "vln_bias")))
    w["wr"], w["br"], w["gamma"], w["beta"] = (g["L1_ffn_" + n] for n in ("Wr", "br", "gamma", "beta"))
    return {n: np.ascontiguousarray(a) for n, a in w.items()}


def kernel(**inputs):
    import concourse.bacc as bacc
    from concourse.bass_utils import run_bass_kernel_spmd

    w = layout(inputs)
    nc = bacc.Bacc("TRN2", target_bir_lowering=False, num_devices=1)
    aps = {n: nc.dram_tensor(f"in_{n}", a.shape, mybir.dt.from_np(a.dtype), kind="ExternalInput").ap()
           for n, a in w.items()}
    out = nc.dram_tensor("out", (NPAD, D), F32, kind="ExternalOutput").ap()
    program(nc, aps, out, lambda name, shape, dt: nc.dram_tensor(f"s_{name}", shape, dt).ap())
    r = run_bass_kernel_spmd(nc, [{f"in_{n}": a for n, a in w.items()}], core_ids=[0])
    return r.results[0]["out"][:N]
```

```python
from contextlib import ExitStack, nullcontext

import concourse.bass as bass
from concourse import mybir

P = 128
ALU = mybir.AluOpType
ACT = mybir.ActivationFunctionType
F32 = mybir.dt.float32
BF16 = mybir.dt.bfloat16
I32 = mybir.dt.int32
AX = mybir.AxisListType.X

N = 3125
D = 256
NB = -(-N // P)
NPAD = NB * P
BINS = 32
TOP = BINS * P - 1
UN = 8
GE = 2 * P
FAR = float(1 << 20)
LOW = -1.0e38


class EdgeList:

    def __init__(self, name, edges, heads, attr, steps=1):
        self.name = name
        self.heads = heads
        self.attr = attr
        self.width = attr + 4
        self.chunks = -(-edges // (P * 2 * UN * steps)) * 2 * UN * steps
        self.groups = -(-((edges + NB * GE) // GE) // 8) * 8
        self.pieces = P // heads
        self.per_piece = -(-self.groups // self.pieces)
        self.all_groups = self.per_piece * self.pieces
        self.places = self.all_groups * GE


CONV = EdgeList("conv", 103125, 8, 64)
GAT = EdgeList("gat", 65536 + N, 4, 0, steps=36)


class Chain:

    def __init__(self, engine, sem, base=0):
        self.engine, self.sem, self.base, self.n = engine, sem, base, 0

    def __call__(self, instruction):
        self.n += 1
        instruction.then_inc(self.sem, 1)
        self.engine.wait_ge(self.sem, self.base + self.n)


class Steps:

    def __init__(self, engine, sem, per):
        self.engine, self.sem, self.per, self.n = engine, sem, per, 0

    def at(self, number):
        assert self.n in (0, self.per), self.n
        self.number, self.n = number, 0

    def __call__(self, instruction):
        self.n += 1
        instruction.then_inc(self.sem, 1)
        self.engine.wait_ge(self.sem, self.number * self.per + self.n)


class Tools:

    def __init__(self, nc, phase, ctx):
        self.nc, self.phase, self.ctx, self.sems = nc, phase, ctx, []

    def sb(self, name, shape, dt=F32):
        return self.ctx.enter_context(self.nc.sbuf_tensor(f"{self.phase}_{name}", shape, dt))

    def ps(self, name, shape, dt=F32):
        return self.ctx.enter_context(self.nc.psum_tensor(f"{self.phase}_{name}", shape, dt))

    def sem(self, name):
        if not self.sems:
            self.ctx.callback(self.clear)
        self.sems.append(self.nc.alloc_semaphore(name=f"{self.phase}_{name}"))
        return self.sems[-1]

    def clear(self):
        self.nc.clear_and_free_semaphores(self.sems)
        self.nc.all_engine_barrier()


def make_constants(nc, t):
    k = {
        "iota_row": t.sb("iota_row", [P, P]),
        "iota_bf": t.sb("iota_bf", [P, P], BF16),
        "iota_col": t.sb("iota_col", [P, 1]),
        "ident": t.sb("ident", [P, P]),
        "before": t.sb("before", [P, P]),
        "minus_half": t.sb("minus_half", [P, 1]),
        "same_head": t.sb("same_head", [P, P]),
        "before_bf": t.sb("before_bf", [P, P], BF16),
        "ones": t.sb("ones", [P, P]),
        "exists": t.sb("exists", [P, BINS]),
        "group_start": t.sb("group_start", [P, 4]),
    }
    s_iota, s_dve = t.sem("iota"), t.sem("dve")
    row_i = t.sb("row_i", [P, P], I32)
    col_i = t.sb("col_i", [P, 1], I32)
    node_i = t.sb("node_i", [P, BINS], I32)
    group_i = t.sb("group_i", [P, 4], I32)
    col_f = t.sb("col_f", [P, 1])
    with nc.Block() as block:

        @block.gpsimd
        def _(pool):
            pool.iota(row_i[:], pattern=[[1, P]], base=0, channel_multiplier=0).then_inc(s_iota, 1)
            pool.iota(col_i[:], pattern=[[0, 1]], base=0, channel_multiplier=1).then_inc(s_iota, 1)
            pool.iota(node_i[:], pattern=[[P, BINS]], base=0, channel_multiplier=1).then_inc(s_iota, 1)
            pool.iota(group_i[:], pattern=[[P, 4]], base=0, channel_multiplier=1).then_inc(s_iota, 1)

        @block.vector
        def _(dve):
            link = Chain(dve, s_dve)
            dve.wait_ge(s_iota, 4)
            link(dve.memset(k["ones"][:], 1.0))
            link(dve.memset(k["minus_half"][:], -0.5))
            link(dve.tensor_copy(k["iota_row"][:], row_i[:]))
            link(dve.tensor_copy(k["iota_bf"][:], row_i[:]))
            link(dve.tensor_copy(k["iota_col"][:], col_i[:]))
            link(dve.tensor_copy(k["exists"][:], node_i[:]))
            link(dve.tensor_copy(k["group_start"][:], group_i[:]))
            link(dve.tensor_scalar(k["exists"][:], k["exists"][:], float(N), None, ALU.is_lt))
            link(dve.tensor_scalar(k["group_start"][:], k["group_start"][:], float(GE), None, ALU.mult))
            link(dve.tensor_scalar(k["ident"][:], k["iota_row"][:], k["iota_col"][:, 0:1], None, ALU.is_equal))
            link(dve.tensor_scalar(k["before"][:], k["iota_row"][:], k["iota_col"][:, 0:1], None, ALU.is_gt))
            link(dve.tensor_copy(k["before_bf"][:], k["before"][:]))
            link(dve.tensor_scalar(row_i[:], row_i[:], 5, None, ALU.logical_shift_right))
            link(dve.tensor_scalar(col_i[:], col_i[:], 5, None, ALU.logical_shift_right))
            link(dve.tensor_copy(k["same_head"][:], row_i[:]))
            link(dve.tensor_copy(col_f[:], col_i[:]))
            link(dve.tensor_scalar(k["same_head"][:], k["same_head"][:], col_f[:, 0:1], None, ALU.is_equal))
    return k


class Placing:

    def __init__(self, k, u, L, meta, lo, lo_bf, hi_bf, places, lo_dram, attr, sorted_rows):
        self.k, self.L, self.meta, self.lo, self.lo_bf, self.hi_bf, self.places = (
            k, L, meta, lo, lo_bf, hi_bf, places)
        self.lo_dram, self.attr, self.sorted_rows = lo_dram, attr, sorted_rows
        self.rows = u.sb("rows", [P, 2, UN, L.width], I32)
        self.lo_row = u.sb("lo_row", [P, 2, UN * P], BF16)
        self.lo_hot = u.sb("lo_hot", [P, 2, UN, P], BF16)
        self.hi_hot = u.sb("hi_hot", [P, 2, UN, BINS], BF16)
        self.lo_hot_t = u.sb("lo_hot_t", [P, 2, UN * P])
        self.earlier = u.sb("earlier", [P, 2, UN, P], BF16)
        self.zero = u.sb("zero", [P, P], BF16)
        self.snap = u.sb("snap", [P, 2, BINS])
        self.masked = u.sb("masked", [P, 2, UN, BINS])
        self.where = u.sb("where", [P, 2, UN])
        self.where_i = u.sb("where_i", [P, 2, UN], I32)
        self.running = u.ps("running", [P, 512])
        self.looked = u.ps("looked", [P, 2, 512])
        self.s_zero, self.s_snap, self.s_run, self.s_look, self.s_dve, self.s_hot, self.s_where = (
            u.sem(x) for x in ("zero", "snap", "run", "look", "dve", "hot", "where"))
        self.s_lo = [u.sem(f"lo{h}") for h in range(2)]
        self.s_attr = [u.sem(f"attr{h}") for h in range(2)]
        self.s_out = [u.sem(f"out{h}") for h in range(2)]
        self.s_meta, self.s_go = u.sem("meta"), u.sem("go")
        self.steps = L.chunks // (2 * UN)

    def sync(self, sp):
        A = self.L.attr
        attr_v = self.attr.rearrange("(c p) f -> p c f", p=P) if A else None
        with sp.Fori(0, self.steps) as i:
            for h in range(2):
                c0 = i * (2 * UN) + h * UN
                sp.wait_ge(self.s_hot, i * 2 + h)
                src = self.lo_dram.rearrange("(o e) -> o e", o=1)[:, bass.ds(c0 * P, UN * P)]
                sp.dma_start(self.lo_row[:, h], src.to_broadcast([P, UN * P])).then_inc(self.s_lo[h], 16)
                if A:
                    sp.wait_ge(self.s_out[h], i * (16 * UN))
                    sp.dma_start(self.rows[:, h, :, 0:A].bitcast(F32), attr_v[:, bass.ds(c0, UN), :]
                                 ).then_inc(self.s_attr[h], 16)

    def gpsimd(self, pool):
        most = pool.to_reg(self.L.places - 1)
        with pool.Fori(0, self.steps) as i:
            for h in range(2):
                pool.wait_ge(self.s_where, i * 2 + (h + 2))
                pool.wait_ge(self.s_meta, i * 2 + (h + 1))
                if self.L.attr:
                    pool.wait_ge(self.s_attr[h], i * 16 + 16)
                pool.sem_inc(self.s_go, 1)
                for j in range(UN):
                    pool.indirect_dma_start(
                        out=self.sorted_rows, out_offset=bass.IndirectOffsetOnAxis(
                            ap=self.where_i[:, h, j:j + 1], axis=0),
                        in_=self.rows[:, h, j], in_offset=None, bounds_check=most,
                        oob_is_err=False).then_inc(self.s_out[h], 16)
        for h in range(2):
            pool.wait_ge(self.s_out[h], self.steps * 16 * UN)

    def first_snapshot(self, act):
        act.copy(self.snap[:, 0], self.places[:]).then_inc(self.s_snap, 1)
        act.wait_ge(self.s_snap, 1)

    def snapshot(self, act, i, h, j):
        act.wait_ge(self.s_run, i * (2 * UN) + (h * UN + j + 1))
        act.wait_ge(self.s_look, i * (2 * UN) + (h * UN + j))
        act.copy(self.snap[:, j % 2], self.running[:, 0:BINS]).then_inc(self.s_snap, 1)

    def copy_meta(self, act, i, h):
        A = self.L.attr
        act.wait_ge(self.s_out[h], i * (16 * UN))
        act.copy(self.rows[:, h, :, A:A + 4], self.meta[:, bass.ds(i * (2 * UN) + h * UN, UN), :]
                 ).then_inc(self.s_meta, 1)

    def first_product(self, pe):
        pe.wait_ge(self.s_zero, 1)
        pe.matmul(self.running[:, 0:BINS], self.zero[:], self.zero[:, 0:BINS], start=True, stop=False,
                  skip_group_check=True)
        pe.matmul(self.running[:, 0:BINS], self.k["ident"][:], self.places[:], start=False, stop=False,
                  skip_group_check=True).then_inc(self.s_run, 1)
        pe.matmul(self.looked[:, 0, 0:BINS], self.zero[:], self.zero[:, 0:BINS], start=True, stop=True
                  ).then_inc(self.s_look, 1)

    def look_up(self, pe, i, h, j):
        if j == 0:
            pe.wait_ge(self.s_hot, i * 2 + (h + 2))
            pe.wait_ge(self.s_where, i * 2 + h)
        out = self.looked[:, h, j * BINS:(j + 1) * BINS]
        pe.wait_ge(self.s_snap, i * (2 * UN) + (h * UN + j + 2))
        pe.matmul(self.running[:, 0:BINS], self.lo_hot[:, h, j], self.hi_hot[:, h, j], start=False,
                  stop=False, skip_group_check=True).then_inc(self.s_run, 1)
        pe.matmul(out, self.lo_hot_t[:, h, j * P:(j + 1) * P], self.snap[:, j % 2], start=True, stop=False)
        pe.matmul(out, self.earlier[:, h, j], self.hi_hot[:, h, j], start=False, stop=True
                  ).then_inc(self.s_look, 1)

    def first_codes(self, dve):
        dve.memset(self.zero[:], 0.0).then_inc(self.s_zero, 1)
        dve.memset(self.where[:], 0.0).then_inc(self.s_hot, 1)
        dve.memset(self.where_i[:], 0).then_inc(self.s_where, 1)
        dve.wait_ge(self.s_hot, 1)
        dve.wait_ge(self.s_where, 1)
        self.codes(dve, 0, 0)

    def codes(self, dve, i, h):
        k, c0 = self.k, i * (2 * UN) + h * UN
        dve.tensor_tensor(
            self.lo_hot[:, h], k["iota_bf"][:].unsqueeze(1).to_broadcast([P, UN, P]),
            self.lo_bf[:, bass.ds(c0, UN)].unsqueeze(2).to_broadcast([P, UN, P]), ALU.is_equal)
        dve.tensor_tensor(
            self.hi_hot[:, h], k["iota_bf"][:, 0:BINS].unsqueeze(1).to_broadcast([P, UN, BINS]),
            self.hi_bf[:, bass.ds(c0, UN)].unsqueeze(2).to_broadcast([P, UN, BINS]), ALU.is_equal)
        dve.wait_ge(self.s_lo[h], i * 16 + 16)
        dve.tensor_scalar(self.lo_hot_t[:, h], self.lo_row[:, h], k["iota_col"][:, 0:1], None, ALU.is_equal)
        for j in range(UN):
            last = dve.scalar_tensor_tensor(
                self.earlier[:, h, j], self.lo_row[:, h, j * P:(j + 1) * P], self.lo[:, bass.ds(c0 + j, 1)],
                k["before_bf"][:], ALU.is_equal, ALU.mult)
        last.then_inc(self.s_hot, 1)

    def find(self, dve, i, h):
        dve.wait_ge(self.s_look, i * (2 * UN) + ((h + 1) * UN + 1))
        dve.tensor_tensor(self.masked[:, h], self.looked[:, h, 0:UN * BINS].rearrange(
            "p (j b) -> p j b", j=UN), self.hi_hot[:, h], ALU.mult).then_inc(self.s_dve, 1)
        dve.wait_ge(self.s_dve, i * 4 + (h * 2 + 1))
        dve.tensor_reduce(self.where[:, h], self.masked[:, h], AX, ALU.add).then_inc(self.s_dve, 1)
        dve.wait_ge(self.s_dve, i * 4 + (h * 2 + 2))
        dve.wait_ge(self.s_out[h], i * (16 * UN))
        dve.tensor_copy(self.where_i[:, h], self.where[:, h]).then_inc(self.s_where, 1)


def place_alone(nc, placing):
    steps = placing.steps
    with nc.Block() as block:

        @block.sync
        def _(sp):
            placing.sync(sp)

        @block.scalar
        def _(act):
            placing.first_snapshot(act)
            with act.Fori(0, steps) as i:
                for h in range(2):
                    for j in range(UN):
                        placing.snapshot(act, i, h, j)
                    placing.copy_meta(act, i, h)

        @block.tensor
        def _(pe):
            placing.first_product(pe)
            with pe.Fori(0, steps) as i:
                for h in range(2):
                    for j in range(UN):
                        placing.look_up(pe, i, h, j)

        @block.vector
        def _(dve):
            placing.first_codes(dve)
            with dve.Fori(0, steps - 1) as i:
                placing.codes(dve, i, 1)
                placing.find(dve, i, 0)
                placing.codes(dve, i + 1, 0)
                placing.find(dve, i, 1)
            placing.codes(dve, steps - 1, 1)
            placing.find(dve, steps - 1, 0)
            placing.find(dve, steps - 1, 1)

        @block.gpsimd
        def _(pool):
            placing.gpsimd(pool)


def sort_edges(nc, L, k, table, dst_rows, dst_cols, src_cols, attr, lo_dram, table_dram, sorted_rows,
               beside=None):
    C, W, A = L.chunks, L.width, L.attr
    with ExitStack() as ctx:
        t = Tools(nc, f"sort_{L.name}", ctx)
        meta = t.sb("meta", [P, C, 4], I32)
        lo = t.sb("lo", [P, C])
        lo_bf = t.sb("lo_bf", [P, C], BF16)
        hi_bf = t.sb("hi_bf", [P, C], BF16)
        places = t.sb("places", [P, BINS])
        with ExitStack() as inner:
            u = Tools(nc, f"count_{L.name}", inner)
            dst_i = u.sb("dst_i", [P, C], I32)
            src_i = u.sb("src_i", [P, C], I32)
            hi_i = u.sb("hi_i", [P, C], I32)
            row_i = u.sb("row_i", [P, C], I32)
            row_f = u.sb("row_f", [P, C], BF16)
            fill = u.sb("fill", [P, L.per_piece * 2, W], I32)
            lo_hot = u.sb("lo_hot", [P, 2, UN, P], BF16)
            hi_hot = u.sb("hi_hot", [P, 2, UN, BINS], BF16)
            zero = u.sb("zero", [P, P], BF16)
            cnt = u.sb("cnt", [P, BINS])
            total_i = u.sb("total_i", [P, BINS], I32)
            padded = u.sb("padded", [P, NB])
            end = u.sb("end", [P, NB])
            tmp = u.sb("tmp", [P, BINS])
            onesrow = u.sb("onesrow", [P, NB])
            cmp = u.sb("cmp", [P, 4, NB])
            group_end = u.sb("group_end", [P, 4])
            found = u.sb("found", [P, 4])
            found_i = u.sb("found_i", [P, 2, 4], I32)
            bits = u.sb("bits", [1, 64, 8])
            not_end = u.sb("not_end", [1, 64, 8])
            word = u.sb("word", [1, 2, 64])
            hist = u.ps("hist", [P, BINS])
            totals = u.ps("totals", [P, BINS])
            prefix = u.ps("prefix", [P, BINS])
            s_in, s_row, s_rowf, s_fill, s_filled = (u.sem(x) for x in ("in", "row", "rowf", "fill", "filled"))
            s_prep, s_hot, s_counted, s_cnt, s_sums = (u.sem(x) for x in ("prep", "hot", "counted", "cnt", "sums"))
            s_dve, s_tab, s_tabd, s_lo = (u.sem(x) for x in ("dve", "tab", "tabd", "lo"))
            NF = L.places // (P * L.per_piece * 2)

            with nc.Block() as block:

                @block.sync
                def _(sp):
                    sp.dma_start(dst_i[:], dst_cols).then_inc(s_in, 16)
                    sp.dma_start(src_i[:], src_cols).then_inc(s_in, 16)
                    sp.dma_start(row_i[:], dst_rows.rearrange("(p c) -> p c", p=P)).then_inc(s_row, 16)
                    sp.wait_ge(s_rowf, 1)
                    sp.dma_start(lo_dram.rearrange("(p c) -> p c", p=P), row_f[:]).then_inc(s_lo, 16)
                    sp.wait_ge(s_fill, 3)
                    view = sorted_rows.rearrange("(f p c) w -> f p (c w)", f=NF, p=P)
                    for f in range(NF):
                        sp.dma_start(view[f], fill[:].rearrange("p c w -> p (c w)")).then_inc(s_filled, 16)
                    sp.wait_ge(s_tab, 2)
                    sp.dma_start(table_dram.rearrange("a (q p) -> p a q", p=P), found_i[:]).then_inc(s_tabd, 16)
                    sp.wait_ge(s_tabd, 16)
                    sp.dma_start(table[:, 0:1024], table_dram.rearrange("a g -> (a g)").rearrange("(o g) -> o g", o=1)
                                 ).then_inc(s_tabd, 16)
                    sp.wait_ge(s_tabd, 32)
                    sp.wait_ge(s_lo, 16)
                    sp.wait_ge(s_filled, 16 * NF)

                @block.gpsimd
                def _(pool):
                    pool.memset(zero[:], 0.0).then_inc(s_fill, 1)
                    pool.memset(fill[:], 0).then_inc(s_fill, 1)
                    pool.wait_ge(s_fill, 2)
                    pool.memset(fill[:, :, A + 1:A + 3], -1).then_inc(s_fill, 1)

                @block.vector
                def _(dve):
                    link = Chain(dve, s_dve)
                    dve.wait_ge(s_in, 32)
                    link(dve.tensor_scalar(dst_i[:], dst_i[:], float(TOP), None, ALU.min))
                    link(dve.tensor_scalar(hi_i[:], dst_i[:], 7, None, ALU.logical_shift_right))
                    link(dve.tensor_copy(hi_bf[:], hi_i[:]))
                    link(dve.memset(meta[:], 0))
                    link(dve.tensor_scalar(meta[:, :, 0], src_i[:], float(N - 1), None, ALU.min))
                    link(dve.tensor_copy(meta[:, :, 1], dst_i[:]))
                    link(dve.tensor_scalar(meta[:, :, 2], dst_i[:], 127, None, ALU.bitwise_and))
                    link(dve.tensor_copy(lo[:], meta[:, :, 2]))
                    link(dve.tensor_copy(lo_bf[:], meta[:, :, 2]))
                    dve.wait_ge(s_row, 16)
                    link(dve.tensor_scalar(row_i[:], row_i[:], float(TOP), None, ALU.min))
                    link(dve.tensor_scalar(row_i[:], row_i[:], 127, None, ALU.bitwise_and))
                    dve.tensor_copy(row_f[:], row_i[:]).then_inc(s_rowf, 1)
                    with dve.Fori(0, C // (2 * UN)) as i:
                        for h in range(2):
                            c0 = i * (2 * UN) + h * UN
                            dve.wait_ge(s_counted, i * 2 + (h + 1))
                            dve.tensor_tensor(
                                lo_hot[:, h], k["iota_bf"][:].unsqueeze(1).to_broadcast([P, UN, P]),
                                lo_bf[:, bass.ds(c0, UN)].unsqueeze(2).to_broadcast([P, UN, P]), ALU.is_equal)
                            dve.tensor_tensor(
                                hi_hot[:, h], k["iota_bf"][:, 0:BINS].unsqueeze(1).to_broadcast([P, UN, BINS]),
                                hi_bf[:, bass.ds(c0, UN)].unsqueeze(2).to_broadcast([P, UN, BINS]),
                                ALU.is_equal).then_inc(s_hot, 1)
                    dve.wait_ge(s_counted, 2 + C // UN)
                    dve.tensor_tensor(cnt[:], hist[:], k["exists"][:], ALU.mult).then_inc(s_cnt, 1)
                    dve.wait_ge(s_sums, 1)
                    link(dve.tensor_scalar(tmp[:], totals[:], float(GE - 1), None, ALU.add))
                    link(dve.tensor_copy(total_i[:], tmp[:]))
                    link(dve.tensor_scalar(total_i[:], total_i[:], 8, None, ALU.logical_shift_right))
                    link(dve.tensor_copy(tmp[:], total_i[:]))
                    link(dve.tensor_scalar(padded[:], tmp[:, 0:NB], 1.0, float(GE), ALU.max, ALU.mult))
                    link(dve.memset(onesrow[:], 1.0))
                    link(dve.tensor_tensor_scan(end[:], onesrow[:], padded[:], 0.0, ALU.mult, ALU.add))
                    link(dve.tensor_scalar(tmp[:], k["exists"][:], -FAR, FAR, ALU.mult, ALU.add))
                    link(dve.tensor_tensor(places[:], prefix[:], tmp[:], ALU.add))
                    link(dve.tensor_tensor(places[:, 0:NB], places[:, 0:NB], end[:], ALU.add))
                    link(dve.tensor_tensor(places[:, 0:NB], places[:, 0:NB], padded[:], ALU.subtract))
                    ends = end[:].unsqueeze(1).to_broadcast([P, 4, NB])
                    link(dve.tensor_tensor(
                        cmp[:], ends, k["group_start"][:].unsqueeze(2).to_broadcast([P, 4, NB]), ALU.is_le))
                    link(dve.tensor_reduce(found[:], cmp[:], AX, ALU.add))
                    link(dve.tensor_scalar(found[:], found[:], float(NB - 1), None, ALU.min))
                    dve.tensor_copy(found_i[:, 0], found[:]).then_inc(s_tab, 1)
                    link(dve.tensor_scalar(group_end[:], k["group_start"][:], float(GE), None, ALU.add))
                    link(dve.tensor_tensor(
                        cmp[:], ends, group_end[:].unsqueeze(2).to_broadcast([P, 4, NB]), ALU.is_equal))
                    dve.wait_ge(s_tab, 1)
                    link(dve.tensor_reduce(found[:], cmp[:], AX, ALU.add))
                    dve.tensor_copy(found_i[:, 1], found[:]).then_inc(s_tab, 1)
                    blocks, lasts = (table[:, a * 512:a * 512 + 512].rearrange("o (i r) -> o i r", r=8)
                                     for a in range(2))
                    dve.wait_ge(s_tabd, 32)
                    link(dve.tensor_copy(bits[:], lasts))
                    for r in range(1, 8):
                        link(dve.tensor_scalar(bits[:, :, r:r + 1], bits[:, :, r:r + 1], float(1 << r), None, ALU.mult))
                    link(dve.tensor_reduce(word[:, 0], bits[:], AX, ALU.add))
                    link(dve.tensor_copy(table[:, 1088:1152], word[:, 0]))
                    link(dve.tensor_scalar(not_end[:], blocks, float(NB - 1), None, ALU.is_lt))
                    link(dve.tensor_tensor(bits[:], bits[:], not_end[:], ALU.mult))
                    link(dve.tensor_reduce(word[:, 0], bits[:], AX, ALU.add))
                    link(dve.tensor_copy(word[:, 1], blocks[:, :, 0]))
                    link(dve.tensor_scalar(word[:, 1], word[:, 1], 256.0, None, ALU.mult))
                    link(dve.tensor_tensor(word[:, 0], word[:, 0], word[:, 1], ALU.add))
                    link(dve.tensor_copy(table[:, 1024:1088], word[:, 0]))

                @block.tensor
                def _(pe):
                    pe.wait_ge(s_fill, 1)
                    pe.matmul(hist[:], zero[:], zero[:, 0:BINS], start=True, stop=False,
                              skip_group_check=True).then_inc(s_counted, 1)
                    pe.matmul(hist[:], zero[:], zero[:, 0:BINS], start=False, stop=False,
                              skip_group_check=True).then_inc(s_counted, 1)
                    with pe.Fori(0, C // (2 * UN)) as i:
                        for h in range(2):
                            pe.wait_ge(s_hot, i * 2 + (h + 1))
                            for j in range(UN):
                                last = pe.matmul(hist[:], lo_hot[:, h, j], hi_hot[:, h, j], start=False,
                                                 stop=False, skip_group_check=True)
                            last.then_inc(s_counted, 1)
                    pe.wait_ge(s_cnt, 1)
                    pe.matmul(totals[:], k["ones"][:], cnt[:], start=True, stop=True)
                    pe.matmul(prefix[:], k["before"][:], cnt[:], start=True, stop=True).then_inc(s_sums, 1)

        with ExitStack() as inner:
            u = Tools(nc, f"place_{L.name}", inner)
            placing = Placing(k, u, L, meta, lo, lo_bf, hi_bf, places, lo_dram, attr, sorted_rows)
            (beside or place_alone)(nc, placing)


def per_tile(engine, body):
    with engine.Fori(0, NB // 2) as i:
        body(i, 0)
        body(i, 1)
    body(NB // 2, 0)


class Norm:

    def __init__(self, k, t, per=1):
        self.per, self.half = per, k["minus_half"][:]
        self.stats = t.sb("ln_stats", [P, 6])
        self.mv = t.sb("ln_mv", [P, per, 2])
        self.rstd = t.sb("ln_rstd", [P, per])
        self.s_var, self.s_rstd, self.s_carry = t.sem("ln_var"), t.sem("ln_rstd"), t.sem("ln_carry")

    def power(self, pool, tt, j=0):
        pool.wait_ge(self.s_var, tt * self.per + (j + 1))
        pool.sem_inc(self.s_carry, 1)
        pool.tensor_tensor(self.rstd[:, j:j + 1], self.mv[:, j, 1:2], self.half, ALU.pow
                           ).then_inc(self.s_rstd, 1)

    def __call__(self, dve, link, out, x, tt, j=0):
        self.statistics(dve, link, x, j)
        dve.wait_ge(self.s_rstd, tt * self.per + (j + 1))
        return dve.tensor_scalar(out, x, self.mv[:, j, 0:1], self.rstd[:, j:j + 1], ALU.subtract, ALU.mult)

    def affine(self, dve, link, out, x, weight, bias, tt, j=0):
        self.statistics(dve, link, x, j)
        link(dve.scalar_tensor_tensor(out, x, self.mv[:, j, 0:1], weight, ALU.subtract, ALU.mult))
        dve.wait_ge(self.s_rstd, tt * self.per + (j + 1))
        return dve.scalar_tensor_tensor(out, out, self.rstd[:, j:j + 1], bias, ALU.mult, ALU.add)

    def statistics(self, dve, link, x, j):
        link(dve.bn_stats(self.stats[:], x))
        dve.sem_inc(self.s_carry, 1)
        link(dve.bn_aggr(self.mv[:, j], self.stats[:]))
        dve.tensor_scalar(self.mv[:, j, 1:2], self.mv[:, j, 1:2], 1e-5, None, ALU.add).then_inc(self.s_var, 1)


def spread(row):
    return row.rearrange("(o n) -> o n", o=1).to_broadcast([P, row.shape[0]])


def project(nc, k, w, x_dram, xn_dram, q3, q_mix, kv_all, kv_dram, skip_dram):
    WIDE = 6 * D
    with ExitStack() as ctx:
        t = Tools(nc, "proj", ctx)
        wcat = t.sb("wcat", [P, 2, WIDE])
        bcat = t.sb("bcat", [P, WIDE])
        wq = t.sb("wq", [P, 2, D])
        bq = t.sb("bq", [P, 2])
        xb = t.sb("xb", [P, 2, D])
        xnb = t.sb("xnb", [P, 2, D])
        norm = Norm(k, t)
        xt = t.sb("xt", [P, 2, 2, P])
        kvb = t.sb("kvb", [P, 2, 2 * D])
        skb = t.sb("skb", [P, 2, D])
        qf = t.sb("qf", [P, D])
        mk = t.sb("mk", [P, 2, 2, D])
        low = t.sb("low", [P, 2, 2, D])
        up = t.sb("up", [P, 2, 2, D])
        feat = t.sb("feat", [P, 2, D])
        mv1 = t.sb("mv1", [P, 2, D + 1])
        warm = t.sb("warm", [P, 1])
        p_t = t.ps("p_t", [P, 2, 512])
        p_w = t.ps("p_w", [P, 3, 512])
        p_q = t.ps("p_q", [P, 512])
        p_kv = t.ps("p_kv", [P, 2, 512])
        s_w, s_one = t.sem("w"), t.sem("one")
        s_x = [t.sem(f"x{h}") for h in range(2)]
        s_st = [t.sem(f"st{h}") for h in range(2)]
        s_xn, s_tr, s_xt, s_low, s_up, s_feat, s_kv = (
            t.sem(x) for x in ("xn", "tr", "xt", "low", "up", "feat", "kv"))
        s_pw = [t.sem(f"pw{c}") for c in range(4)]
        s_dw = [t.sem(f"dw{c}") for c in range(4)]
        s_stx = [t.sem(f"stx{h}") for h in range(2)]
        s_sent2 = t.sem("sent2")
        s_dve, s_make = t.sem("dve"), t.sem("make")
        s_sent = t.sem("sent")
        with nc.Block() as block:

            @block.sync
            def _(sp):
                sp.dma_start(wcat[:], w["wcat"].rearrange("(k p) n -> p k n", p=P)).then_inc(s_w, 16)
                sp.dma_start(bcat[:], spread(w["bcat"])).then_inc(s_w, 16)
                sp.dma_start(wq[:], w["mix_wq"].rearrange("(k p) n -> p k n", p=P)).then_inc(s_w, 16)
                sp.dma_start(bq[:], w["mix_bq"].rearrange("(k p) -> p k", p=P)).then_inc(s_w, 16)

                def load(i, h):
                    sp.wait_ge(s_xn, i * 2 + h)
                    sp.dma_start(xb[:, h], x_dram[bass.ds((i * 2 + h) * P, P), :]).then_inc(s_x[h], 16)

                def store(i, h):
                    tt = i * 2 + h
                    sp.wait_ge(s_xn, tt + 2)
                    sp.sem_inc(s_sent, 1)
                    sp.dma_start(xn_dram[bass.ds(tt * P, P), :], xnb[:, h]).then_inc(s_stx[h], 16)

                one_ahead(sp, load, store)
                sp.wait_ge(s_stx[0], (NB + 1) // 2 * 16)
                sp.wait_ge(s_stx[1], NB // 2 * 16)

            @block.gpsimd
            def _(pool):
                per_tile(pool, lambda i, h: norm.power(pool, i * 2 + h))

            @block.vector
            def _(dve):
                for s in (s_xn, *s_dw, s_low, s_feat):
                    dve.sem_inc(s, 1)
                dve.memset(mv1[:, :, D:D + 1], 1.0).then_inc(s_one, 1)
                dve.wait_ge(s_w, 64)
                dve.wait_ge(s_one, 1)
                make, link = Steps(dve, s_make, 2), Steps(dve, s_dve, 6 + 1)

                def rows(i, h):
                    tt = i * 2 + h
                    make.at(tt)
                    dve.wait_ge(s_x[h], i * 16 + 16)
                    dve.wait_ge(s_tr, tt)
                    dve.wait_ge(s_stx[h], i * 16)
                    norm(dve, make, xnb[:, h], xb[:, h], tt).then_inc(s_xn, 1)

                def tile(i, h):
                    tt = i * 2 + h
                    link.at(tt)
                    dve.wait_ge(s_pw[0], tt + 2)
                    link(dve.tensor_tensor(qf[:], p_w[:, 0, 0:D], bcat[:, 0:D], ALU.add))
                    for part in range(3):
                        out = q3[:, bass.ds(tt * (3 * D) + part * D, D)]
                        link(dve.tensor_copy(out, qf[:]))
                        if part < 2:
                            link(dve.tensor_tensor(qf[:], qf[:], out, ALU.subtract))
                    dve.wait_ge(s_st[h], i * 32)
                    dve.tensor_tensor(kvb[:, h, 0:D], p_w[:, 0, D:2 * D], bcat[:, D:2 * D], ALU.add
                                      ).then_inc(s_dw[0], 1)
                    dve.wait_ge(s_pw[1], tt + 2)
                    dve.tensor_tensor(kvb[:, h, D:2 * D], p_w[:, 1, 0:D], bcat[:, 2 * D:3 * D], ALU.add)
                    dve.tensor_tensor(skb[:, h], p_w[:, 1, D:2 * D], bcat[:, 3 * D:4 * D], ALU.add
                                      ).then_inc(s_dw[1], 1)
                    dve.wait_ge(s_pw[2], tt + 2)
                    dve.wait_ge(s_kv, tt)
                    dve.tensor_tensor(mk[:, h, 0], p_w[:, 2, 0:D], bcat[:, 4 * D:5 * D], ALU.add)
                    dve.tensor_tensor(mv1[:, h, 0:D], p_w[:, 2, D:2 * D], bcat[:, 5 * D:6 * D], ALU.add
                                      ).then_inc(s_dw[2], 1)
                    dve.wait_ge(s_pw[3], tt + 2)
                    for a in range(2):
                        last = dve.tensor_scalar(mk[:, h, 1, a * P:(a + 1) * P], p_q[:, a * P:(a + 1) * P],
                                                 bq[:, a:a + 1], None, ALU.add)
                    last.then_inc(s_dw[3], 1)
                    dve.wait_ge(s_dw[3], tt + 2)
                    dve.tensor_scalar(low[:, h], mk[:, h], 0.0, None, ALU.min).then_inc(s_low, 1)
                    dve.wait_ge(s_up, tt + 2)
                    link(dve.scalar_tensor_tensor(feat[:, h], mk[:, h, 0], 0.0, up[:, h, 0], ALU.max, ALU.add))
                    if isinstance(i, int):
                        dve.tensor_scalar(feat[:, h], feat[:, h], k["exists"][:, NB - 1:NB], None, ALU.mult)
                    dve.scalar_tensor_tensor(q_mix[:, bass.ds(tt * D, D)], mk[:, h, 1], 0.0, up[:, h, 1],
                                             ALU.max, ALU.add).then_inc(s_feat, 1)

                one_ahead(dve, rows, tile)
                dve.wait_ge(s_kv, NB + 1)
                dve.tensor_copy(kv_all[:], p_kv[:, :, 0:D + 1]).then_inc(s_one, 1)

            @block.scalar
            def _(act):
                act.sem_inc(s_xt, 1)
                act.sem_inc(s_up, 1)
                act.wait_ge(s_w, 64)
                act.activation(warm[:], k["ones"][:, 0:1], ACT.Exp)

                def copy(i, h):
                    tt = i * 2 + h
                    act.wait_ge(s_tr, tt + 2)
                    act.wait_ge(s_pw[3], tt)
                    act.copy(xt[:, h], p_t[:, h, 0:D].rearrange("p (a b) -> p a b", a=2)).then_inc(s_xt, 1)

                def exponentials(i, h):
                    tt = i * 2 + h
                    act.wait_ge(s_low, tt + 2)
                    act.wait_ge(s_feat, tt)
                    act.activation(up[:, h], low[:, h], ACT.Exp).then_inc(s_up, 1)
                    act.wait_ge(s_dw[3], tt + 2)
                    act.sem_inc(s_sent2, 1)
                    act.dma_start(kv_dram[bass.ds(tt * P, P), :], kvb[:, h]).then_inc(s_st[h], 16)
                    act.dma_start(skip_dram[bass.ds(tt * P, P), :], skb[:, h]).then_inc(s_st[h], 16)

                one_ahead(act, copy, exponentials)
                act.wait_ge(s_st[0], (NB + 1) // 2 * 32)
                act.wait_ge(s_st[1], NB // 2 * 32)

            @block.tensor
            def _(pe):
                for s in (s_tr, *s_pw, s_kv):
                    pe.sem_inc(s, 1)
                pe.wait_ge(s_w, 64)

                def turn(i, h):
                    tt = i * 2 + h
                    pe.wait_ge(s_xn, tt + 2)
                    pe.wait_ge(s_xt, tt)
                    for a in range(2):
                        last = pe.transpose(p_t[:, h, a * P:(a + 1) * P], xnb[:, h, a * P:(a + 1) * P], k["ident"][:])
                    last.then_inc(s_tr, 1)

                def products(i, h):
                    tt = i * 2 + h
                    pe.wait_ge(s_xt, tt + 2)
                    for c in range(3):
                        pe.wait_ge(s_dw[c], tt + 1)
                        for a in range(2):
                            last = pe.matmul(p_w[:, c], xt[:, h, a], wcat[:, a, c * 512:(c + 1) * 512],
                                             start=(a == 0), stop=(a == 1))
                        last.then_inc(s_pw[c], 1)
                    pe.wait_ge(s_dw[3], tt + 1)
                    for b in range(2):
                        for a in range(2):
                            last = pe.matmul(p_q[:, b * P:(b + 1) * P], wq[:, a, b * P:(b + 1) * P], xt[:, h, a],
                                             start=(a == 0), stop=(a == 1))
                    last.then_inc(s_pw[3], 1)

                def sums(i, h, first=False):
                    tt = i * 2 + h
                    pe.wait_ge(s_feat, tt + 2)
                    for a in range(2):
                        last = pe.matmul(p_kv[:, a, 0:D + 1], feat[:, h, a * P:(a + 1) * P], mv1[:, h],
                                         start=first, stop=False, skip_group_check=True)
                    last.then_inc(s_kv, 1)

                turn(0, 0)
                products(0, 0)
                turn(0, 1)
                products(0, 1)
                turn(1, 0)
                sums(0, 0, first=True)
                with pe.Fori(1, NB // 2) as i:
                    products(i, 0)
                    turn(i, 1)
                    sums(i - 1, 1)
                    products(i, 1)
                    turn(i + 1, 0)
                    sums(i, 0)
                products(NB // 2, 0)
                sums(NB // 2 - 1, 1)
                sums(NB // 2, 0)


def conv_scores(nc, k, table, sorted_rows, kv_dram, we2, q3, alpha, ids, index, ve_dram):
    L = CONV
    G, A, W = L.groups, L.attr, L.width
    R = 8
    with ExitStack() as ctx:
        t = Tools(nc, "scores", ctx)
        we = t.sb("we", [A, D])
        rows = t.sb("rows", [P, R, 2, W], I32)
        hot = t.sb("hot", [P, R, 2, P], BF16)
        hot_t = t.sb("hot_t", [P, R, 2 * P], BF16)
        attr_t = t.sb("attr_t", [A, R, 2 * P])
        kv = t.sb("kv", [P, R, 2, 2 * D])
        prod = t.sb("prod", [P, 2 * D])
        ident_bf = t.sb("ident_bf", [P, P], BF16)
        p_at = t.ps("p_at", [P, 2, 512])
        p_ht = t.ps("p_ht", [P, 2, 1024], BF16)
        p_e = t.ps("p_e", [P, 2, 512])
        p_q = t.ps("p_q", [P, 2, 512])
        s_w, s_id, s_go, s_carry = t.sem("w"), t.sem("id"), t.sem("go"), t.sem("carry")
        s_rows = [t.sem(f"rows{r}") for r in range(R)]
        s_got = [t.sem(f"got{r}") for r in range(R)]
        s_ve = [t.sem(f"ve{r}") for r in range(R)]
        s_hot, s_turn, s_cat, s_e, s_q, s_kv, s_prod, s_alpha = (
            t.sem(x) for x in ("hot", "turn", "cat", "e", "q", "kv", "prod", "alpha"))
        with nc.Block() as block:
            AHEAD = R - 1

            @block.sync
            def _(sp):
                sp.dma_start(we[:], we2).then_inc(s_w, 16)
                view = sorted_rows.rearrange("(g p j) w -> g p (j w)", p=P, j=2)

                def load(g, i, r):
                    sp.wait_ge(s_got[r], i * 32)
                    sp.sem_inc(s_carry, 1)
                    sp.wait_ge(s_turn, g)
                    sp.wait_ge(s_hot, g)
                    sp.sem_inc(s_carry, 1)
                    sp.dma_start(rows[:, r].rearrange("p j w -> p (j w)"), view[bass.ds(g, 1)].squeeze(0)
                                 ).then_inc(s_rows[r], 16)

                def store(g, i, r):
                    sp.wait_ge(s_got[r], i * 32 + 32)
                    sp.sem_inc(s_carry, 1)
                    sp.dma_start(ve_dram[bass.ds(g, 1)].squeeze(0), kv[:, r, :, D:2 * D]).then_inc(s_ve[r], 16)

                for r in range(R):
                    load(r, 0, r)
                with sp.Fori(0, G // R - 1) as i:
                    for r in range(R):
                        store(i * R + r, i, r)
                        load(i * R + (R + r), i + 1, r)
                for r in range(R):
                    store(G - R + r, G // R - 1, r)
                for r in range(R):
                    sp.wait_ge(s_ve[r], G // R * 16)

            @block.vector
            def _(dve):
                dve.sem_inc(s_hot, AHEAD)
                dve.sem_inc(s_prod, AHEAD)
                dve.sem_inc(s_alpha, AHEAD)
                dve.tensor_copy(ident_bf[:], k["ident"][:]).then_inc(s_id, 1)
                if G < L.all_groups:
                    dve.memset(alpha[:, G * 16:], 0.0)
                    dve.memset(ids[:, G * 4:], -1.0)

                def codes(g, i, r):
                    dve.wait_ge(s_rows[r], i * 16 + 16)
                    dve.wait_ge(s_turn, g)
                    dve.tensor_tensor(hot[:, r], k["iota_row"][:].unsqueeze(1).to_broadcast([P, 2, P]),
                                      rows[:, r, :, A + 2:A + 3].to_broadcast([P, 2, P]), ALU.is_equal)
                    dve.tensor_copy(index[:, bass.ds(g * 2, 2)], rows[:, r, :, A])
                    dve.tensor_copy(ids[:, bass.ds(g * 4, 4)].rearrange("p (j w) -> p j w", j=2),
                                    rows[:, r, :, A + 1:A + 3]).then_inc(s_hot, 1)

                def scores(g, i, r):
                    dve.wait_ge(s_got[r], i * 32 + 32)
                    dve.wait_ge(s_q, g + AHEAD + 1)
                    dve.wait_ge(s_alpha, g + AHEAD)
                    dve.tensor_tensor(prod[:].rearrange("p (j f) -> p j f", j=2), kv[:, r, :, 0:D],
                                      p_q[:, r % 2].rearrange("p (j f) -> p j f", j=2), ALU.mult
                                      ).then_inc(s_prod, 1)
                    dve.wait_ge(s_prod, g + AHEAD + 1)
                    dve.tensor_reduce(alpha[:, bass.ds(g * 16, 16)], prod[:].rearrange("p (x f) -> p x f", f=32),
                                      AX, ALU.add).then_inc(s_alpha, 1)

                staged_groups(dve, G, R, (5, codes), (0, scores))

            @block.scalar
            def _(act):
                act.sem_inc(s_cat, AHEAD)
                act.sem_inc(s_kv, AHEAD)
                act.copy(attr_t[:, 0, 0:P], k["iota_row"][0:A]).then_inc(s_id, 1)
                act.wait_ge(s_id, 2)

                def turned(g, i, r):
                    act.wait_ge(s_turn, g + AHEAD + 1)
                    act.wait_ge(s_q, g)
                    act.copy(attr_t[:, r], p_at[0:A, r % 2, 0:2 * P])
                    act.copy(hot_t[:, r], p_ht[:, r % 2, 0:2 * P]).then_inc(s_cat, 1)

                def start_kv(g, i, r):
                    act.wait_ge(s_e, g + AHEAD + 1)
                    act.wait_ge(s_prod, g)
                    act.wait_ge(s_ve[r], i * 16)
                    act.copy(kv[:, r].rearrange("p j (c f) -> p j c f", c=2),
                             p_e[:, r % 2].rearrange("p (j f) -> p j f", j=2).unsqueeze(2)
                             .to_broadcast([P, 2, 2, D])).then_inc(s_kv, 1)

                staged_groups(act, G, R, (4, turned), (3, start_kv))

            @block.gpsimd
            def _(pool):
                with pool.Fori(0, G // R) as i:
                    for r in range(R):
                        pool.wait_ge(s_kv, i * R + (r + AHEAD + 1))
                        pool.sem_inc(s_go, 1)
                        for j in range(2):
                            pool.indirect_dma_start(
                                out=kv[:, r, j], out_offset=None, in_=kv_dram,
                                in_offset=bass.IndirectOffsetOnAxis(ap=rows[:, r, j, A:A + 1], axis=0),
                                compute_op=ALU.add).then_inc(s_got[r], 16)
                for r in range(R):
                    pool.wait_ge(s_got[r], G // R * 32)

            @block.tensor
            def _(pe):
                pe.sem_inc(s_turn, AHEAD)
                pe.sem_inc(s_e, AHEAD)
                pe.sem_inc(s_q, AHEAD)
                pe.wait_ge(s_w, 16)
                pe.wait_ge(s_id, 2)

                def turn(g, i, r):
                    pe.wait_ge(s_hot, g + AHEAD + 1)
                    pe.wait_ge(s_cat, g + (AHEAD - 1))
                    for j in range(2):
                        pe.transpose(p_ht[:, r % 2, j * P:(j + 1) * P], hot[:, r, j], ident_bf[:])
                    for j in range(2):
                        last = pe.transpose(p_at[0:A, r % 2, j * P:(j + 1) * P],
                                            rows[:, r, j, 0:A].bitcast(F32), k["ident"][:])
                    last.then_inc(s_turn, 1)

                def product_e(g, i, r):
                    pe.wait_ge(s_cat, g + AHEAD + 1)
                    pe.wait_ge(s_kv, g + (AHEAD - 1))
                    for j in range(2):
                        last = pe.matmul(p_e[:, r % 2, j * D:(j + 1) * D], attr_t[:, r, j * P:(j + 1) * P],
                                         we[:], start=True, stop=True)
                    last.then_inc(s_e, 1)

                def product_q(g, i, r):
                    block_of = blocks[r]
                    pe.wait_ge(s_prod, g + (AHEAD - 1))
                    for j in range(2):
                        for part in range(3):
                            last = pe.matmul(p_q[:, r % 2, j * D:(j + 1) * D], hot_t[:, r, j * P:(j + 1) * P],
                                             q3[:, bass.ds(block_of * (3 * D) + part * D, D)],
                                             start=(part == 0), stop=(part == 2))
                    last.then_inc(s_q, 1)

                blocks = {}

                def load_blocks(i):
                    blocks.update(enumerate(block_numbers(pe, table, i)))

                staged_groups(pe, G, R, (4, turn), (3, product_e), (0, product_q), head=load_blocks)


def segment_softmax(nc, k, L, alpha, ids, scale):
    H, M, Q = L.heads, L.pieces, L.per_piece
    LEN = 2 * Q * P
    with ExitStack() as ctx:
        t = Tools(nc, f"soft_{L.name}", ctx)
        a = t.sb("a", [P, LEN])
        seg = t.sb("seg", [P, LEN + 1])
        best = t.sb("best", [P, LEN])
        wide = t.sb("wide", [P, 4, P])
        edge = t.sb("edge", [P, 8])
        row = t.sb("row", [1, 8, P])
        p_t = t.ps("p_t", [P, 4, 512])
        p_row = t.ps("p_row", [P, 512])
        p_col = t.ps("p_col", [P, 512])
        s_wide, s_t, s_out = (t.sem(x) for x in ("wide", "t", "out"))
        s_dve, s_ask, s_turned, s_exp = (t.sem(x) for x in ("dve", "ask", "turned", "exp"))
        b_wide, b_t, b_out = (t.sem(x) for x in ("b_wide", "b_t", "b_out"))
        av = alpha[:, 0:M * 2 * Q * H].rearrange("p (m t w) -> p m t w", m=M, w=H)
        idv = ids[:, 0:M * 2 * Q * 2].rearrange("p (m t w) -> p m t w", m=M, w=2)

        def ordered(x, q, j):
            return x.rearrange("p (q e j) -> p q j e", q=Q, j=2)[:, bass.ds(q, 1), j, :].squeeze(1)

        with nc.Block() as block:

            @block.vector
            def _(dve):
                dve.sem_inc(s_wide, 3)
                with dve.Fori(0, Q) as q:
                    for n in range(4):
                        dve.wait_ge(s_t, q * 4 + n)
                        c = bass.ds(q * 2 + n // 2, 1)
                        src = (idv[:, :, c, 0:1].squeeze(2).to_broadcast([P, M, H]) if n % 2 == 0
                               else av[:, :, c, :].squeeze(2))
                        dve.tensor_copy(wide[:, n].rearrange("p (m h) -> p m h", m=M), src).then_inc(s_wide, 1)

            @block.tensor
            def _(pe):
                pe.sem_inc(s_t, 3)
                with pe.Fori(0, Q) as q:
                    for n in range(4):
                        pe.wait_ge(s_wide, q * 4 + (n + 4))
                        pe.wait_ge(s_out, q * 4 + n)
                        pe.transpose(p_t[:, n, 0:P], wide[:, n], k["ident"][:]).then_inc(s_t, 1)

            @block.scalar
            def _(act):
                act.sem_inc(s_out, 3)
                act.copy(row[0:1, 0], k["ones"][0:1]).then_inc(s_exp, 1)
                with act.Fori(0, Q) as q:
                    for n in range(4):
                        act.wait_ge(s_t, q * 4 + (n + 4))
                        act.copy(ordered(seg[:, 0:LEN] if n % 2 == 0 else a[:], q, n // 2), p_t[:, n, 0:P]
                                 ).then_inc(s_out, 1)
                act.wait_ge(s_exp, 1)

        with nc.Block() as block:

            @block.vector
            def _(dve):
                link = Chain(dve, s_dve)
                asked = [0]

                def turned():
                    asked[0] += 1
                    dve.sem_inc(s_ask, 1)
                    dve.wait_ge(s_turned, asked[0])

                link(dve.tensor_copy(edge[:, 0:1], seg[:, 0:1]))
                link(dve.tensor_copy(edge[:, 1:2], seg[:, LEN - 1:LEN]))
                link(dve.tensor_tensor(best[:, 1:LEN], seg[:, 1:LEN], seg[:, 0:LEN - 1], ALU.not_equal))
                turned()
                link(dve.tensor_copy(row[:, 0:2].rearrange("o a p -> o (a p)"), p_row[0:1, 0:2 * P]))
                link(dve.memset(row[:, 2:4], 1.0))
                link(dve.tensor_tensor(row[:, 2, H:P], row[:, 0, H:P], row[:, 1, 0:P - H], ALU.not_equal))
                link(dve.tensor_copy(row[:, 3, 0:P - H], row[:, 2, H:P]))
                link(dve.tensor_scalar(row[:, 2:4], row[:, 2:4], LOW, None, ALU.mult))
                turned()
                link(dve.tensor_copy(seg[:, 0:1], p_col[:, 0:1]))
                link(dve.tensor_copy(seg[:, LEN:LEN + 1], p_col[:, 1:2]))
                link(dve.tensor_scalar(seg[:, 1:LEN], best[:, 1:LEN], LOW, None, ALU.mult))
                link(dve.tensor_reduce(edge[:, 2:3], seg[:, 0:LEN], AX, ALU.min))
                link(dve.tensor_reduce(edge[:, 3:4], seg[:, 1:LEN + 1], AX, ALU.min))
                forth = (seg[:, 0:LEN], a[:])
                back_out = alpha[:, 0:LEN]
                back = (seg[:, 1:LEN + 1][:, ::-1], a[:, ::-1])
                link(dve.tensor_tensor_scan(best[:], *forth, LOW, ALU.add, ALU.max))
                link(dve.tensor_tensor_scan(back_out[:, ::-1], *back, LOW, ALU.add, ALU.max))
                link(dve.tensor_copy(edge[:, 0:1], best[:, LEN - 1:LEN]))
                link(dve.tensor_copy(edge[:, 1:2], back_out[:, 0:1]))
                turned()
                link(dve.tensor_copy(row[:, 0:4].rearrange("o a (h m) -> o a h m", h=H),
                                     p_row[0:1, 0:4 * P].rearrange("o (a m h) -> o a h m", a=4, h=H)))
                by_head = row[:].rearrange("o a (h m) -> o a h m", h=H)
                link(dve.memset(by_head[:, 2, :, 0:1], LOW))
                link(dve.memset(by_head[:, 3, :, M - 1:M], LOW))
                link(dve.tensor_tensor_scan(row[:, 4], row[:, 2], row[:, 0], LOW, ALU.add, ALU.max))
                link(dve.tensor_tensor_scan(row[:, 5, ::-1], row[:, 3, ::-1], row[:, 1, ::-1], LOW, ALU.add, ALU.max))
                link(dve.memset(row[:, 6:8], LOW))
                by_piece = row[:].rearrange("o a (m h) -> o a h m", h=H)
                link(dve.tensor_copy(by_piece[:, 6, :, 1:M], by_head[:, 4, :, 0:M - 1]))
                link(dve.tensor_copy(by_piece[:, 7, :, 0:M - 1], by_head[:, 5, :, 1:M]))
                turned()
                link(dve.tensor_copy(edge[:, 4:6], p_col[:, 0:2]))
                link(dve.tensor_tensor_scan(best[:], *forth, edge[:, 4:5], ALU.add, ALU.max))
                link(dve.tensor_tensor_scan(back_out[:, ::-1], *back, edge[:, 5:6], ALU.add, ALU.max))
                link(dve.tensor_tensor(best[:], best[:], back_out, ALU.max))
                dve.tensor_tensor(a[:], a[:], best[:], ALU.subtract).then_inc(s_ask, 1)

            @block.tensor
            def _(pe):
                one = k["ident"][0:1, 0:1]
                for n, (cols, rows) in enumerate((((0, 1), ()), ((), (2, 3)), ((0, 1, 2, 3), ()), ((), (6, 7)))):
                    pe.wait_ge(s_ask, n + 1)
                    for c in cols:
                        last = pe.transpose(p_row[0:1, c * P:(c + 1) * P], edge[:, c:c + 1], k["ident"][:])
                    for c, r in enumerate(rows):
                        last = pe.transpose(p_col[:, c:c + 1], row[0:1, r], one)
                    last.then_inc(s_turned, 1)

            @block.scalar
            def _(act):
                act.wait_ge(s_ask, 5)
                act.activation(a[:], a[:], ACT.Exp, scale=scale).then_inc(s_exp, 1)
                act.wait_ge(s_exp, 2)

        with nc.Block() as block:

            @block.tensor
            def _(pe):
                pe.sem_inc(b_t, 1)
                with pe.Fori(0, Q) as q:
                    for n in range(2):
                        pe.wait_ge(b_wide, q * 2 + (n + 1))
                        pe.wait_ge(b_out, q * 2 + n)
                        pe.transpose(p_t[:, n, 0:P], wide[:, n], k["ident"][:]).then_inc(b_t, 1)

            @block.vector
            def _(dve):
                with dve.Fori(0, Q) as q:
                    for n in range(2):
                        dve.wait_ge(b_t, q * 2 + n)
                        dve.tensor_copy(wide[:, n], ordered(a[:], q, n)).then_inc(b_wide, 1)

            @block.scalar
            def _(act):
                act.sem_inc(b_out, 1)
                act.copy(edge[:, 0:1], k["ones"][:, 0:1]).then_inc(s_exp, 1)
                with act.Fori(0, Q) as q:
                    for n in range(2):
                        act.wait_ge(b_t, q * 2 + (n + 2))
                        act.copy(av[:, :, bass.ds(q * 2 + n, 1), :].squeeze(2),
                                 p_t[:, n, 0:P].rearrange("p (m h) -> p m h", m=M)).then_inc(b_out, 1)
                act.wait_ge(s_exp, 3)


def block_sums(nc, k, L, table, ids, weights, acc, values_dram=None, values=None):
    G, H = L.groups, L.heads
    F = D if L is CONV else 16
    R = 8
    with ExitStack() as ctx:
        t = Tools(nc, f"sums_{L.name}", ctx)
        hot = t.sb("hot", [P, R, 2, P])
        msg = t.sb("msg", [P, R, 2, F + H])
        zero = t.sb("zero", [P, P], BF16)
        vb = t.sb("vb", [P, R, 2, F]) if values_dram is not None else None
        p_acc = t.ps("p_acc", [P, 512])
        s_v = [t.sem(f"v{r}") for r in range(R)]
        s_zero, s_full, s_copied, s_carry = t.sem("zero"), t.sem("full"), t.sem("copied"), t.sem("carry")
        s_w, s_msg, s_sum = (t.sem(x) for x in ("w", "msg", "sum"))
        with nc.Block() as block:

            if values_dram is not None:
                @block.sync
                def _(sp):
                    with sp.Fori(0, G // R) as i:
                        for r in range(R):
                            sp.wait_ge(s_msg, i * R + r)
                            sp.sem_inc(s_carry, 1)
                            sp.dma_start(vb[:, r], values_dram[bass.ds(i * R + r, 1)].squeeze(0)
                                         ).then_inc(s_v[r], 16)

            @block.gpsimd
            def _(pool):
                pool.memset(zero[:], 0.0).then_inc(s_zero, 1)
                with pool.Fori(0, G // R) as i:
                    for r in range(R):
                        g = i * R + r
                        pool.wait_ge(s_sum, g)
                        pool.tensor_copy(msg[:, r, :, F:F + H],
                                         weights[:, bass.ds(g * 2 * H, 2 * H)].rearrange("p (j h) -> p j h", j=2)
                                         ).then_inc(s_w, 1)

            @block.vector
            def _(dve):
                dve.sem_inc(s_msg, 7)
                with dve.Fori(0, G // R) as i:
                    for r in range(R):
                        g = i * R + r
                        if vb is not None:
                            dve.wait_ge(s_v[r], i * 16 + 16)
                            src = vb[:, r]
                        else:
                            src = values[:, bass.ds(g * 2 * F, 2 * F)].rearrange("p (j f) -> p j f", j=2)
                        dve.wait_ge(s_sum, g)
                        w = weights[:, bass.ds(g * 2 * H, 2 * H)].rearrange("p (j h) -> p j h", j=2)
                        for j in range(2):
                            dve.tensor_scalar(hot[:, r, j], k["iota_row"][:], ids[:, bass.ds(g * 4 + (2 * j + 1), 1)],
                                              None, ALU.is_equal)
                        last = dve.tensor_tensor(
                            msg[:, r, :, 0:F].rearrange("p j (h f) -> p j h f", h=H),
                            src.rearrange("p j (h f) -> p j h f", h=H),
                            w.unsqueeze(3).to_broadcast([P, 2, H, F // H]), ALU.mult)
                        last.then_inc(s_msg, 1)

            @block.tensor
            def _(pe):
                pe.sem_inc(s_sum, 7)
                pe.wait_ge(s_zero, 1)

                def clear():
                    pe.matmul(p_acc[:, 0:F + H], zero[:], acc_zero, start=True, stop=False, skip_group_check=True)

                acc_zero = zero[:, 0:1].to_broadcast([P, F + H])
                clear()
                with pe.Fori(0, G // R) as i:
                    is_last = last_groups(pe, table, i)
                    for r in range(R):
                        g = i * R + r
                        pe.wait_ge(s_w, g + 1)
                        pe.wait_ge(s_msg, g + 8)
                        for j in range(2):
                            last = pe.matmul(p_acc[:, 0:F + H], hot[:, r, j], msg[:, r, j], start=False,
                                             stop=False, skip_group_check=True)
                        last.then_inc(s_sum, 1)
                        with pe.If(is_last[r] == 1):
                            pe.matmul(p_acc[:, 0:F + H], zero[:], acc_zero, start=False, stop=False,
                                      skip_group_check=True).then_inc(s_full, 1)
                            pe.wait_ge(s_copied, block_of_group(pe, table, g) + 1)
                            clear()

            @block.scalar
            def _(act):
                with act.Fori(0, NB) as b:
                    act.wait_ge(s_full, b + 1)
                    act.copy(acc[:, bass.ds(b * (F + H), F + H)], p_acc[:, 0:F + H]).then_inc(s_copied, 1)
                act.wait_ge(s_copied, NB)


def one_ahead(engine, first, second):
    first(0, 0)
    with engine.Fori(0, NB // 2) as i:
        first(i, 1)
        second(i, 0)
        first(i + 1, 0)
        second(i, 1)
    second(NB // 2, 0)


def staged_groups(engine, G, R, *stages, head=None):
    for lead, body in stages:
        for g in range(lead):
            body(g, 0, g)
    with engine.Fori(0, G // R - 1) as i:
        if head:
            head(i)
        for r in range(R):
            for lead, body in stages:
                later = (r + lead) // R
                body(i * R + (r + lead), i + later, (r + lead) % R)
    if head:
        head(G // R - 1)
    for g in range(G - R, G):
        for lead, body in stages:
            if g + lead < G:
                body(g + lead, (g + lead) // R, (g + lead) % R)


def block_numbers(engine, table, i):
    held = lambda value, most: engine.snap(engine.to_reg(value), min_val=0, max_val=most)
    word = engine.value_load(table[0:1, bass.ds(i + 1024, 1)], min_val=0, max_val=NB * 256 - 1)
    blocks = [held(word >> 8, NB - 1)]
    for r in range(7):
        blocks.append(held(blocks[r] + ((word >> r) & 1), NB - 1))
    return blocks


def block_of_group(engine, table, g):
    return engine.value_load(table[0:1, bass.ds(g, 1)], min_val=0, max_val=NB - 1)


def last_groups(engine, table, i):
    word = engine.value_load(table[0:1, bass.ds(i + 1088, 1)], min_val=0, max_val=255)
    return [(word >> r) & 1 for r in range(8)]


def load_all(sp, sem, pairs):
    for out, src in pairs:
        sp.dma_start(out, src).then_inc(sem, 16)
    return 16 * len(pairs)


def linear_attention(nc, k, w, x_dram, q_mix, kv_all, out_dram):
    with ExitStack() as ctx:
        t = Tools(nc, "mixer", ctx)
        wo = t.sb("wo", [P, 2, D])
        bo = t.sb("bo", [P, D])
        kv_m = t.sb("kv_m", [P, 2, P])
        ks_m = t.sb("ks_m", [P, 2, P])
        xb = t.sb("xb", [P, 2, D])
        den = t.sb("den", [P, D])
        o_t = t.sb("o_t", [P, 2, D])
        yb = t.sb("yb", [P, 2, D])
        p_o = t.ps("p_o", [P, 2, 512])
        p_y = t.ps("p_y", [P, 2, 512])
        s_w, s_set, s_ratio, s_add = (t.sem(x) for x in ("w", "set", "ratio", "add"))
        s_x = [t.sem(f"x{h}") for h in range(2)]
        s_st = [t.sem(f"st{h}") for h in range(2)]
        s_o, s_ot, s_py, s_y = (t.sem(x) for x in ("o", "ot", "py", "y"))
        s_sent = t.sem("sent")
        with nc.Block() as block:

            @block.sync
            def _(sp):
                load_all(sp, s_w, [(wo[:], w["mix_wo"].rearrange("(k p) n -> p k n", p=P)),
                                   (bo[:], spread(w["mix_bo"]))])

                def load(i, h):
                    sp.wait_ge(s_y, i * 2 + h)
                    sp.dma_start(xb[:, h], x_dram[bass.ds((i * 2 + h) * P, P), :]).then_inc(s_x[h], 16)

                per_tile(sp, load)

            @block.gpsimd
            def _(pool):
                def store(i, h):
                    pool.wait_ge(s_y, i * 2 + (h + 2))
                    pool.sem_inc(s_sent, 1)
                    pool.dma_start(out_dram[bass.ds((i * 2 + h) * P, P), :], yb[:, h]).then_inc(s_st[h], 16)

                per_tile(pool, store)
                pool.wait_ge(s_st[0], (NB + 1) // 2 * 16)
                pool.wait_ge(s_st[1], NB // 2 * 16)

            @block.vector
            def _(dve):
                dve.sem_inc(s_ot, 1)
                dve.sem_inc(s_y, 1)
                for a in range(2):
                    dve.tensor_tensor(kv_m[:, a], kv_all[:, a, a * P:(a + 1) * P], k["same_head"][:], ALU.mult)
                    last = dve.tensor_scalar(ks_m[:, a], k["same_head"][:], kv_all[:, a, D:D + 1], None, ALU.mult)
                last.then_inc(s_set, 1)
                dve.wait_ge(s_w, 32)
                link = Steps(dve, s_ratio, 2)
                add = Steps(dve, s_add, 1)

                def ratio(i, h):
                    tt = i * 2 + h
                    link.at(tt)
                    dve.wait_ge(s_o, tt + 2)
                    dve.wait_ge(s_ot, tt + 1)
                    link(dve.tensor_scalar(den[:], p_o[:, h, D:2 * D], 1e-6, None, ALU.add))
                    link(dve.reciprocal(den[:], den[:]))
                    dve.wait_ge(s_py, tt)
                    dve.tensor_tensor(o_t[:, h], p_o[:, h, 0:D], den[:], ALU.mult).then_inc(s_ot, 1)

                def total(i, h):
                    tt = i * 2 + h
                    add.at(tt)
                    dve.wait_ge(s_py, tt + 2)
                    dve.wait_ge(s_st[h], i * 16)
                    add(dve.tensor_tensor(yb[:, h], p_y[:, h, 0:D], bo[:], ALU.add))
                    dve.wait_ge(s_x[h], i * 16 + 16)
                    dve.tensor_tensor(yb[:, h], yb[:, h], xb[:, h], ALU.add).then_inc(s_y, 1)

                one_ahead(dve, ratio, total)

            @block.tensor
            def _(pe):
                pe.sem_inc(s_o, 1)
                pe.sem_inc(s_py, 1)
                pe.wait_ge(s_set, 1)
                pe.wait_ge(s_w, 32)

                def mix(i, h):
                    tt = i * 2 + h
                    pe.wait_ge(s_ot, tt)
                    for a in range(2):
                        q = q_mix[:, bass.ds(tt * D + a * P, P)]
                        pe.matmul(p_o[:, h, a * P:(a + 1) * P], kv_m[:, a], q, start=True, stop=True)
                        last = pe.matmul(p_o[:, h, D + a * P:D + (a + 1) * P], ks_m[:, a], q, start=True, stop=True)
                    last.then_inc(s_o, 1)

                def out(i, h):
                    tt = i * 2 + h
                    pe.wait_ge(s_ot, tt + 2)
                    pe.wait_ge(s_y, tt)
                    for a in range(2):
                        last = pe.matmul(p_y[:, h, 0:D], o_t[:, h, a * P:(a + 1) * P], wo[:, a],
                                         start=(a == 0), stop=(a == 1))
                    last.then_inc(s_py, 1)

                one_ahead(pe, mix, out)


def conv_tail(nc, k, w, acc, xn_dram, skip_dram, out_dram):
    H = CONV.heads
    F = D + H
    with ExitStack() as ctx:
        t = Tools(nc, "tail", ctx)
        wb = t.sb("wb", [P, 3 * D])
        g1 = t.sb("g1", [P, D])
        b1 = t.sb("b1", [P, D])
        euler = t.sb("euler", [P, 1])
        cat = t.sb("cat", [P, 2, 3, D])
        xb = t.sb("xb", [P, 2, D])
        prod = t.sb("prod", [P, 3 * D])
        den = t.sb("den", [P, H])
        z = t.sb("z", [P, 2])
        ez = t.sb("ez", [P, 1])
        res = t.sb("res", [P, D])
        yb = t.sb("yb", [P, 2, D])
        norm = Norm(k, t)
        s_w, s_dve, s_z, s_ez, s_e, s_carry, s_carry2 = (
            t.sem(x) for x in ("w", "dve", "z", "ez", "e", "carry", "carry2"))
        s_in = [t.sem(f"in{h}") for h in range(2)]
        s_st = [t.sem(f"st{h}") for h in range(2)]
        s_y = t.sem("y")
        s_sent = t.sem("sent")
        with nc.Block() as block:

            @block.sync
            def _(sp):
                load_all(sp, s_w, [(wb[:], spread(w["wbeta"])), (g1[:], spread(w["ln1_g"])),
                                   (b1[:], spread(w["ln1_b"]))])

                def load(i, h):
                    tt = i * 2 + h
                    sp.wait_ge(s_y, tt)
                    sp.sem_inc(s_carry, 1)
                    sp.dma_start(cat[:, h, 1], skip_dram[bass.ds(tt * P, P), :]).then_inc(s_in[h], 16)
                    sp.dma_start(xb[:, h], xn_dram[bass.ds(tt * P, P), :]).then_inc(s_in[h], 16)

                per_tile(sp, load)

            @block.gpsimd
            def _(pool):
                pool.memset(euler[:], 2.718281828459045).then_inc(s_e, 1)
                pool.wait_ge(s_e, 1)

                def tile(i, h):
                    tt = i * 2 + h
                    pool.wait_ge(s_z, tt + 1)
                    pool.sem_inc(s_carry2, 1)
                    pool.tensor_tensor(ez[:], euler[:], z[:, 0:1], ALU.pow).then_inc(s_ez, 1)
                    norm.power(pool, tt)

                per_tile(pool, tile)

            @block.scalar
            def _(act):
                def store(i, h):
                    tt = i * 2 + h
                    act.wait_ge(s_y, tt + 2)
                    act.sem_inc(s_sent, 1)
                    act.dma_start(out_dram[bass.ds(tt * P, P), :], yb[:, h]).then_inc(s_st[h], 16)

                per_tile(act, store)
                act.wait_ge(s_st[0], (NB + 1) // 2 * 16)
                act.wait_ge(s_st[1], NB // 2 * 16)

            @block.vector
            def _(dve):
                dve.sem_inc(s_y, 1)
                dve.wait_ge(s_w, 48)
                link = Steps(dve, s_dve, 14)

                def tile(i, h):
                    tt = i * 2 + h
                    link.at(tt)
                    o, skip, diff = (cat[:, h, c] for c in range(3))
                    link(dve.tensor_scalar(den[:], acc[:, bass.ds(tt * F + D, H)], 1e-16, None, ALU.add))
                    link(dve.reciprocal(den[:], den[:]))
                    link(dve.tensor_tensor(o.rearrange("p (h f) -> p h f", h=H),
                                           acc[:, bass.ds(tt * F, D)].rearrange("p (h f) -> p h f", h=H),
                                           den[:].unsqueeze(2).to_broadcast([P, H, D // H]), ALU.mult))
                    dve.wait_ge(s_in[h], i * 32 + 32)
                    link(dve.tensor_tensor(diff, o, skip, ALU.subtract))
                    link(dve.tensor_tensor(prod[:], cat[:, h].rearrange("p c f -> p (c f)"), wb[:], ALU.mult))
                    link(dve.tensor_reduce(z[:, 1:2], prod[:], AX, ALU.add))
                    dve.tensor_scalar(z[:, 0:1], z[:, 1:2], -1.0, None, ALU.mult).then_inc(s_z, 1)
                    link(dve.tensor_tensor(res[:], o, xb[:, h], ALU.add))
                    dve.wait_ge(s_ez, tt + 1)
                    link(dve.tensor_scalar(z[:, 1:2], ez[:], 1.0, None, ALU.add))
                    link(dve.reciprocal(z[:, 1:2], z[:, 1:2]))
                    link(dve.tensor_scalar(diff, diff, z[:, 1:2], None, ALU.mult))
                    link(dve.tensor_tensor(res[:], res[:], diff, ALU.subtract))
                    dve.wait_ge(s_st[h], i * 16)
                    norm.affine(dve, link, yb[:, h], res[:], g1[:], b1[:], tt).then_inc(s_y, 1)

                per_tile(dve, tile)


def experts(nc, k, name, units, w, x_dram, base_dram, out_dram, gates=None):
    HID = 512
    with ExitStack() as ctx:
        t = Tools(nc, name, ctx)
        w1 = t.sb("w1", [P, units, 2, HID])
        w2 = t.sb("w2", [P, units, 4, D])
        b1 = t.sb("b1", [P, units * 4])
        b2 = t.sb("b2", [P, D * (units if gates is not None else 1)])
        xb = t.sb("xb", [P, 2, D])
        yb = t.sb("yb", [P, 2, D])
        part = t.sb("part", [P, D])
        warm = t.sb("warm", [P, 1])
        xt = t.sb("xt", [P, 2, D])
        ht = t.sb("ht", [P, 2, HID])
        p_t = t.ps("p_t", [P, 2, 512])
        p_h = t.ps("p_h", [P, 2, 512])
        p_y = t.ps("p_y", [P, 2, 512])
        s_w, s_carry, s_dve, s_done = (t.sem(x) for x in ("w", "carry", "dve", "done"))
        s_x = [t.sem(f"x{h}") for h in range(2)]
        s_base = [t.sem(f"base{h}") for h in range(2)]
        s_st = [t.sem(f"st{h}") for h in range(2)]
        s_turn, s_xt, s_h, s_gelu, s_y, s_read = (
            t.sem(x) for x in ("turn", "xt", "h", "gelu", "y", "read"))
        NW = 16 * (2 * units + 2)

        def with_next(engine, tile):
            with engine.Fori(0, NB // 2) as i:
                tile(i, 0, (i, 1))
                tile(i, 1, (i + 1, 0))
            tile(NB // 2, 0, None)

        s_sent = t.sem("sent")
        with nc.Block() as block:

            @block.sync
            def _(sp):
                for u in range(units):
                    load_all(sp, s_w, [(w1[:, u], w["w1"][u].rearrange("(a p) n -> p a n", p=P)),
                                       (w2[:, u], w["w2"][u].rearrange("(c p) n -> p c n", p=P))])
                load_all(sp, s_w, [(b1[:], w["b1"].rearrange("(u p) -> p u", p=P)), (b2[:], spread(w["b2"]))])

                def load(i, h):
                    tt = i * 2 + h
                    sp.wait_ge(s_turn, tt)
                    sp.sem_inc(s_carry, 1)
                    sp.dma_start(xb[:, h], x_dram[bass.ds(tt * P, P), :]).then_inc(s_x[h], 16)
                    sp.wait_ge(s_st[h], i * 16)
                    sp.sem_inc(s_carry, 1)
                    sp.dma_start(yb[:, h], base_dram[bass.ds(tt * P, P), :]).then_inc(s_base[h], 16)

                per_tile(sp, load)

            @block.gpsimd
            def _(pool):
                def store(i, h):
                    pool.wait_ge(s_done, i * 2 + (h + 1))
                    pool.sem_inc(s_sent, 1)
                    pool.dma_start(out_dram[bass.ds((i * 2 + h) * P, P), :], yb[:, h]).then_inc(s_st[h], 16)

                per_tile(pool, store)
                pool.wait_ge(s_st[0], (NB + 1) // 2 * 16)
                pool.wait_ge(s_st[1], NB // 2 * 16)

            @block.vector
            def _(dve):
                dve.sem_inc(s_read, 1)
                dve.wait_ge(s_w, NW)
                shift = Steps(dve, s_dve, units if gates is not None else 1)

                def tile(i, h):
                    tt = i * 2 + h
                    shift.at(tt)
                    dve.wait_ge(s_base[h], i * 16 + 16)
                    for u in range(units):
                        v = tt * units + u
                        y = p_y[:, u % 2, 0:D]
                        dve.wait_ge(s_y, v + 2)
                        if gates is not None:
                            shift(dve.tensor_tensor(part[:], y, b2[:, u * D:(u + 1) * D], ALU.add))
                            last = dve.scalar_tensor_tensor(yb[:, h], part[:], gates[:, bass.ds(v, 1)],
                                                            yb[:, h], ALU.mult, ALU.add)
                        else:
                            if u == 0:
                                shift(dve.tensor_tensor(yb[:, h], yb[:, h], b2[:], ALU.add))
                            last = dve.tensor_tensor(yb[:, h], yb[:, h], y, ALU.add)
                        last.then_inc(s_read, 1)
                        dve.wait_ge(s_read, v + 2)
                    dve.sem_inc(s_done, 1)

                per_tile(dve, tile)

            @block.scalar
            def _(act):
                act.sem_inc(s_xt, 1)
                act.sem_inc(s_gelu, 1)
                act.wait_ge(s_w, NW)
                act.activation(warm[:], k["ones"][:, 0:1], ACT.Gelu)

                def copy(i, h):
                    tt = i * 2 + h
                    act.wait_ge(s_turn, tt + 2)
                    act.copy(xt[:, h], p_t[:, h, 0:D]).then_inc(s_xt, 1)

                def tile(i, h, nxt):
                    tt = i * 2 + h
                    for u in range(units):
                        v = tt * units + u
                        act.wait_ge(s_h, v + 2)
                        act.wait_ge(s_y, v)
                        for c in range(4):
                            last = act.activation(ht[:, u % 2, c * P:(c + 1) * P], p_h[:, u % 2, c * P:(c + 1) * P],
                                                  ACT.Gelu, bias=b1[:, u * 4 + c:u * 4 + c + 1])
                        last.then_inc(s_gelu, 1)
                        if u == 0 and nxt is not None:
                            copy(*nxt)

                copy(0, 0)
                with_next(act, tile)

            @block.tensor
            def _(pe):
                for s in (s_turn, s_h, s_y):
                    pe.sem_inc(s, 1)
                pe.wait_ge(s_w, NW)

                def turn(i, h):
                    tt = i * 2 + h
                    pe.wait_ge(s_x[h], i * 16 + 16)
                    pe.wait_ge(s_xt, tt)
                    for a in range(2):
                        last = pe.transpose(p_t[:, h, a * P:(a + 1) * P], xb[:, h, a * P:(a + 1) * P], k["ident"][:])
                    last.then_inc(s_turn, 1)

                def hidden(i, h, u):
                    tt = i * 2 + h
                    v = tt * units + u
                    if u == 0:
                        pe.wait_ge(s_xt, tt + 2)
                    pe.wait_ge(s_gelu, v)
                    for c in range(4):
                        for a in range(2):
                            last = pe.matmul(p_h[:, u % 2, c * P:(c + 1) * P], w1[:, u, a, c * P:(c + 1) * P],
                                             xt[:, h, a * P:(a + 1) * P], start=(a == 0), stop=(a == 1))
                    last.then_inc(s_h, 1)

                def outer(i, h, u):
                    v = (i * 2 + h) * units + u
                    pe.wait_ge(s_gelu, v + 2)
                    pe.wait_ge(s_read, v)
                    for c in range(4):
                        last = pe.matmul(p_y[:, u % 2, 0:D], ht[:, u % 2, c * P:(c + 1) * P], w2[:, u, c],
                                         start=(c == 0), stop=(c == 3))
                    last.then_inc(s_y, 1)

                def tile(i, h, nxt):
                    if nxt is not None:
                        turn(*nxt)
                    for u in range(units):
                        if u + 1 < units:
                            hidden(i, h, u + 1)
                        elif nxt is not None:
                            hidden(*nxt, 0)
                        outer(i, h, u)

                turn(0, 0)
                hidden(0, 0, 0)
                with_next(pe, tile)


class Product:

    def __init__(self, k, t):
        self.ident = k["ident"]
        self.turned = t.sb("turned", [P, 2, D])
        self.p_t = t.ps("p_t", [P, 2, 512])
        self.p_out = t.ps("p_out", [P, 2, 512])
        self.s_made, self.s_turned, self.s_copied, self.s_product, self.s_used = (
            t.sem(x) for x in ("made", "turned", "copied", "product", "used"))

    def turn(self, pe, tt, h, rows):
        pe.wait_ge(self.s_made, tt + 2)
        pe.wait_ge(self.s_copied, tt)
        for a in range(2):
            last = pe.transpose(self.p_t[:, h, a * P:(a + 1) * P], rows[:, a * P:(a + 1) * P], self.ident[:])
        last.then_inc(self.s_turned, 1)

    def copy(self, act, tt, h):
        act.wait_ge(self.s_turned, tt + 2)
        act.wait_ge(self.s_product, tt)
        act.copy(self.turned[:, h], self.p_t[:, h, 0:D]).then_inc(self.s_copied, 1)

    def multiply(self, pe, tt, h, weights):
        pe.wait_ge(self.s_copied, tt + 2)
        pe.wait_ge(self.s_used, tt)
        for first, halves in weights:
            for n, (a, wa) in enumerate(halves):
                last = pe.matmul(self.p_out[:, h, first:first + wa.shape[1]], self.turned[:, h, a * P:(a + 1) * P],
                                 wa, start=(n == 0), stop=(n == len(halves) - 1))
        last.then_inc(self.s_product, 1)


def gat_in(nc, k, w, z_dram, xm_dram, x1_dram, xl_dram, h_dram, ad3):
    with ExitStack() as ctx:
        t = Tools(nc, "gat_in", ctx)
        wg = t.sb("wg", [P, 2, 16])
        att = t.sb("att", [P, 2, 16])
        g2 = t.sb("g2", [P, D])
        b2 = t.sb("b2", [P, D])
        zb = t.sb("zb", [P, 2, D])
        xm = t.sb("xm", [P, 2, D])
        res = t.sb("res", [P, D])
        x1 = t.sb("x1", [P, 2, D])
        xl = t.sb("xl", [P, 2, D])
        hb = t.sb("hb", [P, 2, 20])
        prod = t.sb("prod", [P, 2, 16])
        score = t.sb("score", [P, 8])
        norm = Norm(k, t, 2)
        mul = Product(k, t)
        s_w, s_make, s_use, s_x1, s_carry = (t.sem(x) for x in ("w", "make", "use", "x1", "carry"))
        s_in = [t.sem(f"in{h}") for h in range(2)]
        s_st = [t.sem(f"st{h}") for h in range(2)]
        s_sth = [t.sem(f"sth{h}") for h in range(2)]
        s_sent = t.sem("sent")
        with nc.Block() as block:

            @block.sync
            def _(sp):
                load_all(sp, s_w, [(wg[:], w["w_gat"].rearrange("(a p) n -> p a n", p=P)),
                                   (att[:].rearrange("p a b -> p (a b)"), spread(w["att"])),
                                   (g2[:], spread(w["ln2_g"])), (b2[:], spread(w["ln2_b"]))])

                def load(i, h):
                    tt = i * 2 + h
                    sp.wait_ge(mul.s_made, tt)
                    sp.sem_inc(s_carry, 1)
                    sp.dma_start(zb[:, h], z_dram[bass.ds(tt * P, P), :]).then_inc(s_in[h], 16)
                    sp.dma_start(xm[:, h], xm_dram[bass.ds(tt * P, P), :]).then_inc(s_in[h], 16)

                per_tile(sp, load)

            @block.gpsimd
            def _(pool):
                def powers(i, h):
                    norm.power(pool, i * 2 + h, 0)
                    norm.power(pool, i * 2 + h, 1)

                per_tile(pool, powers)

            @block.vector
            def _(dve):
                dve.sem_inc(mul.s_made, 1)
                dve.sem_inc(mul.s_used, 1)
                dve.wait_ge(s_w, 64)
                make, use = Steps(dve, s_make, 7), Steps(dve, s_use, 8)

                def rows(i, h):
                    tt = i * 2 + h
                    make.at(tt)
                    dve.wait_ge(s_in[h], i * 32 + 32)
                    dve.wait_ge(s_st[h], i * 32)
                    dve.wait_ge(mul.s_turned, tt)
                    make(norm.affine(dve, make, res[:], zb[:, h], g2[:], b2[:], tt, 0))
                    make(dve.tensor_tensor(x1[:, h], res[:], xm[:, h], ALU.add))
                    norm(dve, make, xl[:, h], x1[:, h], tt, 1).then_inc(mul.s_made, 1)

                def heads(i, h):
                    tt = i * 2 + h
                    use.at(tt)
                    dve.wait_ge(mul.s_product, tt + 2)
                    dve.wait_ge(s_sth[h], i * 16)
                    use(dve.tensor_copy(hb[:, h, 0:16], mul.p_out[:, h, 0:16]))
                    use(dve.tensor_tensor(prod[:], hb[:, h, 0:16].unsqueeze(1).to_broadcast([P, 2, 16]),
                                          att[:], ALU.mult))
                    use(dve.tensor_reduce(score[:], prod[:].rearrange("p a (h e) -> p (a h) e", e=4), AX, ALU.add))
                    for part in range(3):
                        out = ad3[:, bass.ds(tt * 12 + part * 4, 4)]
                        use(dve.tensor_copy(out, score[:, 4:8]))
                        if part < 2:
                            use(dve.tensor_tensor(score[:, 4:8], score[:, 4:8], out, ALU.subtract))
                    dve.tensor_copy(hb[:, h, 16:20], score[:, 0:4]).then_inc(mul.s_used, 1)

                one_ahead(dve, rows, heads)

            @block.scalar
            def _(act):
                act.sem_inc(mul.s_copied, 1)
                def store(i, h):
                    tt = i * 2 + h
                    act.wait_ge(mul.s_made, tt + 2)
                    act.sem_inc(s_sent, 1)
                    act.dma_start(x1_dram[bass.ds(tt * P, P), :], x1[:, h]).then_inc(s_st[h], 16)
                    act.dma_start(xl_dram[bass.ds(tt * P, P), :], xl[:, h]).then_inc(s_st[h], 16)
                    mul.copy(act, tt, h)

                def store_heads(i, h):
                    tt = i * 2 + h
                    act.wait_ge(mul.s_used, tt + 2)
                    act.sem_inc(s_sent, 1)
                    act.dma_start(h_dram[bass.ds(tt * P, P), :], hb[:, h]).then_inc(s_sth[h], 16)

                one_ahead(act, store, store_heads)
                for h, n in ((0, (NB + 1) // 2), (1, NB // 2)):
                    act.wait_ge(s_st[h], n * 32)
                    act.wait_ge(s_sth[h], n * 16)

            @block.tensor
            def _(pe):
                pe.sem_inc(mul.s_turned, 1)
                pe.sem_inc(mul.s_product, 1)
                pe.wait_ge(s_w, 64)
                def tile(i, h):
                    mul.turn(pe, i * 2 + h, h, xl[:, h])
                    mul.multiply(pe, i * 2 + h, h, [(0, [(a, wg[:, a]) for a in range(2)])])

                per_tile(pe, tile)


def load_meta(nc, L, sorted_rows, ids, index):
    G, GA = L.groups, L.all_groups
    with ExitStack() as ctx:
        t = Tools(nc, f"meta_{L.name}", ctx)
        meta = t.sb("meta", [P, G * 2, 4], I32)
        s_in, s_out = t.sem("in"), t.sem("out")
        CUT = 8
        with nc.Block() as block:

            @block.sync
            def _(sp):
                view = sorted_rows.rearrange("(g p j) w -> p g (j w)", p=P, j=2)
                for c in range(CUT):
                    g0, g1 = G * c // CUT, G * (c + 1) // CUT
                    sp.dma_start(meta[:, 2 * g0:2 * g1].rearrange("p (g j) w -> p g (j w)", j=2), view[:, g0:g1]
                                 ).then_inc(s_in, 16)

            @block.vector
            def _(dve):
                if G < GA and ids.shape[1] > G * 4:
                    dve.memset(ids[:, G * 4:], -1.0)
                dve.wait_ge(s_in, 16 * CUT)
                dve.tensor_copy(ids[:, 0:G * 4].rearrange("p (c w) -> p c w", w=2), meta[:, :, 1:3])
                dve.tensor_copy(index[:], meta[:, :, 0]).then_inc(s_out, 1)
                dve.wait_ge(s_out, 1)


class GatScores:
    R, AHEAD = 8, 7

    def __init__(self, k, t, table, h_dram, ad3, alpha, ids, index, values):
        self.k, self.table, self.h_dram, self.ad3, self.alpha, self.ids, self.index, self.values = (
            k, table, h_dram, ad3, alpha, ids, index, values)
        R = self.R
        self.hot = t.sb("hot", [P, R, 2, P], BF16)
        self.hot_t = t.sb("hot_t", [P, R, 2 * P], BF16)
        self.idx = t.sb("idx", [P, R, 2], I32)
        self.got = t.sb("got", [P, R, 2, 20])
        self.total = t.sb("total", [P, 2, 2, GAT.heads])
        self.ident_bf = t.sb("ident_bf", [P, P], BF16)
        self.p_ht = t.ps("p_ht", [P, 2, 1024], BF16)
        self.p_a = t.ps("p_a", [P, 2, 512])
        self.s_id, self.s_go = t.sem("id"), t.sem("go")
        self.s_got = [t.sem(f"got{r}") for r in range(R)]
        self.s_hot, self.s_turn, self.s_cat, self.s_q, self.s_sum, self.s_alpha = (
            t.sem(x) for x in ("hot", "turn", "cat", "q", "sum", "alpha"))
        self.blocks = None

    def first_codes(self, dve):
        for s in (self.s_hot, self.s_sum, self.s_alpha):
            dve.sem_inc(s, self.AHEAD)
        dve.tensor_copy(self.ident_bf[:], self.k["ident"][:]).then_inc(self.s_id, 1)
        if GAT.groups < GAT.all_groups:
            dve.memset(self.alpha[:, GAT.groups * 2 * GAT.heads:], 0.0)

    def codes(self, dve, g, i, r):
        dve.wait_ge(self.s_alpha, g)
        dve.wait_ge(self.s_turn, g)
        dve.tensor_copy(self.idx[:, r], self.index[:, bass.ds(g * 2, 2)])
        dve.tensor_tensor(self.hot[:, r], self.k["iota_row"][:].unsqueeze(1).to_broadcast([P, 2, P]),
                          self.ids[:, bass.ds(g * 4, 4)].rearrange("p (j w) -> p j w", w=2)[:, :, 1:2]
                          .to_broadcast([P, 2, P]), ALU.is_equal).then_inc(self.s_hot, 1)

    def scores(self, dve, g, i, r):
        H = GAT.heads
        dve.wait_ge(self.s_got[r], i * 32 + 32)
        dve.wait_ge(self.s_q, g + self.AHEAD + 1)
        dve.wait_ge(self.s_alpha, g + (self.AHEAD - 1))
        dve.tensor_copy(self.values[:, bass.ds(g * 32, 32)].rearrange("p (j f) -> p j f", j=2),
                        self.got[:, r, :, 0:16])
        dve.tensor_tensor(self.total[:, r % 2], self.got[:, r, :, 16:20],
                          self.p_a[:, r % 2, 0:2 * H].rearrange("p (j h) -> p j h", j=2), ALU.add
                          ).then_inc(self.s_sum, 1)
        dve.wait_ge(self.s_sum, g + self.AHEAD + 1)
        a = self.alpha[:, bass.ds(g * 2 * H, 2 * H)].rearrange("p (j h) -> p j h", j=2)
        dve.scalar_tensor_tensor(a, self.total[:, r % 2], 0.2, self.total[:, r % 2], ALU.mult, ALU.max
                                 ).then_inc(self.s_alpha, 1)

    def turned(self, act, g, i, r):
        act.wait_ge(self.s_turn, g + self.AHEAD + 1)
        act.wait_ge(self.s_q, g)
        act.copy(self.hot_t[:, r], self.p_ht[:, r % 2, 0:2 * P]).then_inc(self.s_cat, 1)

    def gpsimd(self, pool):
        with pool.Fori(0, GAT.groups // self.R) as i:
            for r in range(self.R):
                pool.wait_ge(self.s_hot, i * self.R + (r + self.AHEAD + 1))
                pool.sem_inc(self.s_go, 1)
                for j in range(2):
                    pool.indirect_dma_start(
                        out=self.got[:, r, j], out_offset=None, in_=self.h_dram,
                        in_offset=bass.IndirectOffsetOnAxis(ap=self.idx[:, r, j:j + 1], axis=0),
                        ).then_inc(self.s_got[r], 16)

    def first_product(self, pe):
        pe.sem_inc(self.s_turn, self.AHEAD)
        pe.sem_inc(self.s_q, self.AHEAD)
        pe.wait_ge(self.s_id, 1)

    def turn(self, pe, g, i, r):
        pe.wait_ge(self.s_hot, g + self.AHEAD + 1)
        pe.wait_ge(self.s_cat, g + (self.AHEAD - 1))
        for j in range(2):
            last = pe.transpose(self.p_ht[:, r % 2, j * P:(j + 1) * P], self.hot[:, r, j], self.ident_bf[:])
        last.then_inc(self.s_turn, 1)

    def load_blocks(self, pe, i):
        self.blocks = block_numbers(pe, self.table, i)

    def product(self, pe, g, i, r):
        H = GAT.heads
        pe.wait_ge(self.s_cat, g + self.AHEAD + 1)
        pe.wait_ge(self.s_sum, g + (self.AHEAD - 1))
        for j in range(2):
            for part in range(3):
                last = pe.matmul(self.p_a[:, r % 2, j * H:(j + 1) * H], self.hot_t[:, r, j * P:(j + 1) * P],
                                 self.ad3[:, bass.ds(self.blocks[r] * (3 * H) + part * H, H)],
                                 start=(part == 0), stop=(part == 2))
        last.then_inc(self.s_q, 1)


def pick_two(nc, k, name, E, scores, gates):
    NE = NB * E
    with ExitStack() as ctx:
        t = Tools(nc, name, ctx)
        col_i = t.sb("col_i", [P, 2, E, E], I32)
        col = t.sb("col", [P, 2, E, E])
        lower = t.sb("lower", [P, E, E])
        more = t.sb("more", [P, NB, E, E])
        same = t.sb("same", [P, NB, E, E])
        rank = t.sb("rank", [P, NE])
        is_it = t.sb("is_it", [P, 2, NE])
        part = t.sb("part", [P, 2, NE])
        top = t.sb("top", [P, 2, NB])
        gap = t.sb("gap", [P, NB])
        weight = t.sb("weight", [P, 2, NB])
        s_i, s_dve, s_gap, s_exp = (t.sem(x) for x in ("i", "dve", "gap", "exp"))
        with nc.Block() as block:

            @block.gpsimd
            def _(pool):
                pool.iota(col_i[:, 0], pattern=[[1, E], [0, E]], base=0, channel_multiplier=0).then_inc(s_i, 1)
                pool.iota(col_i[:, 1], pattern=[[0, E], [1, E]], base=0, channel_multiplier=0).then_inc(s_i, 1)

            @block.vector
            def _(dve):
                link = Chain(dve, s_dve)
                by = lambda x: x.rearrange("p (b e) -> p b e", e=E)
                mine = by(scores[:]).unsqueeze(3).to_broadcast([P, NB, E, E])
                other = by(scores[:]).unsqueeze(2).to_broadcast([P, NB, E, E])
                dve.wait_ge(s_i, 2)
                link(dve.tensor_copy(col[:], col_i[:]))
                link(dve.tensor_tensor(lower[:], col[:, 1], col[:, 0], ALU.is_lt))
                link(dve.tensor_tensor(more[:], other, mine, ALU.is_gt))
                link(dve.tensor_tensor(same[:], other, mine, ALU.is_equal))
                link(dve.tensor_tensor(same[:], same[:], lower[:].unsqueeze(1).to_broadcast([P, NB, E, E]), ALU.mult))
                link(dve.tensor_tensor(more[:], more[:], same[:], ALU.add))
                link(dve.tensor_reduce(rank[:], more[:].rearrange("p b e f -> p (b e) f"), AX, ALU.add))
                for n in range(2):
                    link(dve.tensor_scalar(is_it[:, n], rank[:], float(n), None, ALU.is_equal))
                    link(dve.tensor_tensor(part[:, n], is_it[:, n], scores[:], ALU.mult))
                    link(dve.tensor_reduce(top[:, n], by(part[:, n]), AX, ALU.add))
                dve.tensor_tensor(gap[:], top[:, 1], top[:, 0], ALU.subtract).then_inc(s_gap, 1)
                dve.wait_ge(s_exp, 1)
                link(dve.tensor_scalar(top[:, 0], weight[:, 1], 1.0, None, ALU.add))
                link(dve.reciprocal(weight[:, 0], top[:, 0]))
                link(dve.tensor_tensor(weight[:, 1], weight[:, 1], weight[:, 0], ALU.mult))
                for n in range(2):
                    link(dve.tensor_tensor(by(part[:, n]), by(is_it[:, n]),
                                           weight[:, n].unsqueeze(2).to_broadcast([P, NB, E]), ALU.mult))
                link(dve.tensor_tensor(gates[:], part[:, 0], part[:, 1], ALU.add))

            @block.scalar
            def _(act):
                act.wait_ge(s_gap, 1)
                act.activation(weight[:, 1], gap[:], ACT.Exp).then_inc(s_exp, 1)


def gat_gates(nc, k, w, acc, scores):
    with ExitStack() as ctx:
        t = Tools(nc, "gat_ln", ctx)
        bias = t.sb("bias", [P, 3, 16])
        den = t.sb("den", [P, NB, 4])
        agg = t.sb("agg", [P, NB, 16])
        sq = t.sb("sq", [P, NB, 16])
        mean = t.sb("mean", [P, NB])
        var = t.sb("var", [P, NB])
        half = t.sb("half", [P, NB])
        rstd = t.sb("rstd", [P, NB])
        s_w, s_dve, s_var, s_rstd = (t.sem(x) for x in ("w", "dve", "var", "rstd"))
        with nc.Block() as block:

            @block.sync
            def _(sp):
                load_all(sp, s_w, [(bias[:].rearrange("p a b -> p (a b)"), spread(w["gat_ln"]))])

            @block.gpsimd
            def _(pool):
                pool.wait_ge(s_var, 1)
                pool.tensor_tensor(rstd[:], var[:], half[:], ALU.pow).then_inc(s_rstd, 1)

            @block.vector
            def _(dve):
                link = Chain(dve, s_dve)
                wide = lambda x: x.unsqueeze(2).to_broadcast([P, NB, 16])
                each = lambda n: bias[:, n].unsqueeze(1).to_broadcast([P, NB, 16])
                a = acc[:].rearrange("p (b f) -> p b f", f=20)
                dve.wait_ge(s_w, 16)
                link(dve.memset(half[:], -0.5))
                link(dve.tensor_scalar(den[:], a[:, :, 16:20], 1e-16, None, ALU.add))
                link(dve.reciprocal(den[:], den[:]))
                link(dve.tensor_tensor(agg[:].rearrange("p b (h e) -> p b h e", e=4),
                                       a[:, :, 0:16].rearrange("p b (h e) -> p b h e", e=4),
                                       den[:].unsqueeze(3).to_broadcast([P, NB, 4, 4]), ALU.mult))
                link(dve.tensor_tensor(agg[:], agg[:], each(0), ALU.add))
                link(dve.tensor_reduce(mean[:], agg[:], AX, ALU.add))
                link(dve.tensor_scalar(mean[:], mean[:], 1.0 / 16, None, ALU.mult))
                link(dve.tensor_tensor(agg[:], agg[:], wide(mean[:]), ALU.subtract))
                link(dve.tensor_tensor(sq[:], agg[:], agg[:], ALU.mult))
                link(dve.tensor_reduce(var[:], sq[:], AX, ALU.add))
                dve.tensor_scalar(var[:], var[:], 1.0 / 16, 1e-5, ALU.mult, ALU.add).then_inc(s_var, 1)
                dve.wait_ge(s_rstd, 1)
                link(dve.tensor_tensor(agg[:], agg[:], wide(rstd[:]), ALU.mult))
                link(dve.tensor_tensor(agg[:], agg[:], each(1), ALU.mult))
                link(dve.tensor_tensor(agg[:], agg[:], each(2), ALU.add))
                link(dve.tensor_reduce(scores[:].rearrange("p (b e) -> p b e", e=4),
                                       agg[:].rearrange("p b (h e) -> p b e h", e=4), AX, ALU.add))
                link(dve.tensor_scalar(scores[:], scores[:], 0.25, None, ALU.mult))


def l1_in(nc, k, w, x_dram, xn_dram, parts, kv):
    H, C = 8, D // 8
    with ExitStack() as ctx:
        t = Tools(nc, "l1_in", ctx)
        w1 = t.sb("w1", [P, 2, D])
        affine = t.sb("affine", [P, 4, D])
        xb = t.sb("xb", [P, 2, D])
        xn = t.sb("xn", [P, 2, D])
        xt = t.sb("xt", [P, D])
        mean = t.sb("mean", [P, H])
        dev = t.sb("dev", [P, D])
        sq = t.sb("sq", [P, D])
        var = t.sb("var", [P, H])
        std = t.sb("std", [P, H])
        half = t.sb("half", [P, H])
        zero = t.sb("zero", [P, D])
        kk = t.sb("kk", [P, 2, D])
        vv = t.sb("vv", [P, 2, D])
        norm = Norm(k, t)
        mul = Product(k, t)
        p_kv = t.ps("p_kv", [P, 512])
        s_w, s_make, s_use, s_var, s_std, s_carry, s_carry2, s_one = (
            t.sem(x) for x in ("w", "make", "use", "var", "std", "carry", "carry2", "one"))
        s_in = [t.sem(f"in{h}") for h in range(2)]
        s_st = [t.sem(f"st{h}") for h in range(2)]
        s_kv, s_sum = t.sem("kv"), t.sem("sum")
        s_sent = t.sem("sent")
        with nc.Block() as block:

            @block.sync
            def _(sp):
                load_all(sp, s_w, [(w1[:], w["gnn_w1"].rearrange("(a p) n -> p a n", p=P)),
                                   (affine[:].rearrange("p a b -> p (a b)"), spread(w["kvln"]))])

                def load(i, h):
                    tt = i * 2 + h
                    sp.wait_ge(mul.s_made, tt)
                    sp.sem_inc(s_carry, 1)
                    sp.dma_start(xb[:, h], x_dram[bass.ds(tt * P, P), :]).then_inc(s_in[h], 16)

                per_tile(sp, load)

            @block.gpsimd
            def _(pool):
                def rows(i, h):
                    tt = i * 2 + h
                    norm.power(pool, tt)

                def heads(i, h):
                    tt = i * 2 + h
                    pool.wait_ge(s_var, tt + 1)
                    pool.sem_inc(s_carry2, 1)
                    pool.tensor_tensor(std[:], var[:], half[:], ALU.pow).then_inc(s_std, 1)

                one_ahead(pool, rows, heads)

            @block.vector
            def _(dve):
                dve.sem_inc(mul.s_made, 1)
                dve.sem_inc(mul.s_used, 1)
                dve.sem_inc(s_kv, 1)
                dve.memset(zero[:], 0.0)
                dve.memset(half[:], 0.5).then_inc(s_one, 1)
                dve.wait_ge(s_w, 32)
                dve.wait_ge(s_one, 1)
                make, use = Steps(dve, s_make, 2), Steps(dve, s_use, 14)
                by = lambda x: x.rearrange("p (h c) -> p h c", h=H)
                wide = lambda x: x.unsqueeze(2).to_broadcast([P, H, C])

                def rows(i, h):
                    tt = i * 2 + h
                    make.at(tt)
                    dve.wait_ge(s_in[h], i * 16 + 16)
                    dve.wait_ge(s_st[h], i * 16)
                    dve.wait_ge(mul.s_turned, tt)
                    norm(dve, make, xn[:, h], xb[:, h], tt).then_inc(mul.s_made, 1)

                def heads(i, h):
                    tt = i * 2 + h
                    use.at(tt)
                    dve.wait_ge(mul.s_made, tt + 2)
                    dve.wait_ge(s_kv, tt + 1)
                    dve.wait_ge(mul.s_used, tt + 1)
                    use(dve.tensor_reduce(mean[:], by(xn[:, h]), AX, ALU.add))
                    use(dve.tensor_scalar(mean[:], mean[:], 1.0 / C, None, ALU.mult))
                    use(dve.tensor_tensor(by(dev[:]), by(xn[:, h]), wide(mean[:]), ALU.subtract))
                    use(dve.tensor_tensor(sq[:], dev[:], dev[:], ALU.mult))
                    use(dve.tensor_reduce(var[:], by(sq[:]), AX, ALU.add))
                    dve.tensor_scalar(var[:], var[:], 1.0 / (C - 1), None, ALU.mult).then_inc(s_var, 1)
                    dve.wait_ge(mul.s_product, tt + 2)
                    use(dve.tensor_copy(xt[:], mul.p_out[:, h, 0:D]))
                    split_parts(dve, use, parts, tt, xt[:]).then_inc(mul.s_used, 1)
                    dve.wait_ge(s_std, tt + 1)
                    use(dve.tensor_scalar(mean[:], std[:], 1e-5, None, ALU.add))
                    use(dve.reciprocal(mean[:], mean[:]))
                    use(dve.tensor_tensor(by(dev[:]), by(dev[:]), wide(mean[:]), ALU.mult))
                    dve.wait_ge(s_sum, tt)
                    dve.tensor_tensor(kk[:, h], dev[:], affine[:, 0], ALU.mult)
                    use(dve.tensor_tensor(vv[:, h], dev[:], affine[:, 2], ALU.mult))
                    dve.tensor_tensor(vv[:, h], vv[:, h], affine[:, 3], ALU.add)
                    if isinstance(i, int):
                        dve.tensor_tensor(kk[:, h], kk[:, h], affine[:, 1], ALU.add).then_inc(s_one, 1)
                        dve.wait_ge(s_one, 2)
                        dve.tensor_scalar(kk[:, h], kk[:, h], k["exists"][:, NB - 1:NB], None, ALU.mult
                                          ).then_inc(s_kv, 1)
                    else:
                        dve.tensor_tensor(kk[:, h], kk[:, h], affine[:, 1], ALU.add).then_inc(s_kv, 1)

                one_ahead(dve, rows, heads)
                dve.wait_ge(s_sum, NB + 1)
                for a in range(2):
                    last = dve.scalar_tensor_tensor(kv[:, a], p_kv[:, a * P:(a + 1) * P], 1.0 / N,
                                                    k["same_head"][:], ALU.mult, ALU.mult)
                last.then_inc(s_one, 1)
                dve.wait_ge(s_one, 3)

            @block.scalar
            def _(act):
                act.sem_inc(mul.s_copied, 1)
                def store(i, h):
                    tt = i * 2 + h
                    act.wait_ge(mul.s_made, tt + 2)
                    act.sem_inc(s_sent, 1)
                    act.dma_start(xn_dram[bass.ds(tt * P, P), :], xn[:, h]).then_inc(s_st[h], 16)

                def tile(i, h):
                    store(i, h)
                    mul.copy(act, i * 2 + h, h)

                per_tile(act, tile)
                for h, n in ((0, (NB + 1) // 2), (1, NB // 2)):
                    act.wait_ge(s_st[h], n * 16)

            @block.tensor
            def _(pe):
                for s in (mul.s_turned, mul.s_product, s_sum):
                    pe.sem_inc(s, 1)
                pe.wait_ge(s_w, 32)
                pe.wait_ge(s_one, 1)
                pe.matmul(p_kv[:, 0:D], k["ident"][:], zero[:], start=True, stop=False, skip_group_check=True)

                def products(i, h):
                    tt = i * 2 + h
                    mul.turn(pe, tt, h, xn[:, h])
                    mul.multiply(pe, tt, h, [(0, [(a, w1[:, a]) for a in range(2)])])

                def sums(i, h):
                    tt = i * 2 + h
                    pe.wait_ge(s_kv, tt + 2)
                    for a in range(2):
                        last = pe.matmul(p_kv[:, a * P:(a + 1) * P], kk[:, h, a * P:(a + 1) * P],
                                         vv[:, h, a * P:(a + 1) * P], start=False, stop=False,
                                         skip_group_check=True)
                    last.then_inc(s_sum, 1)

                one_ahead(pe, products, sums)


def guarded(engine, flag):
    if flag is None:
        return nullcontext()
    return engine.If(engine.value_load(flag[0:1, 0:1], min_val=0, max_val=1) == 1)


class PlacingBeside:

    def __init__(self, placing):
        self.p = placing
        assert placing.steps == 2 * TURNS

    def start(self, kind, engine):
        {"dve": self.p.first_codes, "act": self.p.first_snapshot, "pe": self.p.first_product}[kind](engine)

    def pieces(self, kind, engine, i, q, edge):
        p, step, h = self.p, i * 2 + q // 2, q % 2
        if kind == "pe":
            return [lambda j=j: p.look_up(engine, step, h, j) for j in range(UN)]
        if kind == "act":
            return ([lambda j=j: p.snapshot(engine, step, h, j) for j in range(UN)] +
                    [lambda: p.copy_meta(engine, step, h)])
        out = []
        if not (edge == "first" and q == 0):
            out.append(lambda: p.find(engine, step - (1 - h), 1 - h))
        if not (edge == "last" and q == 3):
            out.append(lambda: p.codes(engine, step + h, 1 - h))
        return out

    def finish(self, kind, engine):
        if kind == "dve":
            self.p.find(engine, self.p.steps - 1, 1)

    def sync(self, sp):
        self.p.sync(sp)

    def gpsimd(self, pool):
        self.p.gpsimd(pool)


class ScoresBeside:

    def __init__(self, scores):
        self.s = scores
        self.left = GAT.groups - TURNS * 2 * scores.R
        assert 0 < self.left <= scores.R

    def stages(self, kind, engine):
        s = self.s
        return {"dve": ((7, s.codes), (0, s.scores)), "act": ((1, s.turned),),
                "pe": ((3, s.turn), (1, s.product))}[kind]

    def start(self, kind, engine):
        if kind == "dve":
            self.s.first_codes(engine)
        elif kind == "pe":
            self.s.first_product(engine)
            self.s.load_blocks(engine, 0)
        else:
            engine.sem_inc(self.s.s_cat, self.s.AHEAD)
        for lead, body in self.stages(kind, engine):
            for g in range(lead):
                body(engine, g, 0, g)

    def sync(self, sp):
        pass

    def gpsimd(self, pool):
        self.s.gpsimd(pool)

    def group(self, kind, engine, i, x):
        R = self.s.R
        if kind == "pe" and (x == 0 or (x + 1) % R == 0):
            self.s.load_blocks(engine, i * 2 + (x + 1) // R)
        for lead, body in self.stages(kind, engine):
            y = x + lead
            body(engine, i * (2 * R) + y, i * 2 + y // R, y % R)

    def pieces(self, kind, engine, i, q, edge):
        return [lambda x=x: self.group(kind, engine, i, 4 * q + x) for x in range(4)]

    def finish(self, kind, engine):
        R = self.s.R
        for g in range(GAT.groups - self.left, GAT.groups):
            for lead, body in self.stages(kind, engine):
                if g + lead < GAT.groups:
                    body(engine, g + lead, (g + lead) // R, (g + lead) % R)


TURNS = CONV.groups // 24
assert CONV.groups == TURNS * 24


def count_matrix(nc, k, phase, table, ids, index, by_target, by_source, s0, s1, rest=None, beside=None):
    G, C, WIDE = CONV.groups, 8 if rest is None else 4, (s1 - s0) * P
    with ExitStack() as ctx:
        t = Tools(nc, phase, ctx)
        number = t.sb("number", [P, WIDE], mybir.dt.int16)
        key = t.sb("key", [P, G * 2], I32)
        hot_to = t.sb("hot_to", [P, C, P], BF16)
        hot_from = t.sb("hot_from", [P, C, WIDE], BF16)
        counts = t.sb("counts", [P, WIDE], BF16)
        turned = t.sb("turned", [P, WIDE], BF16)
        ident_bf = t.sb("ident_bf", [P, P], BF16)
        minus = t.sb("minus", [P, P], BF16)
        zero = t.sb("zero", [P, 512], BF16)
        banks = [(c, min(WIDE, c + 512)) for c in range(0, WIDE, 512)]
        NBANK = len(banks)
        p_cnt = t.ps("p_cnt", [P, NBANK * 512])
        p_t = t.ps("p_t", [P, 1024], BF16)
        s_set, s_full, s_hi, s_sub, s_out, s_turn, s_back = (
            t.sem(x) for x in ("set", "full", "hi", "sub", "out", "turn", "back"))
        s_hot, s_used = t.sem("hot"), t.sem("used")
        s_st, s_carry = t.sem("st"), t.sem("carry")
        batches = [(a, min(s1 - s0, a + 8)) for a in range(0, s1 - s0, 8)]
        NBAT = len(batches)
        after = {min(NBANK - 1, (a1 * P - 1) // 512): q for q, (a0, a1) in enumerate(batches)}
        with ExitStack() as early:
            e = Tools(nc, phase + "_set", early)
            number_i = e.sb("number_i", [P, WIDE], I32)
            with nc.Block() as block:

                @block.gpsimd
                def _(pool):
                    pool.iota(number_i[:], pattern=[[1, WIDE]], base=0x4000 + s0 * P, channel_multiplier=0
                              ).then_inc(s_set, 1)

                @block.vector
                def _(dve):
                    dve.wait_ge(s_set, 1)
                    dve.tensor_copy(number[:], number_i[:])
                    dve.memset(zero[:], 0.0)
                    dve.tensor_copy(ident_bf[:], k["ident"][:])
                    dve.tensor_scalar(minus[:], k["ident"][:], -1.0, None, ALU.mult)
                    dve.tensor_scalar(key[:], index[:], float(0x4000), None, ALU.add).then_inc(s_set, 1)
                    dve.wait_ge(s_set, 2)
                    dve.tensor_scalar(key[:], key[:], 16, None, ALU.logical_shift_left).then_inc(s_set, 1)
                    dve.wait_ge(s_set, 3)

        def turns(kind, engine, group, head=None):
            def turn(i, edge):
                if head:
                    head(i)
                for q in range(4):
                    pieces = beside.pieces(kind, engine, i, q, edge) if beside else []
                    for x in range(6):
                        group(i, 6 * q + x)
                        for piece in pieces[x * len(pieces) // 6:(x + 1) * len(pieces) // 6]:
                            piece()

            if beside:
                beside.start(kind, engine)
            turn(0, "first")
            with engine.Fori(1, TURNS - 1) as i:
                turn(i, None)
            turn(TURNS - 1, "last")
            if beside:
                beside.finish(kind, engine)

        with nc.Block() as block:

            if beside:
                @block.sync
                def _(sp):
                    beside.sync(sp)

                @block.gpsimd
                def _(pool):
                    beside.gpsimd(pool)

            @block.vector
            def _(dve):
                def codes(i, x):
                    for j in range(2):
                        chunk, c = i * 48 + (2 * x + j), (2 * x + j) % C
                        dve.wait_ge(s_used, chunk)
                        dve.tensor_scalar(hot_to[:, c], k["iota_bf"][:], ids[:, bass.ds(chunk * 2 + 1, 1)],
                                          None, ALU.is_equal)
                        dve.tensor_scalar(hot_from[:, c], number[:].bitcast(BF16),
                                          key[:, bass.ds(chunk, 1)].bitcast(F32), None, ALU.is_equal
                                          ).then_inc(s_hot, 1)

                with guarded(dve, rest):
                    turns("dve", dve, codes)

            @block.scalar
            def _(act):
                words = []

                def head(i):
                    words[:] = [bit for n in range(3) for bit in last_groups(act, table, i * 3 + n)]

                def store(i, x):
                    with act.If(words[x] == 1):
                        b = block_of_group(act, table, i * 24 + x)
                        act.wait_ge(s_full, b + 1)
                        act.wait_ge(s_st, b * 32)
                        for n, (c0, c1) in enumerate(banks):
                            if rest is not None:
                                act.copy(counts[:, c0:c1], p_cnt[:, c0:c1]).then_inc(s_hi, 1)
                                act.wait_ge(s_sub, b * NBANK + (n + 1))
                            act.copy(counts[:, c0:c1], p_cnt[:, c0:c1]).then_inc(s_out, 1)
                            if n in after:
                                a0, a1 = batches[after[n]]
                                act.wait_ge(s_turn, b * NBAT + (after[n] + 1))
                                act.copy(turned[:, a0 * P:a1 * P], p_t[:, 0:(a1 - a0) * P]).then_inc(s_back, 1)
                        act.wait_ge(s_back, b * NBAT + NBAT)
                        act.wait_ge(s_out, b * NBANK + NBANK)
                        act.sem_inc(s_carry, 1)
                        act.dma_start(by_target[bass.ds(b, 1)].squeeze(0)[:, s0 * P:s1 * P], counts[:]
                                      ).then_inc(s_st, 16)
                        act.dma_start(by_source[bass.ds(b, 1)].squeeze(0)[:, s0 * P:s1 * P], turned[:]
                                      ).then_inc(s_st, 16)

                act.copy(counts[:, 0:P], k["iota_bf"][:]).then_inc(s_carry, 1)
                act.wait_ge(s_carry, 1)
                with guarded(act, rest):
                    turns("act", act, store, head)
                    act.wait_ge(s_st, NB * 32)

            @block.tensor
            def _(pe):
                words = []

                def clear(n):
                    c0, c1 = banks[n]
                    pe.matmul(p_cnt[:, c0:c1], zero[:, 0:P], zero[:, 0:c1 - c0], start=True, stop=False,
                              skip_group_check=True)

                def head(i):
                    words[:] = [bit for n in range(3) for bit in last_groups(pe, table, i * 3 + n)]

                def count(i, x):
                    for j in range(2):
                        chunk, c = i * 48 + (2 * x + j), (2 * x + j) % C
                        pe.wait_ge(s_hot, chunk + 1)
                        for c0, c1 in banks:
                            last = pe.matmul(p_cnt[:, c0:c1], hot_to[:, c], hot_from[:, c, c0:c1],
                                             start=False, stop=False, skip_group_check=True)
                        last.then_inc(s_used, 1)
                    with pe.If(words[x] == 1):
                        b = block_of_group(pe, table, i * 24 + x)
                        pe.matmul(p_cnt[:, 0:1], zero[:, 0:P], zero[:, 0:1], start=False, stop=False,
                                  skip_group_check=True).then_inc(s_full, 1)
                        for n, (c0, c1) in enumerate(banks):
                            if rest is not None:
                                pe.wait_ge(s_hi, b * NBANK + (n + 1))
                                pe.matmul(p_cnt[:, c0:c1], minus[:], counts[:, c0:c1], start=False,
                                          stop=False, skip_group_check=True).then_inc(s_sub, 1)
                            pe.wait_ge(s_out, b * NBANK + (n + 1))
                            clear(n)
                            if n in after:
                                q = after[n]
                                a0, a1 = batches[q]
                                pe.wait_ge(s_back, b * NBAT + q)
                                for a in range(a0, a1):
                                    turn = pe.transpose(p_t[:, (a - a0) * P:(a - a0 + 1) * P],
                                                        counts[:, a * P:(a + 1) * P], ident_bf[:])
                                turn.then_inc(s_turn, 1)

                with guarded(pe, rest):
                    pe.sem_inc(s_used, C - 1)
                    for n in range(NBANK):
                        clear(n)
                    turns("pe", pe, count, head)


def rounded_counts(nc, k, biggest, flag):
    with ExitStack() as ctx:
        t = Tools(nc, "rounded", ctx)
        most = t.sb("most", [P, 1])
        row = t.sb("row", [1, 2])
        p_row = t.ps("p_row", [P, 512])
        s_dve, s_turn = t.sem("dve"), t.sem("turn")
        with nc.Block() as block:

            @block.vector
            def _(dve):
                link = Chain(dve, s_dve)
                link(dve.tensor_reduce(most[:], biggest[:], AX, ALU.max))
                dve.wait_ge(s_turn, 1)
                link(dve.tensor_reduce(row[:, 0:1], p_row[0:1, 0:P], AX, ALU.max))
                link(dve.tensor_scalar(row[:, 1:2], row[:, 0:1], 256.0, None, ALU.is_ge))
                link(dve.tensor_copy(flag[:], row[:, 1:2]))

            @block.tensor
            def _(pe):
                pe.wait_ge(s_dve, 1)
                pe.transpose(p_row[0:1, 0:P], most[:], k["ident"][:]).then_inc(s_turn, 1)


def target_means(dve, link, tt, acc, counts, small, inverse, val, parts):
    one = bass.ds(tt, 1)
    link(dve.tensor_scalar(small[:, 0:1], counts[:, one], 1.0, None, ALU.max))
    link(dve.reciprocal(small[:, 1:2], small[:, 0:1]))
    link(dve.tensor_scalar(small[:, 0:1], counts[:, one], 1.0, None, ALU.min))
    link(dve.tensor_tensor(inverse[:, one], small[:, 1:2], small[:, 0:1], ALU.mult))
    link(dve.tensor_scalar(val[:], acc[:, bass.ds(tt * D, D)], inverse[:, one], None, ALU.mult))
    return split_parts(dve, link, parts, tt, val[:])


def sums_by_target(nc, phase, by_source, parts, acc, counts, inverse, out, biggest=None, flag=None):
    with ExitStack() as ctx:
        t = Tools(nc, phase, ctx)
        cnt = t.sb("cnt", [P, 2, NPAD], BF16)
        ones = t.sb("ones", [P, 1], BF16)
        small = t.sb("small", [P, 2])
        val = t.sb("val", [P, D])
        p_sum = t.ps("p_sum", [P, 2, 512])
        s_in = [t.sem(f"in{h}") for h in range(2)]
        s_one, s_dve, s_carry = t.sem("one"), t.sem("dve"), t.sem("carry")
        s_sum, s_copied, s_done = t.sem("sum"), t.sem("copied"), t.sem("done")
        with nc.Block() as block:

            @block.sync
            def _(sp):
                with guarded(sp, flag):
                    def load(i, h):
                        sp.wait_ge(s_sum, i * 2 + h)
                        if biggest is not None:
                            sp.wait_ge(s_done, i * 2 + h)
                        sp.sem_inc(s_carry, 1)
                        sp.dma_start(cnt[:, h], by_source[bass.ds(i * 2 + h, 1)].squeeze(0)).then_inc(s_in[h], 16)

                    per_tile(sp, load)

            @block.vector
            def _(dve):
                with guarded(dve, flag):
                    dve.sem_inc(s_copied, 1)
                    dve.sem_inc(s_done, 1)
                    dve.memset(ones[:], 1.0).then_inc(s_one, 1)
                    link = Steps(dve, s_dve, 9)

                    def tile(i, h):
                        tt = i * 2 + h
                        link.at(tt)
                        if biggest is not None:
                            dve.wait_ge(s_in[h], i * 16 + 16)
                            dve.tensor_reduce(biggest[:, bass.ds(tt, 1)], cnt[:, h], AX, ALU.max)
                        dve.wait_ge(s_sum, tt + 2)
                        for to, src in ((acc[:, bass.ds(tt * D, D)], p_sum[:, h, 0:D]),
                                        (counts[:, bass.ds(tt, 1)], p_sum[:, h, D:D + 1])):
                            if flag is None:
                                last = dve.tensor_copy(to, src)
                            else:
                                last = dve.tensor_tensor(to, src, to, ALU.add)
                        last.then_inc(s_copied, 1)
                        dve.wait_ge(s_copied, tt + 2)
                        dve.wait_ge(s_done, tt + 1)
                        target_means(dve, link, tt, acc, counts, small, inverse, val, out).then_inc(s_done, 1)

                    per_tile(dve, tile)
                    dve.wait_ge(s_done, NB + 1)

            @block.tensor
            def _(pe):
                with guarded(pe, flag):
                    pe.sem_inc(s_sum, 1)
                    pe.wait_ge(s_one, 1)

                    def tile(i, h):
                        pe.wait_ge(s_in[h], i * 16 + 16)
                        pe.wait_ge(s_copied, i * 2 + h)
                        for s in range(NB):
                            block_s = cnt[:, h, s * P:(s + 1) * P]
                            for part in range(3):
                                pe.matmul(p_sum[:, h, 0:D], block_s,
                                          parts[:, (s * 3 + part) * D:(s * 3 + part + 1) * D],
                                          start=(s == 0 and part == 0), stop=(s == NB - 1 and part == 2))
                        for s in range(NB):
                            last = pe.matmul(p_sum[:, h, D:D + 1], cnt[:, h, s * P:(s + 1) * P], ones[:],
                                             start=(s == 0), stop=(s == NB - 1))
                        last.then_inc(s_sum, 1)

                    per_tile(pe, tile)


def sums_by_source(nc, phase, by_target, parts, acc, counts=None, flag=None):
    HALVES = [(0, 14), (14, NB)]
    with ExitStack() as ctx:
        t = Tools(nc, phase, ctx)
        cnt = t.sb("cnt", [P, 2, 14 * P], BF16)
        ones = t.sb("ones", [P, 1], BF16)
        zero = t.sb("zero", [P, 512], BF16)
        p_sum = t.ps("p_sum", [P, 7 * 512])
        p_cnt = t.ps("p_cnt", [P, 512])
        s_in = [t.sem(f"in{h}") for h in range(2)]
        s_one, s_done, s_copied = t.sem("one"), t.sem("done"), t.sem("copied")
        s_used = t.sem("used")
        steps = NB // 2 + 1
        with nc.Block() as block:

            @block.sync
            def _(sp):
                with guarded(sp, flag):
                    for half, (s0, s1) in enumerate(HALVES):
                        def load(i, h):
                            tt = i * 2 + (half * NB + h)
                            sp.wait_ge(s_used, tt)
                            sp.dma_start(cnt[:, (h + half) % 2, 0:(s1 - s0) * P],
                                         by_target[bass.ds(i * 2 + h, 1)].squeeze(0)[:, s0 * P:s1 * P]
                                         ).then_inc(s_in[(h + half) % 2], 16)

                        per_tile(sp, load)

            @block.vector
            def _(dve):
                with guarded(dve, flag):
                    dve.memset(zero[:], 0.0)
                    dve.memset(ones[:], 1.0).then_inc(s_one, 1)
                    for half, (s0, s1) in enumerate(HALVES):
                        dve.wait_ge(s_done, half + 1)
                        pairs = [(acc[:, s0 * D + n * 512:min(s0 * D + n * 512 + 512, s1 * D)],
                                  p_sum[:, n * 512:min(n * 512 + 512, (s1 - s0) * D)]) for n in range((s1 - s0 + 1) // 2)]
                        if counts is not None:
                            pairs.append((counts[:, s0:s1], p_cnt[:, s0:s1]))
                        for out, src in pairs:
                            if flag is None:
                                last = dve.tensor_copy(out, src)
                            else:
                                last = dve.tensor_tensor(out, src, out, ALU.add)
                        last.then_inc(s_copied, 1)
                    dve.wait_ge(s_copied, 2)

            @block.tensor
            def _(pe):
                with guarded(pe, flag):
                    pe.sem_inc(s_used, 1)
                    pe.wait_ge(s_one, 1)
                    for half, (s0, s1) in enumerate(HALVES):
                        if half:
                            pe.wait_ge(s_copied, half)
                        for n in range(7):
                            pe.matmul(p_sum[:, n * 512:(n + 1) * 512], zero[:, 0:P], zero[:], start=True,
                                      stop=False, skip_group_check=True)
                        if not half and counts is not None:
                            pe.matmul(p_cnt[:], zero[:, 0:P], zero[:], start=True, stop=False,
                                      skip_group_check=True)

                        def tile(i, h):
                            tt = i * 2 + h
                            slot = (h + half) % 2
                            before = half * (steps if slot == 0 else steps - 1)
                            pe.wait_ge(s_in[slot], i * 16 + (before * 16 + 16))
                            for s in range(s0, s1):
                                block_s = cnt[:, slot, (s - s0) * P:(s - s0 + 1) * P]
                                for part in range(3):
                                    last = pe.matmul(p_sum[:, (s - s0) * D:(s - s0 + 1) * D], block_s,
                                                     parts[:, bass.ds(tt * (3 * D) + part * D, D)],
                                                     start=False, stop=False, skip_group_check=True)
                                if counts is not None:
                                    last = pe.matmul(p_cnt[:, s:s + 1], block_s, ones[:], start=False, stop=False,
                                                     skip_group_check=True)
                            last.then_inc(s_used, 1)

                        per_tile(pe, tile)
                        pe.matmul(p_sum[:, 0:1], zero[:, 0:P], zero[:, 0:1], start=False, stop=False,
                                  skip_group_check=True).then_inc(s_done, 1)


def inverse_counts(nc, phase, counts, inverse):
    with ExitStack() as ctx:
        t = Tools(nc, phase, ctx)
        some = t.sb("some", [P, NB])
        s_dve = t.sem("dve")
        with nc.Block() as block:

            @block.vector
            def _(dve):
                link = Chain(dve, s_dve)
                link(dve.tensor_scalar(some[:], counts[:], 1.0, None, ALU.min))
                link(dve.tensor_scalar(inverse[:], counts[:], 1.0, None, ALU.max))
                link(dve.reciprocal(inverse[:], inverse[:]))
                link(dve.tensor_tensor(inverse[:], inverse[:], some[:], ALU.mult))


def split_parts(dve, link, parts, tt, value):
    for part in range(3):
        out = parts[:, bass.ds(tt * (3 * D) + part * D, D)]
        if part == 2:
            return dve.tensor_copy(out, value)
        link(dve.tensor_copy(out, value))
        link(dve.tensor_tensor(value, value, out, ALU.subtract))


def prelu(dve, link, out, x, low, slope):
    link(dve.tensor_scalar(low, x, 0.0, slope, ALU.min, ALU.mult))
    return dve.scalar_tensor_tensor(out, x, 0.0, low, ALU.max, ALU.add)


def gnn_middle(nc, k, w, acc, inverse, parts):
    with ExitStack() as ctx:
        t = Tools(nc, "middle", ctx)
        w2 = t.sb("w2", [P, 2, D])
        b1 = t.sb("b1", [P, D])
        slope = t.sb("slope", [P, 1])
        pre = t.sb("pre", [P, D])
        low = t.sb("low", [P, D])
        rows_b = t.sb("rows", [P, 2, D])
        xt = t.sb("xt", [P, D])
        mul = Product(k, t)
        s_w, s_dve, s_use = t.sem("w"), t.sem("dve"), t.sem("use")
        with nc.Block() as block:

            @block.sync
            def _(sp):
                load_all(sp, s_w, [(w2[:], w["gnn_w2"].rearrange("(a p) n -> p a n", p=P)),
                                   (b1[:], spread(w["gnn_b1"])), (slope[:], spread(w["gnn_a"]))])

            @block.vector
            def _(dve):
                dve.sem_inc(mul.s_made, 1)
                dve.sem_inc(mul.s_used, 1)
                dve.wait_ge(s_w, 48)
                link, use = Steps(dve, s_dve, 2), Steps(dve, s_use, 5)

                def rows(i, h):
                    tt = i * 2 + h
                    link.at(tt)
                    dve.wait_ge(mul.s_made, tt + 1)
                    link(dve.scalar_tensor_tensor(pre[:], acc[:, bass.ds(tt * D, D)], inverse[:, bass.ds(tt, 1)],
                                                  b1[:], ALU.mult, ALU.add))
                    dve.wait_ge(mul.s_turned, tt)
                    prelu(dve, link, rows_b[:, h], pre[:], low[:], slope[:, 0:1]).then_inc(mul.s_made, 1)

                def out(i, h):
                    tt = i * 2 + h
                    use.at(tt)
                    dve.wait_ge(mul.s_product, tt + 2)
                    dve.wait_ge(mul.s_used, tt + 1)
                    use(dve.tensor_copy(xt[:], mul.p_out[:, h, 0:D]))
                    split_parts(dve, use, parts, tt, xt[:]).then_inc(mul.s_used, 1)

                one_ahead(dve, rows, out)
                dve.wait_ge(mul.s_used, NB + 1)

            @block.scalar
            def _(act):
                act.sem_inc(mul.s_copied, 1)
                per_tile(act, lambda i, h: mul.copy(act, i * 2 + h, h))

            @block.tensor
            def _(pe):
                pe.sem_inc(mul.s_turned, 1)
                pe.sem_inc(mul.s_product, 1)
                pe.wait_ge(s_w, 48)
                def tile(i, h):
                    mul.turn(pe, i * 2 + h, h, rows_b[:, h])
                    mul.multiply(pe, i * 2 + h, h, [(0, [(a, w2[:, a]) for a in range(2)])])

                per_tile(pe, tile)


def l1_mix(nc, k, w, acc, inverse, kv, xn_dram, x2_dram, x3_dram):
    with ExitStack() as ctx:
        t = Tools(nc, "l1_mix", ctx)
        b2 = t.sb("b2", [P, D])
        slope = t.sb("slope", [P, 1])
        xn = t.sb("xn", [P, 2, D])
        x2 = t.sb("x2", [P, 2, D])
        pre = t.sb("pre", [P, D])
        low = t.sb("low", [P, D])
        total = t.sb("total", [P, 2, D])
        mul = Product(k, t)
        s_w, s_dve, s_carry = t.sem("w"), t.sem("dve"), t.sem("carry")
        s_xn = [t.sem(f"xn{h}") for h in range(2)]
        s_x2 = [t.sem(f"x2{h}") for h in range(2)]
        s_st = [t.sem(f"st{h}") for h in range(2)]
        s_sent = t.sem("sent")
        with nc.Block() as block:

            @block.sync
            def _(sp):
                load_all(sp, s_w, [(b2[:], spread(w["gnn_b2"])), (slope[:], spread(w["gnn_a"]))])

                def load(i, h):
                    tt = i * 2 + h
                    sp.wait_ge(mul.s_used, tt)
                    sp.sem_inc(s_carry, 1)
                    sp.dma_start(xn[:, h], xn_dram[bass.ds(tt * P, P), :]).then_inc(s_xn[h], 16)
                    sp.dma_start(x2[:, h], x2_dram[bass.ds(tt * P, P), :]).then_inc(s_x2[h], 16)

                per_tile(sp, load)

            @block.gpsimd
            def _(pool):
                def store(i, h):
                    pool.wait_ge(mul.s_used, i * 2 + (h + 2))
                    pool.sem_inc(s_sent, 1)
                    pool.dma_start(x3_dram[bass.ds((i * 2 + h) * P, P), :], total[:, h]).then_inc(s_st[h], 16)

                per_tile(pool, store)
                pool.wait_ge(s_st[0], (NB + 1) // 2 * 16)
                pool.wait_ge(s_st[1], NB // 2 * 16)

            @block.vector
            def _(dve):
                dve.sem_inc(mul.s_used, 1)
                dve.wait_ge(s_w, 32)
                link = Steps(dve, s_dve, 6)

                def tile(i, h):
                    tt = i * 2 + h
                    link.at(tt)
                    dve.wait_ge(s_xn[h], i * 16 + 16)
                    dve.wait_ge(s_x2[h], i * 16 + 16)
                    dve.wait_ge(mul.s_used, tt + 1)
                    dve.wait_ge(s_st[h], i * 16)
                    link(dve.scalar_tensor_tensor(pre[:], acc[:, bass.ds(tt * D, D)], inverse[:, bass.ds(tt, 1)],
                                                  b2[:], ALU.mult, ALU.add))
                    link(dve.tensor_tensor(pre[:], pre[:], xn[:, h], ALU.add))
                    link(prelu(dve, link, total[:, h], pre[:], low[:], slope[:, 0:1]))
                    link(dve.tensor_tensor(total[:, h], total[:, h], x2[:, h], ALU.add))
                    dve.wait_ge(mul.s_product, tt + 2)
                    link(dve.tensor_tensor(total[:, h], total[:, h], mul.p_out[:, h, 0:D], ALU.add))
                    dve.tensor_tensor(total[:, h], total[:, h], xn[:, h], ALU.add).then_inc(mul.s_used, 1)

                per_tile(dve, tile)

            @block.scalar
            def _(act):
                act.sem_inc(mul.s_copied, 1)
                per_tile(act, lambda i, h: mul.copy(act, i * 2 + h, h))

            @block.tensor
            def _(pe):
                pe.sem_inc(mul.s_turned, 1)
                pe.sem_inc(mul.s_product, 1)
                pe.sem_inc(mul.s_made, 2 + NB)

                def turn(i, h):
                    pe.wait_ge(s_xn[h], i * 16 + 16)
                    mul.turn(pe, i * 2 + h, h, xn[:, h])

                def tile(i, h):
                    turn(i, h)
                    mul.multiply(pe, i * 2 + h, h, [(a * P, [(a, kv[:, a])]) for a in range(2)])

                per_tile(pe, tile)


def l1_router(nc, k, w, x_dram, xf_dram, scores):
    E = 8
    with ExitStack() as ctx:
        t = Tools(nc, "router", ctx)
        wr = t.sb("wr", [P, 2, E])
        br = t.sb("br", [P, E])
        gamma = t.sb("gamma", [P, D])
        beta = t.sb("beta", [P, D])
        xb = t.sb("xb", [P, 2, D])
        mid = t.sb("mid", [P, D])
        xf = t.sb("xf", [P, 2, D])
        norm = Norm(k, t, 2)
        mul = Product(k, t)
        s_w, s_dve, s_carry = t.sem("w"), t.sem("dve"), t.sem("carry")
        s_in = [t.sem(f"in{h}") for h in range(2)]
        s_st = [t.sem(f"st{h}") for h in range(2)]
        s_sent = t.sem("sent")
        with nc.Block() as block:

            @block.sync
            def _(sp):
                load_all(sp, s_w, [(wr[:], w["wr"].rearrange("(a p) n -> p a n", p=P)), (br[:], spread(w["br"])),
                                   (gamma[:], spread(w["gamma"])), (beta[:], spread(w["beta"]))])

                def load(i, h):
                    tt = i * 2 + h
                    sp.wait_ge(mul.s_made, tt)
                    sp.sem_inc(s_carry, 1)
                    sp.dma_start(xb[:, h], x_dram[bass.ds(tt * P, P), :]).then_inc(s_in[h], 16)

                per_tile(sp, load)

            @block.gpsimd
            def _(pool):
                def tile(i, h):
                    tt = i * 2 + h
                    norm.power(pool, tt, 0)
                    norm.power(pool, tt, 1)

                per_tile(pool, tile)

            @block.vector
            def _(dve):
                dve.sem_inc(mul.s_made, 1)
                dve.sem_inc(mul.s_used, 1)
                dve.wait_ge(s_w, 64)
                link = Steps(dve, s_dve, 6)

                def rows(i, h):
                    tt = i * 2 + h
                    link.at(tt)
                    dve.wait_ge(s_in[h], i * 16 + 16)
                    dve.wait_ge(s_st[h], i * 16)
                    dve.wait_ge(mul.s_turned, tt)
                    link(norm(dve, link, mid[:], xb[:, h], tt, 0))
                    norm.affine(dve, link, xf[:, h], mid[:], gamma[:], beta[:], tt, 1).then_inc(mul.s_made, 1)

                def out(i, h):
                    tt = i * 2 + h
                    dve.wait_ge(mul.s_product, tt + 2)
                    dve.tensor_tensor(scores[:, bass.ds(tt * E, E)], mul.p_out[:, h, 0:E], br[:], ALU.add
                                      ).then_inc(mul.s_used, 1)

                one_ahead(dve, rows, out)
                dve.wait_ge(mul.s_used, NB + 1)

            @block.scalar
            def _(act):
                act.sem_inc(mul.s_copied, 1)
                def store(i, h):
                    tt = i * 2 + h
                    act.wait_ge(mul.s_made, tt + 2)
                    act.sem_inc(s_sent, 1)
                    act.dma_start(xf_dram[bass.ds(tt * P, P), :], xf[:, h]).then_inc(s_st[h], 16)

                def tile(i, h):
                    store(i, h)
                    mul.copy(act, i * 2 + h, h)

                per_tile(act, tile)
                act.wait_ge(s_st[0], (NB + 1) // 2 * 16)
                act.wait_ge(s_st[1], NB // 2 * 16)

            @block.tensor
            def _(pe):
                pe.sem_inc(mul.s_turned, 1)
                pe.sem_inc(mul.s_product, 1)
                pe.wait_ge(s_w, 64)
                def tile(i, h):
                    mul.turn(pe, i * 2 + h, h, xf[:, h])
                    mul.multiply(pe, i * 2 + h, h, [(0, [(a, wr[:, a]) for a in range(2)])])

                per_tile(pe, tile)



def program(nc, w, out, scratch):
    node = lambda name, width=D: scratch(name, [NPAD, width], F32)
    with ExitStack() as whole, nc.allow_non_contiguous_dma("small tables and strided tiles"):
        t = Tools(nc, "all", whole)
        k = make_constants(nc, t)
        table = {L.name: t.sb(f"table_{L.name}", [1, 1152], I32) for L in (CONV, GAT)}
        ids = t.sb("conv_ids", [P, CONV.all_groups * 4])
        index = t.sb("conv_index", [P, CONV.groups * 2], I32)
        rows = {L.name: scratch(f"rows_{L.name}", [L.places, L.width], I32) for L in (CONV, GAT)}

        def sort(L, attr=None, beside=None):
            sort_edges(nc, L, k, table[L.name], w[f"{L.name}_dst_rows"], w[f"{L.name}_dst_cols"],
                       w[f"{L.name}_src_cols"], attr, scratch(f"lo_{L.name}", [L.chunks * P], BF16),
                       scratch(f"tab_{L.name}", [2, 512], I32), rows[L.name], beside)

        xn, kv_d, skip, xm, x2, z = node("xn"), node("kv", 2 * D), node("skip"), node("xm"), node("h1"), node("z")
        with ExitStack() as c:
            u = Tools(nc, "conv", c)
            alpha = u.sb("alpha", [P, CONV.all_groups * 16])
            with ExitStack() as c2:
                v = Tools(nc, "queries", c2)
                q3 = v.sb("q3", [P, NB * 3 * D], BF16)
                with ExitStack() as c3:
                    m = Tools(nc, "attention", c3)
                    q_mix = m.sb("q_mix", [P, NB * D])
                    kv_all = m.sb("kv_all", [P, 2, D + 1])
                    project(nc, k, w, w["x"], xn, q3, q_mix, kv_all, kv_d, skip)
                    linear_attention(nc, k, w, w["x"], q_mix, kv_all, xm)
                sort(CONV, w["attr"])
                ve = scratch("ve", [CONV.groups, P, 2, D], F32)
                conv_scores(nc, k, table["conv"], rows["conv"], kv_d, w["we"], q3, alpha, ids, index, ve)
            segment_softmax(nc, k, CONV, alpha, ids, (D // CONV.heads) ** -0.5)
            acc = u.sb("acc", [P, NB * (D + CONV.heads)])
            block_sums(nc, k, CONV, table["conv"], ids, alpha, acc, values_dram=ve)
            conv_tail(nc, k, w, acc, xn, skip, x2)
        experts(nc, k, "run_ffn", 2, {"w1": w["ffn_w1"], "b1": w["ffn_b1"], "w2": w["ffn_w2"], "b2": w["ffn_b2"]},
                x2, x2, z)

        matrices = {n: scratch(f"counts_{n}", [NB, P, NPAD], BF16) for n in ("t", "s", "t_rest", "s_rest")}
        HALVES = [(0, NB // 2 + 1), (NB // 2 + 1, NB)]

        def count(n, beside=None, rest=None):
            pair = ("t", "s") if rest is None else ("t_rest", "s_rest")
            count_matrix(nc, k, f"matrix{n}" if rest is None else f"rest{n}", table["conv"], ids, index,
                         *(matrices[m] for m in pair), *HALVES[n], rest=rest, beside=beside)

        x1, xl, h_d, xb = node("x1"), node("xl"), node("h", 20), node("xb")
        with ExitStack() as c:
            u = Tools(nc, "gat", c)
            gates = u.sb("gates", [P, NB * 4])
            scores = u.sb("scores", [P, NB * 4])
            ad3 = u.sb("ad3", [P, NB * 12], BF16)
            gat_in(nc, k, w, z, xm, x1, xl, h_d, ad3)
            with ExitStack() as c2:
                v = Tools(nc, "gat_edges", c2)
                sort(GAT, beside=lambda nc, placing: count(0, PlacingBeside(placing)))
                alpha = v.sb("alpha", [P, GAT.all_groups * 8])
                gids = v.sb("ids", [P, GAT.all_groups * 4])
                gindex = v.sb("index", [P, GAT.groups * 2], I32)
                values = v.sb("values", [P, GAT.groups * 32])
                acc = v.sb("acc", [P, NB * 20])
                load_meta(nc, GAT, rows["gat"], gids, gindex)
                with ExitStack() as c3:
                    scoring = GatScores(k, Tools(nc, "gscore", c3), table["gat"], h_d, ad3, alpha, gids, gindex,
                                        values)
                    count(1, ScoresBeside(scoring))
                segment_softmax(nc, k, GAT, alpha, gids, 1.0)
                block_sums(nc, k, GAT, table["gat"], gids, alpha, acc, values=values)
                gat_gates(nc, k, w, acc, scores)
            pick_two(nc, k, "pick4", 4, scores, gates)
            experts(nc, k, "run_moe4", 4, {"w1": w["moe4_w1"], "b1": w["moe4_b1"], "w2": w["moe4_w2"],
                                       "b2": w["moe4_b2"]}, xl, x1, xb, gates)

        xn1, x3, xf = node("xn1"), node("x3"), node("xf")
        with ExitStack() as c:
            u = Tools(nc, "l1", c)
            kv = u.sb("kv", [P, 2, P])
            inv_dst = u.sb("inv_dst", [P, NB])
            inv_src = u.sb("inv_src", [P, NB])
            counts = u.sb("counts", [P, NB])
            biggest = u.sb("biggest", [P, NB])
            flag = u.sb("flag", [1, 1], I32)
            acc = u.sb("acc", [P, NB * D])
            parts = u.sb("parts", [P, NB * 3 * D], BF16)
            means = u.sb("means", [P, NB * 3 * D], BF16)
            l1_in(nc, k, w, xb, xn1, parts, kv)

            def to_targets(name, **more):
                sums_by_target(nc, name, matrices["s"], parts, acc, counts, inv_dst, means, **more)

            def rest_to_targets(name):
                sums_by_target(nc, name, matrices["s_rest"], parts, acc, counts, inv_dst, means, flag=flag)

            def to_sources(name, counted=None):
                sums_by_source(nc, name, matrices["t"], means, acc, counted)
                sums_by_source(nc, name + "_rest", matrices["t_rest"], means, acc, counted, flag)

            to_targets("sweep1", biggest=biggest)
            rounded_counts(nc, k, biggest, flag)
            for n in range(2):
                count(n, rest=flag)
            rest_to_targets("sweep1_rest")
            to_sources("sweep2", counts)
            inverse_counts(nc, "inverse2", counts, inv_src)
            gnn_middle(nc, k, w, acc, inv_src, parts)
            to_targets("sweep3")
            rest_to_targets("sweep3_rest")
            to_sources("sweep4")
            l1_mix(nc, k, w, acc, inv_src, kv, xn1, xb, x3)

        with ExitStack() as c:
            u = Tools(nc, "l1_moe", c)
            gates = u.sb("gates", [P, NB * 8])
            scores = u.sb("scores", [P, NB * 8])
            l1_router(nc, k, w, x3, xf, scores)
            pick_two(nc, k, "pick8", 8, scores, gates)
            experts(nc, k, "run_moe8", 8, {"w1": w["moe8_w1"], "b1": w["moe8_b1"], "w2": w["moe8_w2"],
                                       "b2": w["moe8_b2"]}, xf, x3, out, gates)


def layout(inputs):
    import numpy as np
    g = {n: np.asarray(a) for n, a in inputs.items()}
    f = lambda *names: np.concatenate([g[n].reshape(-1) for n in names])
    w = {"x": np.concatenate([g["x"], np.zeros((NPAD - N, D), g["x"].dtype)])}

    def edges(L, src, dst):
        pad = L.chunks * P - len(src)
        cols = lambda a: np.ascontiguousarray(a.reshape(L.chunks, P).T)
        dst = np.concatenate([dst, np.full(pad, TOP, dst.dtype)])
        src = np.concatenate([src, np.zeros(pad, src.dtype)])
        w[f"{L.name}_dst_rows"], w[f"{L.name}_dst_cols"], w[f"{L.name}_src_cols"] = dst, cols(dst), cols(src)

    edges(CONV, g["src"], g["dst"])
    loops = np.arange(N, dtype=g["L0_ffn_edge_index"].dtype)
    edges(GAT, *(np.concatenate([g["L0_ffn_edge_index"][n], loops]) for n in range(2)))
    attr = g["edge_attr_64"]
    w["attr"] = np.concatenate([attr, np.zeros((CONV.chunks * P - attr.shape[0], attr.shape[1]), attr.dtype)])
    G, M, F = "L0_gnn_", "L0_mix_", "L0_ffn_"
    w["wcat"] = np.concatenate([g[G + n].T for n in ("Wq", "Wk", "Wv", "Wskip")] + [g[M + "wk"], g[M + "wv"]], 1)
    w["bcat"] = f(G + "bq", G + "bk", G + "bv", G + "bskip", M + "bk", M + "bv")
    for n in ("wq", "bq", "wo", "bo"):
        w["mix_" + n] = g[M + n]
    w["we"] = g[G + "We"].T
    w["wbeta"] = g[G + "Wbeta"].reshape(-1)
    for n in ("ln1_g", "ln1_b", "ln2_g", "ln2_b"):
        w[n] = g[G + n]
    w["ffn_w1"] = g[G + "W1"].T.reshape(D, 2, 512).transpose(1, 0, 2)
    w["ffn_w2"] = g[G + "W2"].T.reshape(2, 512, D)
    w["ffn_b1"], w["ffn_b2"] = g[G + "b1"], g[G + "b2"]
    w["w_gat"] = g[F + "W_gat"]
    w["att"] = f(F + "att_src", F + "att_dst")
    w["gat_ln"] = f(F + "b_gat", F + "ln_gamma", F + "ln_beta")
    for name, prefix in (("moe4", F), ("moe8", "L1_ffn_")):
        w[name + "_w1"], w[name + "_w2"] = g[prefix + "W1"], g[prefix + "W2"]
        w[name + "_b1"], w[name + "_b2"] = f(prefix + "b1"), f(prefix + "b2")
    for n in ("W1", "W2", "b1", "b2", "a"):
        w["gnn_" + n.lower()] = g["L1_gnn_" + n]
    w["kvln"] = f(*("L1_mix_" + n for n in ("kln_weight", "kln_bias", "vln_weight", "vln_bias")))
    w["wr"], w["br"], w["gamma"], w["beta"] = (g["L1_ffn_" + n] for n in ("Wr", "br", "gamma", "beta"))
    return {n: np.ascontiguousarray(a) for n, a in w.items()}


def kernel(**inputs):
    import concourse.bacc as bacc
    from concourse.bass_utils import run_bass_kernel_spmd

    w = layout(inputs)
    nc = bacc.Bacc("TRN2", target_bir_lowering=False, num_devices=1)
    aps = {n: nc.dram_tensor(f"in_{n}", a.shape, mybir.dt.from_np(a.dtype), kind="ExternalInput").ap()
           for n, a in w.items()}
    out = nc.dram_tensor("out", (NPAD, D), F32, kind="ExternalOutput").ap()
    program(nc, aps, out, lambda name, shape, dt: nc.dram_tensor(f"s_{name}", shape, dt).ap())
    r = run_bass_kernel_spmd(nc, [{f"in_{n}": a for n, a in w.items()}], core_ids=[0])
    return r.results[0]["out"][:N]
```
